# Optimizing a Trainium2 kernel written in Bass

```python
import numpy as np
import jax
import jax.numpy as jnp

def _softmax(x, axis=-1):
    return jax.nn.softmax(x, axis=axis)

def _gelu(x):
    return jax.nn.gelu(x, approximate=True)

def _silu(x):
    return jax.nn.silu(x)

def _sigmoid(x):
    return jax.nn.sigmoid(x)

def _layernorm(x, axis=-1, eps=1e-05):
    m = jnp.mean(x, axis=axis, keepdims=True)
    v = jnp.var(x, axis=axis, keepdims=True)
    return (x - m) / jnp.sqrt(v + eps)

def _scatter_add(tgt, idx, src, axis=0):
    return tgt.at[idx].add(src)

def _segment_sum(src, seg, n):
    return jax.ops.segment_sum(src, seg, n)
kernel_name = 'mk_flamingo_gated_d2_seqx_r8_6ae345'

def setup_inputs(seed: int=0):
    np.random.seed(seed)
    _w = jnp.asarray

    def _rec_inputs():
        import jax
        import jax.numpy as jnp
        _rk = jax.random.key(seed)
        x = -0.0002928 + 1 * jax.random.normal(jax.random.fold_in(_rk, 1), (16, 128, 256), jnp.float32)
        _lenS = 128 - jax.random.randint(jax.random.fold_in(_rk, 7), (16,), 0, max(1, 128 // 4) + 1, jnp.int32)
        _lenS2 = 128 - jax.random.randint(jax.random.fold_in(_rk, 8), (16,), 0, max(1, 128 // 4) + 1, jnp.int32)
        fside_S2_0 = -0.00337071 + 1.01897 * jax.random.normal(jax.random.fold_in(_rk, 11), (128,), jnp.float32)
        _ctx_2048P = jax.random.normal(jax.random.fold_in(_rk, 12), (16, 16, 256), jnp.float32)
        _ctx_2048c = jax.random.dirichlet(jax.random.fold_in(_rk, 512), 0.3 * jnp.ones((16,), jnp.float32), (16, 128))
        _ctx_2048t = jnp.einsum('bsk,bkd->bsd', _ctx_2048c, _ctx_2048P)
        _ctx_2048t = _ctx_2048t * jax.lax.rsqrt(jnp.mean(jnp.square(_ctx_2048t)) + 1e-12) * 0.953939
        ctx_2048 = 0.000675642 + 1.00031 * (_ctx_2048t + 0.3 * jax.random.normal(jax.random.fold_in(_rk, 612), (16, 128, 256), jnp.float32))
        _validS = jnp.arange(128)[None, :] < _lenS[:, None]
        _validS2 = jnp.arange(128)[None, :] < _lenS2[:, None]
        _causal = jnp.tril(jnp.ones((128, 128), dtype=bool))
        mask_BxS2_bk0 = jnp.logical_not(jnp.broadcast_to(_validS2[:, :], (16, 128)))
        _g = jax.random.normal(jax.random.fold_in(_rk, 9001), (2, 2), jnp.float32)
        _g = jnp.sign(_g) * jnp.maximum(jnp.abs(_g), 1.0) + (_g == 0) * 1.0
        g_xattn = _g[0]
        g_ffn = _g[1]
        return (x, fside_S2_0, ctx_2048, mask_BxS2_bk0, g_xattn, g_ffn)
    x, fside_S2_0, ctx_2048, mask_BxS2_bk0, g_xattn, g_ffn = _rec_inputs()

    def _L0_xattn_setup():
        import jax, jax.numpy as jnp
        import numpy as np
        key = jax.random.key(seed)
        ks = jax.random.split(key, 5)
        B, D, L, NH = (2, 128, 256, 8)
        H = D // NH
        return {'v': jax.random.normal(ks[0], (B, D, L), jnp.float32), 'k': jax.random.normal(ks[1], (H, L), jnp.float32) * 0.1, 'bias': jax.random.normal(ks[2], (D,), jnp.float32), 'x1': jax.random.normal(ks[3], (B, D, L), jnp.float32), 'x2': jax.random.normal(ks[4], (B, D, L), jnp.float32), 'num_heads': NH}
    _L0_xattn_all = _L0_xattn_setup()
    _L0_xattn_in = {k: v for k, v in _L0_xattn_all.items() if k in ('k',)}
    del _L0_xattn_all

    def _L0_ffn_setup():
        import jax, jax.numpy as jnp
        import numpy as np
        SWIGLU_ALPHA = 1.702
        SWIGLU_LIMIT = 7.0
        B, S, H, E, K, I = (2, 256, 256, 32, 4, 128)
        key = jax.random.key(seed)
        ks = jax.random.split(key, 8)
        return {'hidden_states': jax.random.normal(ks[0], (B, S, H), jnp.float32), 'gate_w': jax.random.normal(ks[1], (E, H), jnp.float32) * 0.02, 'gate_b': jnp.zeros((E,), jnp.float32), 'w_gate': jax.random.normal(ks[2], (E, H, I), jnp.float32) * 0.02, 'b_gate': jnp.zeros((E, I), jnp.float32), 'w_up': jax.random.normal(ks[3], (E, H, I), jnp.float32) * 0.02, 'b_up': jnp.zeros((E, I), jnp.float32), 'w_down': jax.random.normal(ks[4], (E, I, H), jnp.float32) * 0.02, 'b_down': jnp.zeros((E, H), jnp.float32)}
    _L0_ffn_all = _L0_ffn_setup()
    _L0_ffn_in = {k: v for k, v in _L0_ffn_all.items() if k in ('gate_w', 'gate_b', 'w_gate', 'b_gate', 'w_up', 'b_up', 'w_down', 'b_down')}
    del _L0_ffn_all

    def _L1_xattn_setup():
        import jax, jax.numpy as jnp
        import numpy as np
        key = jax.random.key(seed)
        k1, k2, k3 = jax.random.split(key, 3)
        B, S, D, M = (8, 256, 256, 128)
        hidden_states = jax.random.normal(k1, (B, S, D), dtype=jnp.float32)
        memory_tokens = jax.random.normal(k2, (B, M, D), dtype=jnp.float32)
        memory_mask = jax.random.randint(k3, (B, M), 0, 2).astype(jnp.bool_)
        return {'hidden_states': hidden_states, 'memory_tokens': memory_tokens, 'memory_mask': memory_mask}
    _L1_xattn_all = _L1_xattn_setup()
    _L1_xattn_in = {k: v for k, v in _L1_xattn_all.items() if k in ()}
    del _L1_xattn_all

    def _L1_ffn_setup():
        import jax, jax.numpy as jnp
        import numpy as np
        NUM_EXPERTS = 32
        TOP_K = 8
        THRESHOLD = 0.8
        HIDDEN = 256
        INTER = 96
        key = jax.random.key(seed)
        k1, k2, k3, k4 = jax.random.split(key, 4)
        hidden_states = jax.random.normal(k1, (2, 128, HIDDEN), jnp.float32)
        gate_weight = jax.random.normal(k2, (NUM_EXPERTS, HIDDEN), jnp.float32) * 0.02
        gate_up_proj = jax.random.normal(k3, (NUM_EXPERTS, 2 * INTER, HIDDEN), jnp.float32) * 0.02
        down_proj = jax.random.normal(k4, (NUM_EXPERTS, HIDDEN, INTER), jnp.float32) * 0.02
        return {'hidden_states': hidden_states, 'gate_weight': gate_weight, 'gate_up_proj': gate_up_proj, 'down_proj': down_proj}
    _L1_ffn_all = _L1_ffn_setup()
    _L1_ffn_in = {k: v for k, v in _L1_ffn_all.items() if k in ('gate_weight', 'gate_up_proj', 'down_proj')}
    del _L1_ffn_all
    return {'x': x, 'fside_S2_0': fside_S2_0, 'ctx_2048': ctx_2048, 'mask_BxS2_bk0': mask_BxS2_bk0, 'g_xattn': g_xattn, 'g_ffn': g_ffn, 'L0_xattn_k': _L0_xattn_in['k'], 'L0_ffn_gate_w': _L0_ffn_in['gate_w'], 'L0_ffn_gate_b': _L0_ffn_in['gate_b'], 'L0_ffn_w_gate': _L0_ffn_in['w_gate'], 'L0_ffn_b_gate': _L0_ffn_in['b_gate'], 'L0_ffn_w_up': _L0_ffn_in['w_up'], 'L0_ffn_b_up': _L0_ffn_in['b_up'], 'L0_ffn_w_down': _L0_ffn_in['w_down'], 'L0_ffn_b_down': _L0_ffn_in['b_down'], 'L1_ffn_gate_weight': _L1_ffn_in['gate_weight'], 'L1_ffn_gate_up_proj': _L1_ffn_in['gate_up_proj'], 'L1_ffn_down_proj': _L1_ffn_in['down_proj']}

def reference(x, fside_S2_0, ctx_2048, mask_BxS2_bk0, g_xattn, g_ffn, L0_xattn_k, L0_ffn_gate_w, L0_ffn_gate_b, L0_ffn_w_gate, L0_ffn_b_gate, L0_ffn_w_up, L0_ffn_b_up, L0_ffn_w_down, L0_ffn_b_down, L1_ffn_gate_weight, L1_ffn_gate_up_proj, L1_ffn_down_proj):
    import jax
    import jax.numpy as jnp

    def _L0_xattn_ref(v, k, bias, x1, x2, num_heads):
        import jax, jax.numpy as jnp
        import numpy as np
        B, D, L = v.shape
        H = D // num_heads
        fft_size = 2 * L
        vr = v.reshape(B, H, num_heads, L)
        x1r = x1.reshape(B, H, num_heads, L)
        x2r = x2.reshape(B, H, num_heads, L)
        kv = vr[:, :, :, None, :] * x2r[:, :, None, :, :]
        k_f = jnp.fft.rfft(k.astype(jnp.float32), n=fft_size)
        y = jnp.fft.irfft(jnp.fft.rfft(kv, n=fft_size) * k_f[None, :, None, None, :], n=fft_size)[..., :L]
        skip = bias.astype(jnp.float32).reshape(H, num_heads)[None, :, :, None, None]
        y = y + kv * skip
        out = jnp.einsum('bhijl,bhil->bhjl', y, x1r)
        return out.reshape(B, D, L)

    def _L0_ffn_ref(hidden_states, gate_w, gate_b, w_gate, b_gate, w_up, b_up, w_down, b_down):
        import jax, jax.numpy as jnp
        import numpy as np
        SWIGLU_ALPHA = 1.702
        SWIGLU_LIMIT = 7.0
        B, S, H, E, K, I = (2, 256, 256, 32, 4, 128)
        Bb, Ss, Hh = hidden_states.shape
        x = hidden_states.reshape(-1, Hh)
        logits = x @ gate_w.T + gate_b
        topk_logits, topk_idx = jax.lax.top_k(logits, K)
        topk_weight = jax.nn.softmax(topk_logits.astype(jnp.float32), axis=-1)
        flat_idx = topk_idx.reshape(-1)
        xs = jnp.repeat(x, K, axis=0)
        order = jnp.argsort(flat_idx)
        xt = xs[order]
        gid = flat_idx[order]
        group_sizes = jnp.bincount(flat_idx, length=E).astype(jnp.int32)
        gate = jax.lax.ragged_dot(xt, w_gate, group_sizes) + b_gate[gid]
        up = jax.lax.ragged_dot(xt, w_up, group_sizes) + b_up[gid]
        gate = jnp.minimum(gate, SWIGLU_LIMIT)
        up = jnp.clip(up, -SWIGLU_LIMIT, SWIGLU_LIMIT)
        glu = gate * jax.nn.sigmoid(SWIGLU_ALPHA * gate)
        activated = (up + 1.0) * glu
        outs = jax.lax.ragged_dot(activated, w_down, group_sizes) + b_down[gid]
        inv = jnp.argsort(order)
        outs = outs[inv].reshape(-1, K, Hh)
        y = jnp.sum(outs * topk_weight[..., None], axis=1).astype(x.dtype)
        return y.reshape(Bb, Ss, Hh)

    def _L1_xattn_ref(hidden_states, memory_tokens, memory_mask):
        import jax, jax.numpy as jnp
        import numpy as np
        B, S, D = hidden_states.shape
        scale = 1.0 / jnp.sqrt(jnp.asarray(D, hidden_states.dtype))
        scores = jnp.einsum('bsd,bmd->bsm', hidden_states, memory_tokens) * scale
        neg_inf = jnp.asarray(-1e+30, scores.dtype)
        scores = jnp.where(memory_mask[:, None, :], scores, neg_inf)
        attn = jax.nn.softmax(scores, axis=-1)
        readout = jnp.einsum('bsm,bmd->bsd', attn, memory_tokens)
        valid_b = jnp.any(memory_mask, axis=-1)
        out = jnp.where(valid_b[:, None, None], readout, jnp.zeros_like(readout))
        return out

    def _L1_ffn_ref(hidden_states, gate_weight, gate_up_proj, down_proj):
        import jax, jax.numpy as jnp
        import numpy as np
        NUM_EXPERTS = 32
        TOP_K = 8
        THRESHOLD = 0.8
        HIDDEN = 256
        INTER = 96
        B, S, H = hidden_states.shape
        x = hidden_states.reshape(-1, H)
        logits = x @ gate_weight.T
        probs = jax.nn.softmax(logits.astype(jnp.float32), axis=-1).astype(logits.dtype)
        top_vals, top_idx = jax.lax.top_k(probs, TOP_K)
        renorm = top_vals / jnp.clip(jnp.sum(top_vals, axis=-1, keepdims=True), 1e-12)
        cum = jnp.cumsum(renorm, axis=-1)
        num_keep = jnp.minimum(jnp.sum((cum < THRESHOLD).astype(jnp.int32), axis=-1) + 1, TOP_K)
        active = jnp.arange(TOP_K)[None, :] < num_keep[:, None]
        rw = top_vals * active.astype(top_vals.dtype)
        rw = rw / jnp.clip(jnp.sum(rw, axis=-1, keepdims=True), 1e-12)
        combine = jnp.sum(jax.nn.one_hot(top_idx, NUM_EXPERTS, dtype=rw.dtype) * rw[..., None], axis=1)

        def body(acc, params):
            w_gu, w_d, ce = params
            gu = x @ w_gu.T
            g, u = jnp.split(gu, 2, axis=-1)
            h = jax.nn.silu(g) * u
            return (acc + h @ w_d.T * ce[:, None], None)
        out, _ = jax.lax.scan(body, jnp.zeros_like(x), (gate_up_proj, down_proj, combine.T))
        return out.reshape(B, S, H)
    x = x + jnp.tanh(g_xattn[0]) * _L0_xattn_ref(_layernorm(x, axis=-1), L0_xattn_k, fside_S2_0, ctx_2048, ctx_2048, 8)
    x = x + jnp.tanh(g_ffn[0]) * _L0_ffn_ref(_layernorm(x, axis=-1), L0_ffn_gate_w, L0_ffn_gate_b, L0_ffn_w_gate, L0_ffn_b_gate, L0_ffn_w_up, L0_ffn_b_up, L0_ffn_w_down, L0_ffn_b_down)
    x = x + jnp.tanh(g_xattn[1]) * _L1_xattn_ref(_layernorm(x, axis=-1), ctx_2048, mask_BxS2_bk0)
    x = x + jnp.tanh(g_ffn[1]) * _L1_ffn_ref(_layernorm(x, axis=-1), L1_ffn_gate_weight, L1_ffn_gate_up_proj, L1_ffn_down_proj)
    return x

_drawn_inputs = setup_inputs


def setup_inputs(seed=0):
    import zlib

    import numpy as np

    out = dict(_drawn_inputs(seed))
    spreads = {'g_ffn': (-1.0, 0.6),
     'L0_ffn_gate_b': (0.0, 0.8),
     'L0_ffn_b_gate': (0.0, 0.8),
     'L0_ffn_b_up': (0.0, 0.8),
     'L0_ffn_b_down': (0.0, 0.8)}
    factors = {'L0_ffn_gate_w': 5.73,
     'L0_ffn_w_gate': 8.0,
     'L0_ffn_w_up': 8.0,
     'L0_ffn_w_down': 8.0,
     'L1_ffn_gate_weight': 8.0,
     'L1_ffn_gate_up_proj': 8.0,
     'L1_ffn_down_proj': 8.0}
    for name, (base, spread) in spreads.items():
        noise = np.random.default_rng([zlib.crc32(name.encode()), seed]).standard_normal(out[name].shape)
        drawn = base * np.exp(spread * noise) if base else spread * noise
        out[name] = jnp.asarray(drawn.astype(out[name].dtype))
    for name, factor in factors.items():
        out[name] = (out[name] * factor).astype(out[name].dtype)
    return out
```

```python
import concourse.bass as bass
from concourse import mybir
from contextlib import ExitStack


def bass_flamingo_gated_two_layers_kernel(
    nc: bass.Bass,
    x_rows: bass.AP,
    ctx_rows: bass.AP,
    ctx_cols: bass.AP,
    ctx_batch: bass.AP,
    filt: bass.AP,
    skip_cols: bass.AP,
    mask: bass.AP,
    gates: bass.AP,
    router0: bass.AP,
    router0_bias: bass.AP,
    gate_bias0: bass.AP,
    up_bias0: bass.AP,
    down_bias0: bass.AP,
    experts0: bass.AP,
    router1: bass.AP,
    experts1: bass.AP,
    out: bass.AP,
):
    fp32 = mybir.dt.float32
    fp32r = mybir.dt.float32r
    u32 = mybir.dt.uint32
    i32 = mybir.dt.int32
    u8 = mybir.dt.uint8
    ALU = mybir.AluOpType
    ACT = mybir.ActivationFunctionType
    AX = mybir.AxisListType
    ds = bass.ds

    P = 128
    NT = x_rows.shape[1]
    D = x_rows.shape[2]
    KB = D // P
    NB = ctx_batch.shape[0]
    G = P // NB
    TOK = NT * P
    NE = experts0.shape[0]
    CH = 512
    NCH = TOK // CH
    TPC = CH // P
    UNITS = NE * NCH
    PAIR = 2 * NCH
    NPAIR = NE // 2
    EPS = 1e-5
    LIMIT = 7.0
    ALPHA = 1.702
    NEG = 1e30
    TOPK = (4, 8)
    THRESHOLD = 0.8
    INNER = (128, 96)
    SCALE = float(D) ** -0.5

    ctx = ExitStack()
    with ctx:
        def sb(name, shape, dt=fp32):
            return ctx.enter_context(nc.sbuf_tensor(name, shape, dt))

        def sem(name):
            return ctx.enter_context(nc.semaphore(name))

        def sems(prefix, names):
            return {n: sem(f"{prefix}_{n}") for n in names.split()}

        X = sb("X", [P, NT * D])
        rows = sb("rows", [P, NT * D])
        cols = sb("cols", [P, KB, NT, P])
        scratch = sb("scratch", [P, 4096])
        xhi = sb("xhi", [P, KB, TOK], fp32r)
        xlo = sb("xlo", [P, KB, TOK], fp32r)
        toep_all = sb("toep_all", [P, NT, D])
        toep = sb("toep", [P, 2, D])
        xn = sb("xn", [P, 2, D])
        vT = sb("vT", [P, 2, KB, P])
        prod = sb("prod", [P, KB, 1024])
        fold1 = sb("fold1", [P, KB, 512])
        fold2 = sb("fold2", [P, KB, 256])
        skipv = sb("skipv", [P, 2, D])
        mixed = sb("mixed", [P, 2, D])
        skc = sb("skc", [P, NT])
        stats = sb("stats", [P, NT, 6])
        mv = sb("mv", [P, NT * 2])
        var_e = sb("var_e", [P, NT])
        std = sb("std", [P, NT])
        rstd = sb("rstd", [P, NT])
        newt = sb("newt", [P, NT])
        ident = sb("ident", [P, P])
        flip = sb("flip", [P, P])
        same_b = sb("same_b", [P, P])
        ones_row = sb("ones_row", [1, P])
        iota_i = sb("iota_i", [P, NE], i32)
        iota_f = sb("iota_f", [P, NE])
        gate_in = sb("gate_in", [P, 4])
        tg = sb("tg", [P, 4])
        mask_u8 = sb("mask_u8", [1, NB * P], u8)
        mbias = sb("mbias", [1, NB * P])
        valid = sb("valid", [1, NB])
        valid_t = sb("valid_t", [P, NB])
        rt_raw = [sb(f"rt_raw{m}", [P, KB * P]) for m in range(2)]
        rt_hi = [sb(f"rt_hi{m}", [P, KB * P], fp32r) for m in range(2)]
        rt_lo = [sb(f"rt_lo{m}", [P, KB * P], fp32r) for m in range(2)]
        rt_bias = sb("rt_bias", [NE, 1])
        gate_b = sb("gate_b", [P, NE])
        up_b = sb("up_b", [P, NE])
        up_b1 = sb("up_b1", [P, NE])
        down_b = sb("down_b", [NE, D])
        lgT = sb("lgT", [NE, TOK])
        lg = sb("lg", [P, NT, NE])
        cw = sb("cw", [P, NT * NE])
        top = sb("top", [P, NT, 8])
        top_i = sb("top_i", [P, NT, 8], u32)
        top_f = sb("top_f", [P, NT, 8])
        tw = sb("tw", [P, NT, 8])
        tcum = sb("tcum", [P, NT, 8])
        row1 = sb("row1", [P, NT])
        row2 = sb("row2", [P, NT])
        W = 4 * P + D
        w_raw = sb("w_raw", [P, 2, W])
        w_hi = sb("w_hi", [P, 2, W], fp32r)
        w_lo = sb("w_lo", [P, 2, W], fp32r)
        h_hi = sb("h_hi", [P, 4, CH], fp32r)
        h_lo = sb("h_lo", [P, 4, CH], fp32r)
        smax = sb("smax", [P, NB])
        nbias = sb("nbias", [P, NB])
        psum_row = sb("psum_row", [P, NB])
        rinv = sb("rinv", [P, NB])

        kv = scratch[:, :].rearrange("p (s k n) -> p s k n", s=2, k=KB)
        one_hot = scratch[:, :]
        xT_b = scratch[:, :].rearrange("p (k b s) -> p k b s", k=KB, b=NB)
        gmin = scratch[:, 0:1024].rearrange("p (s n) -> p s n", s=2)
        umin = scratch[:, 1024:2048].rearrange("p (s n) -> p s n", s=2)
        sig = scratch[:, 2048:3072].rearrange("p (s n) -> p s n", s=2)
        hid = scratch[:, 3072:4096].rearrange("p (s n) -> p s n", s=2)
        turn = prod[:, :, :].rearrange("p k n -> p (k n)")
        xs_b = turn[:, 0:512].rearrange("p (s k n) -> p s k n", s=2, k=KB)
        mem_b = turn[:, 512:1024].rearrange("p (s n) -> p s n", s=2)
        prob = turn[:, 1024:1280].rearrange("p (s n) -> p s n", s=2)
        attn = turn[:, 1280:1536].rearrange("p (s n) -> p s n", s=2)
        attnT = turn[:, 1536:1792].rearrange("p (s n) -> p s n", s=2)
        roT = rows[:, :].rearrange("p (k h s) -> p k h s", k=KB, h=NT)
        lg2 = lg[:, :, :].rearrange("p t e -> p (t e)")

        bank = [ctx.enter_context(nc.psum_tensor(f"bank{i}", [P, 512], fp32)) for i in range(8)]

        s_x = sem("s_x")
        s_ctx = sem("s_ctx")
        s_cols = sem("s_cols")
        s_par = sem("s_par")
        s_par2 = sem("s_par2")
        s_toep = sem("s_toep")
        s_mem = [sem(f"s_mem{p}") for p in range(2)]
        s_w = [[sem(f"s_w{m}{p}") for p in range(2)] for m in range(2)]
        s_const = sem("s_const")
        s_tanh = sem("s_tanh")
        s_rhi = sem("s_rhi")
        s_rlo = sem("s_rlo")
        s_valid = sem("s_valid")
        s_vb = sem("s_vb")
        s_out = sem("s_out")
        s_chain = sem("s_chain")
        s_zeroed = sem("s_zeroed")
        A = sems("A", "var sd flip turned tp vn skv tr vt kv0 kv1 y z f1 f2 out mix mixed x")
        N = [sems(f"N{m}", "var sd xn tr hi lo lt lg l e0 e1 cw cwp cwt bd bdx") for m in range(2)]
        M = [sems(f"M{m}", "whi wlo g u gmin umin sig gs h hhi hlo o acc") for m in range(2)]
        C = sems("C", "var sd xn tr xt xs s mx nb e ri a at atc ro rot fx x")

        block = ctx.enter_context(nc.Block())

        def wait(eng, s, n):
            if isinstance(n, int) and n <= 0:
                return
            eng.wait_ge(s, n)

        def by_two(eng, step, n, peel):
            for t in range(peel):
                step(t, t % 2)
            with eng.Fori(peel // 2, n // 2, 1) as pair:
                for p in range(2):
                    step(2 * pair + p, p)

        def by_pair(eng, step):
            for j in range(PAIR):
                step(0, j)
            with eng.Fori(1, NPAIR - 1, 1) as q:
                for j in range(PAIR):
                    step(q, j)
            for j in range(PAIR):
                step(NPAIR - 1, j)

        @block.sync
        def _(sp):
            def load_experts(m, src):
                width = src.shape[2]

                def load(e, p, at):
                    wait(sp, M[m]["wlo"], e - 1)
                    sp.dma_start(w_raw[:, p, 0:width], src[at, :, :].rearrange("a p n -> p (a n)"))\
                        .then_inc(s_w[m][p], 16)
                for e in range(2):
                    load(e, e, ds(e, 1))
                with sp.Fori(1, NPAIR, 1) as q:
                    for p in range(2):
                        load(2 * q + p, p, ds(2 * q + p, 1))

            sp.dma_start(X[:, :], x_rows.rearrange("p t d -> p (t d)")).then_inc(s_x, 16)
            sp.dma_start(toep_all[:, :, :],
                         bass.AP(tensor=filt.tensor, offset=1, ap=[[1, P], [P + D, NT], [1, D]])).then_inc(s_toep, 16)
            sp.dma_start(skc[:, :], skip_cols).then_inc(s_par, 16)
            sp.dma_start(gate_in[:, :], gates.partition_broadcast(P)).then_inc(s_par, 16)
            sp.dma_start(cols[:, :, :, :], ctx_cols).then_inc(s_cols, 16)
            sp.dma_start(rows[:, :], ctx_rows.rearrange("p t d -> p (t d)")).then_inc(s_ctx, 16)
            sp.dma_start(mask_u8[:, :], mask).then_inc(s_par2, 16)
            sp.dma_start(rt_raw[0][:, :], router0).then_inc(s_par2, 16)
            sp.dma_start(rt_raw[1][:, :], router1).then_inc(s_par2, 16)
            sp.dma_start(rt_bias[:, :], router0_bias).then_inc(s_par2, 16)
            sp.dma_start(gate_b[:, :], gate_bias0).then_inc(s_par2, 16)
            sp.dma_start(up_b[:, :], up_bias0).then_inc(s_par2, 16)
            sp.dma_start(down_b[:, :], down_bias0).then_inc(s_par2, 16)

            load_experts(0, experts0)

            def load_mem(b, p):
                wait(sp, C["ro"], b - 1)
                sp.dma_start(mem_b[:, p, :], ctx_batch[ds(b, 1), :, :].rearrange("a s d -> s (a d)"))\
                    .then_inc(s_mem[p], 16)
            by_two(sp, load_mem, NB, 2)
            sp.wait_ge(M[0]["wlo"], NE)
            load_experts(1, experts1)

            for c in range(NCH):
                sp.wait_ge(M[1]["acc"], TPC * (UNITS - NCH + c + 1))
                n = TPC * D
                sp.dma_start(out.rearrange("p t d -> p (t d)")[:, c * n:(c + 1) * n], X[:, c * n:(c + 1) * n])\
                    .then_inc(s_out, 16)
            sp.wait_ge(s_out, 16 * NCH)

        @block.gpsimd
        def _(pool):
            g = nc.gpsimd
            g.memset(ident[:, :], 0.0).then_inc(s_zeroed, 1)
            g.memset(same_b[:, :], 1.0).then_inc(s_zeroed, 1)
            g.memset(flip[:, :], 0.0).then_inc(s_zeroed, 1)
            g.memset(ones_row[:, :], 1.0).then_inc(s_const, 1)
            g.iota(iota_i[:, :], pattern=[[1, NE]], base=0, channel_multiplier=0).then_inc(s_const, 1)
            pool.wait_ge(s_zeroed, 3)
            g.affine_select(out=flip[:, :], in_=flip[:, :], compare_op=ALU.not_equal, fill=1.0, base=1 - P,
                            pattern=[[1, P]], channel_multiplier=1).then_inc(s_const, 1)
            g.affine_select(out=ident[:, :], in_=ident[:, :], compare_op=ALU.not_equal, fill=1.0, base=0,
                            pattern=[[-1, P]], channel_multiplier=1).then_inc(s_const, 1)
            blocks = same_b[:, :].rearrange("p (b j) -> p b j", j=G)
            g.affine_select(out=blocks, in_=blocks, compare_op=ALU.is_ge, fill=0.0, base=0,
                            pattern=[[-G, NB], [0, G]], channel_multiplier=1).then_inc(s_zeroed, 1)
            pool.wait_ge(s_zeroed, 4)
            g.affine_select(out=blocks, in_=blocks, compare_op=ALU.is_ge, fill=0.0, base=G - 1,
                            pattern=[[G, NB], [0, G]], channel_multiplier=-1).then_inc(s_const, 1)

            def kv_high(h, p):
                wait(pool, A["vt"], h + 1)
                wait(pool, A["y"], 4 * h - 4)
                g.tensor_tensor(
                    kv[:, p, 1, :].rearrange("p (b i j) -> p b i j", b=NB, i=G),
                    vT[:, p, 1, :].rearrange("p (b i) -> p b i", i=G).unsqueeze(3).to_broadcast([P, NB, G, G]),
                    cols[:, 1, ds(h, 1), :].rearrange("p a (b j) -> p (a b) j", j=G).unsqueeze(2).to_broadcast([P, NB, G, G]),
                    ALU.mult).then_inc(A["kv1"], 1)

            def add_mixed(h, p):
                pool.wait_ge(A["mixed"], h + 1)
                xt = X[:, ds(h * D, D)]
                g.tensor_tensor(xt, xt, mixed[:, p, :], ALU.add).then_inc(A["x"], 1)

            def stage_a(h, p):
                kv_high(h, p)
                if not (isinstance(h, int) and h < 2):
                    add_mixed(h - 2, p)
            pool.wait_ge(s_cols, 16)
            by_two(pool, stage_a, NT, 2)
            for h in range(NT - 2, NT):
                add_mixed(h, h % 2)

            def experts(m):
                s, I = M[m], INNER[m]

                def step(q, j):
                    u = PAIR * q + j
                    if m == 0:
                        pool.wait_ge(s["sig"], u + 1)
                        g.tensor_tensor(sig[:, j % 2, :], gmin[:, j % 2, :], sig[:, j % 2, :], ALU.mult)\
                            .then_inc(s["gs"], 1)
                    pool.wait_ge(s["hhi"], u + 1)
                    wait(pool, s["o"], 2 * u - 6)
                    g.tensor_tensor(h_lo[0:I, j % 4, :], hid[0:I, j % 2, :], h_hi[0:I, j % 4, :].bitcast(fp32),
                                    ALU.subtract).then_inc(s["hlo"], 1)
                by_pair(pool, step)

            experts(0)

            def stage_batch(b, p):
                wait(pool, C["s"], b - 1)
                g.tensor_copy(xs_b[:, p, :, :], xT_b[:, :, ds(b, 1), :].rearrange("p k a s -> p k (a s)"))\
                    .then_inc(C["xs"], 1)
            pool.wait_ge(C["xt"], NT)
            by_two(pool, stage_batch, NB, 2)

            experts(1)

        @block.scalar
        def _(act):
            a = nc.scalar
            act.wait_ge(s_par, 32)
            a.activation(tg[:, :], gate_in[:, :], ACT.Tanh).then_inc(s_tanh, 1)

            def std_of(s):
                act.wait_ge(s["var"], 1)
                a.activation(std[:, :], var_e[:, :], ACT.Sqrt).then_inc(s["sd"], 1)

            for n in range(NT // 2):
                act.wait_ge(A["flip"], n + 1)
                a.activation(toep_all[:, 2 * n:2 * n + 2, :], bank[n % 4][:, :].rearrange("p (a n) -> p a n", a=2),
                             ACT.Copy).then_inc(A["turned"], 1)
            act.wait_ge(A["turned"], NT // 2)
            std_of(A)

            def v_copy(h, p):
                act.wait_ge(A["tr"], h + 1)
                wait(act, A["kv0"], h - 1)
                wait(act, A["kv1"], h - 1)
                a.activation(vT[:, p, :, :], bank[4 + p][:, 0:D].rearrange("p (k n) -> p k n", k=KB), ACT.Copy)\
                    .then_inc(A["vt"], 1)
            def filter_copy(h, p):
                wait(act, A["y"], 4 * h - 4)
                a.activation(toep[:, p, :], toep_all[:, ds(h, 1), :].rearrange("p a n -> p (a n)"), ACT.Copy)\
                    .then_inc(A["tp"], 1)

            def stage_a(h, p):
                filter_copy(h, p)
                v_copy(h, p)
            by_two(act, stage_a, NT, 2)

            act.wait_ge(s_par2, 16 * 7)
            for m in range(2):
                a.activation(rt_hi[m][:, :], rt_raw[m][:, :], ACT.Copy).then_inc(s_rhi, 1)

            def prepare(m):
                s = N[m]
                std_of(s)

                def x_high(t, p):
                    act.wait_ge(s["tr"], t + 1)
                    a.activation(xhi[:, :, ds(t * P, P)], bank[4 + p][:, 0:D].rearrange("p (k n) -> p k n", k=KB),
                                 ACT.Copy).then_inc(s["hi"], 1)
                by_two(act, x_high, NT, 2)
                for c in range(NCH):
                    act.wait_ge(s["lt"], c + 1)
                    dst, src = lgT[:, c * CH:(c + 1) * CH], bank[c][0:NE, :]
                    if m == 0:
                        a.activation(dst, src, ACT.Identity, bias=rt_bias[:, 0:1]).then_inc(s["lg"], 1)
                    else:
                        a.activation(dst, src, ACT.Copy).then_inc(s["lg"], 1)
                act.wait_ge(s["e0"], 1)
                if m == 0:
                    a.activation(tw[:, :, 0:4], tw[:, :, 0:4], ACT.Exp).then_inc(s["e1"], 1)
                    for c in range(NCH):
                        act.wait_ge(s["cwp"], c + 1)
                        a.activation(lgT[:, c * CH:(c + 1) * CH], bank[c][0:NE, :], ACT.Copy).then_inc(s["cwt"], 1)
                else:
                    a.activation(lg2, lg2, ACT.Exp).then_inc(s["e1"], 1)

            def experts(m, width):
                s, I = M[m], INNER[m]

                def split(e, p, n):
                    act.wait_ge(s_w[m][p], 16 * n)
                    wait(act, s["o"], 2 * NCH * (e - 1))
                    a.activation(w_hi[:, p, 0:width], w_raw[:, p, 0:width], ACT.Copy).then_inc(s["whi"], 1)

                def step(q, j):
                    u = PAIR * q + j
                    if m == 0:
                        act.wait_ge(s["gmin"], u + 1)
                        wait(act, s["h"], u - 1)
                        a.activation(sig[:, j % 2, :], gmin[:, j % 2, :], ACT.Sigmoid, scale=ALPHA)\
                            .then_inc(s["sig"], 1)
                    else:
                        act.wait_ge(s["g"], u + 1)
                        wait(act, s["h"], u - 1)
                        a.activation(sig[0:I, j % 2, :], bank[j % 2][0:I, :], ACT.Silu).then_inc(s["sig"], 1)
                    act.wait_ge(s["h"], u + 1)
                    wait(act, s["o"], 2 * u - 6)
                    a.activation(h_hi[0:I, j % 4, :], hid[0:I, j % 2, :], ACT.Copy).then_inc(s["hhi"], 1)
                    if j == 2:
                        split(2 * q + 1, 1, q + 1)
                    if j == 6 and not (isinstance(q, int) and q == NPAIR - 1):
                        split(2 * q + 2, 0, q + 2)
                split(0, 0, 1)
                by_pair(act, step)

            prepare(0)
            experts(0, experts0.shape[2])

            std_of(C)

            def x_cols(t, p):
                act.wait_ge(C["tr"], t + 1)
                a.activation(xT_b[:, :, :, ds(t * G, G)],
                             bank[4 + p][:, 0:D].rearrange("p (k b i) -> p k b i", k=KB, b=NB), ACT.Copy)\
                    .then_inc(C["xt"], 1)
            by_two(act, x_cols, NT, 2)

            def exps(b, p):
                act.wait_ge(C["nb"], b + 1)
                wait(act, C["a"], b - 1)
                a.activation(prob[:, p, :], bank[p][:, 0:P], ACT.Exp, bias=nbias[:, ds(b, 1)], scale=SCALE,
                             accum_out=psum_row[:, ds(b, 1)]).then_inc(C["e"], 1)

            def attn_copy(b, p):
                act.wait_ge(C["at"], b + 1)
                wait(act, C["ro"], b - 1)
                a.activation(attnT[:, p, :], bank[2 + p][:, 0:P], ACT.Copy).then_inc(C["atc"], 1)

            def attend(v, p):
                exps(v, p)
                if not (isinstance(v, int) and v < 1):
                    attn_copy(v - 1, 1 - p)
            by_two(act, attend, NB, 4)
            attn_copy(NB - 1, (NB - 1) % 2)

            prepare(1)
            experts(1, experts1.shape[2])

        @block.tensor
        def _(pe):
            t_ = nc.tensor

            def transposes(s, free, t, p, n_free):
                pe.wait_ge(s["xn"], t + 1)
                wait(pe, free, n_free)
                for k in range(KB):
                    mm = t_.transpose(bank[4 + p][:, k * P:(k + 1) * P], xn[:, p, k * P:(k + 1) * P], ident[:, :])
                mm.then_inc(s["tr"], 1)

            def exact(dst, l_hi, l_lo, r_hi, r_lo, start=True, stop=True, all_four=False):
                parts = [(l_hi, r_hi), (l_hi, r_lo), (l_lo, r_hi)] + [(l_lo, r_lo)] * all_four
                for n, (l, r) in enumerate(parts):
                    mm = t_.matmul(dst, l, r, start=start and n == 0, stop=stop and n == len(parts) - 1)
                return mm

            pe.wait_ge(s_const, 5)
            pe.wait_ge(s_toep, 16)
            for n in range(NT // 2):
                wait(pe, A["turned"], n - 3)
                t_.matmul(bank[n % 4][:, :], flip[:, :], toep_all[:, 2 * n:2 * n + 2, :], start=True, stop=True)\
                    .then_inc(A["flip"], 1)
            pe.wait_ge(s_valid, 1)
            t_.matmul(bank[7][:, 0:NB], ones_row[:, :], valid[:, :], start=True, stop=True).then_inc(s_vb, 1)

            def conv(h, p):
                pe.wait_ge(A["tp"], h + 1)
                for n in range(4):
                    lh, half = n // 2, n % 2
                    if n == 0:
                        pe.wait_ge(A["kv0"], h + 1)
                    if n == 2:
                        pe.wait_ge(A["kv1"], h + 1)
                    wait(pe, A["z"], 4 * h - 3 + n)
                    for k in range(lh + 1):
                        mm = t_.matmul(bank[n][:, :], toep[:, p, (lh - k) * P:(lh - k + 1) * P],
                                       kv[:, p, k, half * 512:(half + 1) * 512], start=(k == 0), stop=(k == lh))
                    mm.then_inc(A["y"], 1)

            def gather_i(h, p):
                pe.wait_ge(A["f2"], 2 * h + 2)
                wait(pe, A["mixed"], h)
                for lh in range(KB):
                    for i in range(2):
                        t_.matmul(bank[6][:, lh * P:(lh + 1) * P],
                                  fold2[:, lh, i * P:(i + 1) * P],
                                  ident[:, :], start=(i == 0), stop=(i == 1))
                pe.wait_ge(A["skv"], h + 1)
                t_.matmul(bank[7][:, 0:D], same_b[:, :], skipv[:, p, :], start=True, stop=True).then_inc(A["out"], 1)

            sA = {"xn": A["vn"], "tr": A["tr"]}

            def stage_a(h, p):
                if not (isinstance(h, int) and h > NT - 3):
                    transposes(sA, A["vt"], h + 2, p, h + 1)
                if not (isinstance(h, int) and h > NT - 2):
                    conv(h + 1, 1 - p)
                gather_i(h, p)

            for t in range(2):
                transposes(sA, A["vt"], t, t, t - 1)
            conv(0, 0)
            pe.wait_ge(s_vb, 1)
            pe.wait_ge(s_tanh, 1)
            for h in range(2):
                stage_a(h, h)
            with pe.Fori(1, NT // 2 - 1, 1) as pair:
                for p in range(2):
                    stage_a(2 * pair + p, p)
            for h in range(NT - 2, NT):
                stage_a(h, h % 2)

            def prepare(m):
                s = N[m]
                by_two(pe, lambda t, p: transposes(s, s["lo"], t, p, t - 1), NT, 2)
                pe.wait_ge(s["lo"], NT)
                pe.wait_ge(s_rlo, m + 1)
                for c in range(NCH):
                    at = slice(c * CH, (c + 1) * CH)
                    for k in range(KB):
                        ks = slice(k * P, (k + 1) * P)
                        mm = exact(bank[c][:, :], rt_hi[m][:, ks], rt_lo[m][:, ks], xhi[:, k, at], xlo[:, k, at],
                                   start=(k == 0), stop=(k == KB - 1), all_four=True)
                    mm.then_inc(s["lt"], 1)
                pe.wait_ge(s["lg"], NCH)
                for t in range(NT):
                    mm = t_.matmul(bank[4][:, t * NE:(t + 1) * NE], lgT[:, t * P:(t + 1) * P], ident[0:NE, 0:NE],
                                   start=True, stop=True)
                mm.then_inc(s["l"], 1)
                if m == 0:
                    pe.wait_ge(s["cw"], 1)
                    for t in range(NT):
                        c, n = divmod(t, TPC)
                        mm = t_.matmul(bank[c][0:NE, n * P:(n + 1) * P], cw[:, t * NE:(t + 1) * NE], ident[:, :],
                                       start=True, stop=True)
                        if n == TPC - 1:
                            mm.then_inc(s["cwp"], 1)
                    pe.wait_ge(s["cwt"], NCH)
                    for n in range(NT // 2):
                        wait(pe, s["bdx"], n - 1)
                        for t in range(2):
                            at = (2 * n + t) * P
                            mm = t_.matmul(bank[4 + n % 2][:, t * D:(t + 1) * D], lgT[:, at:at + P], down_b[:, :],
                                           start=True, stop=True)
                        mm.then_inc(s["bd"], 1)
                    pe.wait_ge(s["bdx"], NT // 2)

            def experts(m):
                s, I = M[m], INNER[m]
                g_read, u_read = (s["gmin"], s["umin"]) if m == 0 else (s["sig"], s["h"])

                def gate_up(q, j):
                    u, p, c = PAIR * q + j, j // NCH, j % NCH
                    at = slice(c * CH, (c + 1) * CH)
                    if c == 0:
                        pe.wait_ge(s["wlo"], 2 * q + p + 1)
                    for n, (read, done) in enumerate(((g_read, s["g"]), (u_read, s["u"]))):
                        wait(pe, read, u - 1)
                        for k in range(KB):
                            ks = slice((2 * n + k) * I, (2 * n + k + 1) * I)
                            mm = exact(bank[2 * n + j % 2][0:I, :], w_hi[:, p, ks], w_lo[:, p, ks],
                                       xhi[:, k, at], xlo[:, k, at], start=(k == 0), stop=(k == KB - 1))
                        mm.then_inc(done, 1)

                def down(u, j):
                    p = j // NCH
                    ks = slice(4 * I, 4 * I + D)
                    pe.wait_ge(s["hlo"], u + 1)
                    wait(pe, s["acc"], TPC * (u - 1))
                    for t in range(TPC):
                        hs = slice(t * P, (t + 1) * P)
                        mm = exact(bank[4 + 2 * (j % 2) + t // 2][:, (t % 2) * D:(t % 2 + 1) * D],
                                   h_hi[0:I, j % 4, hs], h_lo[0:I, j % 4, hs],
                                   w_hi[0:I, p, ks], w_lo[0:I, p, ks])
                        if t % 2:
                            mm.then_inc(s["o"], 1)

                def step(q, j):
                    gate_up(q, j)
                    if not (isinstance(q, int) and q == 0 and j < 2):
                        down(PAIR * q + j - 2, (j - 2) % PAIR)
                by_pair(pe, step)
                for u in range(UNITS - 2, UNITS):
                    down(u, u % PAIR)

            prepare(0)
            experts(0)

            by_two(pe, lambda t, p: transposes(C, C["xt"], t, p, t - 1), NT, 2)

            def scores(b, p):
                pe.wait_ge(C["xs"], b + 1)
                wait(pe, C["e"], b - 1)
                dst = bank[p][:, 0:P]
                t_.matmul(dst, ones_row[:, :], mbias[:, ds(b * P, P)], start=True, stop=False)
                for k in range(KB):
                    mm = t_.matmul(dst, xs_b[:, p, k, :], cols[:, k, :, ds(b * G, G)], start=False, stop=(k == KB - 1))
                mm.then_inc(C["s"], 1)

            def attn_turn(b, p):
                pe.wait_ge(C["a"], b + 1)
                wait(pe, C["atc"], b - 1)
                t_.transpose(bank[2 + p][:, 0:P], attn[:, p, :], ident[:, :]).then_inc(C["at"], 1)

            def readout(b, p, count):
                pe.wait_ge(C["atc"], b + 1)
                pe.wait_ge(s_mem[p], 16 * count)
                wait(pe, C["rot"], b - 1)
                for k in range(KB):
                    mm = t_.matmul(bank[4 + p][:, k * P:(k + 1) * P], mem_b[:, p, k * P:(k + 1) * P], attnT[:, p, :],
                                   start=True, stop=True)
                mm.then_inc(C["ro"], 1)

            def attend(v, p, count):
                scores(v, p)
                if not (isinstance(v, int) and v < 1):
                    attn_turn(v - 1, 1 - p)
                if not (isinstance(v, int) and v < 2):
                    readout(v - 2, p, count)
            for v in range(4):
                attend(v, v % 2, v // 2)
            with pe.Fori(2, NB // 2, 1) as vp:
                for p in range(2):
                    attend(2 * vp + p, p, vp)
            attn_turn(NB - 1, 1)
            readout(NB - 2, 0, NB // 2)
            readout(NB - 1, 1, NB // 2)
            pe.wait_ge(C["rot"], NB)
            for n in range(NT // 2):
                wait(pe, C["x"], n - 1)
                for t in range(2):
                    for k in range(KB):
                        mm = t_.transpose(bank[6 + n % 2][:, (t * KB + k) * P:(t * KB + k + 1) * P],
                                          roT[:, k, 2 * n + t, :], ident[:, :])
                mm.then_inc(C["fx"], 1)

            prepare(1)
            experts(1)

        @block.vector
        def _(dve):
            v = nc.vector
            chain = [0]

            def link(ins):
                chain[0] += 1
                ins.then_inc(s_chain, 1)
                dve.wait_ge(s_chain, chain[0])

            def token_stats(s):
                for t in range(NT):
                    last = v.bn_stats(stats[:, t, :], X[:, t * D:(t + 1) * D])
                link(last)
                for t in range(NT):
                    last = v.bn_aggr(mv[:, 2 * t:2 * t + 2], stats[:, t, :])
                link(last)
                v.tensor_scalar(var_e[:, :], mv[:, 1:2 * NT:2], EPS, None, ALU.add).then_inc(s["var"], 1)
                dve.wait_ge(s["sd"], 1)
                link(v.reciprocal(rstd[:, :], std[:, :]))
                link(v.tensor_tensor(newt[:, :], rstd[:, :], rstd[:, :], ALU.mult))
                link(v.tensor_tensor(newt[:, :], newt[:, :], var_e[:, :], ALU.mult))
                link(v.tensor_scalar(newt[:, :], newt[:, :], -0.5, 1.5, ALU.mult, ALU.add))
                link(v.tensor_tensor(rstd[:, :], rstd[:, :], newt[:, :], ALU.mult))

            def normalise(s, t, p, free, n_free):
                wait(dve, free, n_free)
                v.tensor_scalar(xn[:, p, :], X[:, ds(t * D, D)], mv[:, ds(2 * t, 1)], rstd[:, ds(t, 1)],
                                ALU.subtract, ALU.mult).then_inc(s["xn"], 1)

            dve.wait_ge(s_x, 16)
            token_stats(A)
            dve.wait_ge(s_const, 5)
            v.tensor_copy(iota_f[:, :], iota_i[:, :])
            dve.wait_ge(s_par2, 16 * 7)
            v.tensor_scalar(up_b1[:, :], up_b[:, :], 1.0, None, ALU.add)
            link(v.tensor_copy(mbias[:, :], mask_u8[:, :]))
            v.tensor_reduce(valid[:, :], mbias[:, :].rearrange("a (b s) -> a b s", b=NB), AX.X, ALU.max)\
                .then_inc(s_valid, 1)
            dve.wait_ge(s_valid, 1)
            link(v.tensor_scalar(mbias[:, :], mbias[:, :], -1.0, NEG, ALU.add, ALU.mult))
            dve.wait_ge(s_vb, 1)
            dve.wait_ge(s_tanh, 1)
            link(v.tensor_scalar(valid_t[:, :], bank[7][:, 0:NB], tg[:, 1:2], None, ALU.mult))

            sA = {"xn": A["vn"]}

            def v_rows(h, p):
                wait(dve, A["skv"], h - 1)
                normalise(sA, h, p, A["tr"], h - 1)

            def skip_rows(h, p):
                dve.wait_ge(A["vn"], h + 1)
                wait(dve, A["out"], h - 1)
                v.scalar_tensor_tensor(out=skipv[:, p, :], in0=xn[:, p, :], scalar=skc[:, ds(h, 1)],
                                       in1=rows[:, ds(h * D, D)], op0=ALU.mult, op1=ALU.mult)\
                    .then_inc(A["skv"], 1)

            def kv_low(h, p):
                dve.wait_ge(A["vt"], h + 1)
                wait(dve, A["y"], 4 * h - 4)
                v.tensor_tensor(
                    kv[:, p, 0, :].rearrange("p (b i j) -> p b i j", b=NB, i=G),
                    vT[:, p, 0, :].rearrange("p (b i) -> p b i", i=G).unsqueeze(3).to_broadcast([P, NB, G, G]),
                    cols[:, 0, ds(h, 1), :].rearrange("p a (b j) -> p (a b) j", j=G).unsqueeze(2).to_broadcast([P, NB, G, G]),
                    ALU.mult).then_inc(A["kv0"], 1)

            def mix_out(h, p):
                dve.wait_ge(A["out"], h + 1)
                wait(dve, A["x"], h - 1)
                v.scalar_tensor_tensor(out=mixed[:, p, :], in0=bank[7][:, 0:D], scalar=tg[:, 0:1],
                                       in1=rows[:, ds(h * D, D)], op0=ALU.mult, op1=ALU.mult).then_inc(A["mix"], 1)
                dve.wait_ge(A["mix"], h + 1)
                v.scalar_tensor_tensor(out=mixed[:, p, :], in0=bank[6][:, 0:D], scalar=tg[:, 0:1],
                                       in1=mixed[:, p, :], op0=ALU.mult, op1=ALU.add).then_inc(A["mixed"], 1)

            def times_x1(h, p):
                for n in range(4):
                    lh, half = n // 2, n % 2
                    dve.wait_ge(A["y"], 4 * h + n + 1)
                    wait(dve, A["f1"], 2 * h - 1 + lh)
                    v.tensor_tensor(
                        prod[:, lh, half * 512:(half + 1) * 512].rearrange("p (n j) -> p n j", j=G),
                        bank[n][:, :].rearrange("p (n j) -> p n j", j=G),
                        cols[:, lh, ds(h, 1), half * 64:(half + 1) * 64].rearrange("p a n -> p (a n)").unsqueeze(2)
                        .to_broadcast([P, 64, G]),
                        ALU.mult).then_inc(A["z"], 1)
                    if half:
                        dve.wait_ge(A["z"], 4 * h + n + 1)
                        wait(dve, A["f2"], 2 * h - 1 + lh)
                        z = prod[:, lh, :].rearrange("p (b i n) -> p b i n", b=NB, i=2)
                        v.tensor_tensor(fold1[:, lh, :].rearrange("p (b n) -> p b n", b=NB), z[:, :, 0, :],
                                        z[:, :, 1, :], ALU.add).then_inc(A["f1"], 1)
                for lh in range(KB):
                    dve.wait_ge(A["f1"], 2 * h + lh + 1)
                    wait(dve, A["out"], h)
                    z = fold1[:, lh, :].rearrange("p (b a i j) -> p a i b j", b=NB, a=2, i=2)
                    v.tensor_tensor(fold2[:, lh, :].rearrange("p (i b j) -> p i b j", i=2, b=NB), z[:, 0, :, :, :],
                                    z[:, 1, :, :, :], ALU.add).then_inc(A["f2"], 1)

            def stage_a(h, p):
                static = isinstance(h, int)
                if not (static and h > NT - 3):
                    v_rows(h + 2, p)
                if not (static and h > NT - 2):
                    kv_low(h + 1, 1 - p)
                if not (static and h < 1):
                    mix_out(h - 1, 1 - p)
                if not (static and h > NT - 2):
                    skip_rows(h + 1, 1 - p)
                times_x1(h, p)

            dve.wait_ge(s_par, 32)
            dve.wait_ge(s_ctx, 16)
            for h in range(2):
                v_rows(h, h)
            skip_rows(0, 0)
            dve.wait_ge(s_cols, 16)
            kv_low(0, 0)
            for h in range(2):
                stage_a(h, h)
            with dve.Fori(1, NT // 2 - 1, 1) as pair:
                for p in range(2):
                    stage_a(2 * pair + p, p)
            for h in range(NT - 2, NT):
                stage_a(h, h % 2)
            mix_out(NT - 1, 1)
            dve.wait_ge(A["x"], NT)

            for m in range(2):
                dve.wait_ge(s_rhi, m + 1)
                v.tensor_tensor(rt_lo[m][:, :], rt_raw[m][:, :], rt_hi[m][:, :].bitcast(fp32), ALU.subtract)\
                    .then_inc(s_rlo, 1)

            def over_k(a, k):
                return a.unsqueeze(2).to_broadcast([P, NT, k])

            def prepare(m):
                s, K = N[m], TOPK[m]
                token_stats(s)

                def x_low(t, p):
                    dve.wait_ge(s["hi"], t + 1)
                    v.tensor_tensor(xlo[:, :, ds(t * P, P)], bank[4 + p][:, 0:D].rearrange("p (k n) -> p k n", k=KB),
                                    xhi[:, :, ds(t * P, P)].bitcast(fp32), ALU.subtract).then_inc(s["lo"], 1)

                def step(t, p):
                    normalise(s, t, p, s["tr"], t - 1)
                    if not (isinstance(t, int) and t < 1):
                        x_low(t - 1, 1 - p)
                by_two(dve, step, NT, 2)
                x_low(NT - 1, 1)

                dve.wait_ge(s["l"], 1)
                link(v.tensor_copy(lg2, bank[4][:, :]))
                if m == 1:
                    link(v.tensor_reduce(row1[:, :], lg[:, :, :], AX.X, ALU.max))
                    v.tensor_tensor(lg[:, :, :], lg[:, :, :], over_k(row1[:, :], NE), ALU.subtract).then_inc(s["e0"], 1)
                    dve.wait_ge(s["e1"], 1)
                    link(v.tensor_reduce(row1[:, :], lg[:, :, :], AX.X, ALU.add))
                    link(v.reciprocal(row2[:, :], row1[:, :]))
                    link(v.tensor_tensor(lg[:, :, :], lg[:, :, :], over_k(row2[:, :], NE), ALU.mult))
                for t in range(NT):
                    last = v.max(top[:, t, :], lg[:, t, :])
                link(last)
                for t in range(NT):
                    last = v.max_index(top_i[:, t, :], top[:, t, :], lg[:, t, :])
                link(last)
                v.tensor_copy(top_f[:, :, :], top_i[:, :, :])
                wk = tw[:, :, 0:K]
                if m == 0:
                    v.tensor_tensor(wk, top[:, :, 0:K], over_k(top[:, :, 0:1].rearrange("p t a -> p (t a)"), K),
                                    ALU.subtract).then_inc(s["e0"], 1)
                    dve.wait_ge(s["e1"], 1)
                else:
                    link(v.tensor_reduce(row1[:, :], top[:, :, :], AX.X, ALU.add))
                    link(v.tensor_scalar(row1[:, :], row1[:, :], 1e-12, None, ALU.max))
                    link(v.reciprocal(row2[:, :], row1[:, :]))
                    link(v.tensor_tensor(tcum[:, :, :], top[:, :, :], over_k(row2[:, :], K), ALU.mult))
                    for k in range(1, K):
                        link(v.tensor_tensor(tcum[:, :, k], tcum[:, :, k], tcum[:, :, k - 1], ALU.add))
                    v.tensor_copy(tw[:, :, 0:1], top[:, :, 0:1])
                    link(v.scalar_tensor_tensor(out=tw[:, :, 1:K], in0=tcum[:, :, 0:K - 1], scalar=THRESHOLD,
                                                in1=top[:, :, 1:K], op0=ALU.is_lt, op1=ALU.mult))
                link(v.tensor_reduce(row1[:, :], wk, AX.X, ALU.add))
                link(v.tensor_scalar(row1[:, :], row1[:, :], 1e-12, None, ALU.max))
                link(v.reciprocal(row2[:, :], row1[:, :]))
                link(v.tensor_scalar(row2[:, :], row2[:, :], tg[:, 2 + m:3 + m], None, ALU.mult))
                link(v.tensor_tensor(wk, wk, over_k(row2[:, :], K), ALU.mult))
                hot = one_hot[:, 0:NT * K * NE].rearrange("p (t k e) -> p t k e", t=NT, k=K)
                full = [P, NT, K, NE]
                link(v.tensor_tensor(hot, iota_f[:, :].unsqueeze(1).unsqueeze(1).to_broadcast(full),
                                     top_f[:, :, 0:K].unsqueeze(3).to_broadcast(full), ALU.is_equal))
                link(v.tensor_tensor(hot, hot, wk.unsqueeze(3).to_broadcast(full), ALU.mult))
                v.tensor_reduce(cw[:, :].rearrange("p (t e) -> p t e", t=NT), hot.rearrange("p t k e -> p t e k"),
                                AX.X, ALU.add).then_inc(s["cw"], 1)
                dve.wait_ge(s["cw"], 1)
                if m == 0:
                    for n in range(NT // 2):
                        dve.wait_ge(s["bd"], n + 1)
                        xt = X[:, 2 * n * D:2 * (n + 1) * D]
                        v.tensor_tensor(xt, xt, bank[4 + n % 2][:, :], ALU.add).then_inc(s["bdx"], 1)
                    dve.wait_ge(s["bdx"], NT // 2)

            def experts(m, width):
                s, I = M[m], INNER[m]

                def split(e, p):
                    dve.wait_ge(s["whi"], e + 1)
                    v.tensor_tensor(w_lo[:, p, 0:width], w_raw[:, p, 0:width], w_hi[:, p, 0:width].bitcast(fp32),
                                    ALU.subtract).then_inc(s["wlo"], 1)

                def accumulate(u, e, j):
                    for t in range(TPC):
                        tile = (j % NCH) * TPC + t
                        if t % 2 == 0:
                            dve.wait_ge(s["o"], 2 * u + t // 2 + 1)
                        xt = X[:, tile * D:(tile + 1) * D]
                        v.scalar_tensor_tensor(out=xt, in0=bank[4 + 2 * (j % 2) + t // 2][:, (t % 2) * D:(t % 2 + 1) * D],
                                               scalar=cw[:, ds(tile * NE + e, 1)], in1=xt, op0=ALU.mult, op1=ALU.add)\
                            .then_inc(s["acc"], 1)

                def step(q, j):
                    u, first = PAIR * q + j, isinstance(q, int) and q == 0
                    e = 2 * q + j // NCH
                    if m == 0:
                        dve.wait_ge(s["g"], u + 1)
                        wait(dve, s["gs"], u - 1)
                        v.tensor_scalar(gmin[:, j % 2, :], bank[j % 2][:, :], gate_b[:, ds(e, 1)], LIMIT,
                                        ALU.add, ALU.min).then_inc(s["gmin"], 1)
                        dve.wait_ge(s["u"], u + 1)
                        wait(dve, s["h"], u - 1)
                        v.tensor_scalar(umin[:, j % 2, :], bank[2 + j % 2][:, :], up_b1[:, ds(e, 1)], LIMIT + 1.0,
                                        ALU.add, ALU.min).then_inc(s["umin"], 1)
                    if not (first and j < 3):
                        accumulate(u - 3, 2 * q + (j - 3) // NCH, (j - 3) % PAIR)
                    wait(dve, s["hlo"], u - 1)
                    if m == 0:
                        dve.wait_ge(s["gs"], u + 1)
                        dve.wait_ge(s["umin"], u + 1)
                        v.scalar_tensor_tensor(out=hid[:, j % 2, :], in0=umin[:, j % 2, :], scalar=1.0 - LIMIT,
                                               in1=sig[:, j % 2, :], op0=ALU.max, op1=ALU.mult).then_inc(s["h"], 1)
                    else:
                        dve.wait_ge(s["sig"], u + 1)
                        dve.wait_ge(s["u"], u + 1)
                        v.tensor_tensor(hid[0:I, j % 2, :], sig[0:I, j % 2, :], bank[2 + j % 2][0:I, :], ALU.mult)\
                            .then_inc(s["h"], 1)
                    if j == 2:
                        split(2 * q + 1, 1)
                    if j == 6 and not (isinstance(q, int) and q == NPAIR - 1):
                        split(2 * q + 2, 0)

                split(0, 0)
                by_pair(dve, step)
                for u in range(UNITS - 3, UNITS):
                    accumulate(u, u // NCH, u % PAIR)
                dve.wait_ge(s["acc"], TPC * UNITS)

            prepare(0)
            experts(0, experts0.shape[2])

            token_stats(C)
            by_two(dve, lambda t, p: normalise(C, t, p, C["tr"], t - 1), NT, 2)

            def row_max(b, p):
                dve.wait_ge(C["s"], b + 1)
                v.tensor_reduce(smax[:, ds(b, 1)], bank[p][:, 0:P], AX.X, ALU.max).then_inc(C["mx"], 1)
                dve.wait_ge(C["mx"], b + 1)
                v.tensor_scalar(nbias[:, ds(b, 1)], smax[:, ds(b, 1)], -SCALE, None, ALU.mult).then_inc(C["nb"], 1)

            def scale_rows(b, p):
                dve.wait_ge(C["e"], b + 1)
                v.reciprocal(rinv[:, ds(b, 1)], psum_row[:, ds(b, 1)]).then_inc(C["ri"], 1)
                dve.wait_ge(C["ri"], b + 1)
                wait(dve, C["at"], b - 1)
                v.tensor_scalar(attn[:, p, :], prob[:, p, :], rinv[:, ds(b, 1)], valid_t[:, ds(b, 1)],
                                ALU.mult, ALU.mult).then_inc(C["a"], 1)

            def read_copy(b, p):
                dve.wait_ge(C["ro"], b + 1)
                v.tensor_copy(roT[:, :, :, ds(b * G, G)],
                              bank[4 + p][:, 0:D].rearrange("p (k h i) -> p k h i", k=KB, h=NT)).then_inc(C["rot"], 1)

            def attend(b, p):
                row_max(b, p)
                if not (isinstance(b, int) and b < 1):
                    scale_rows(b - 1, 1 - p)
                if not (isinstance(b, int) and b < 2):
                    read_copy(b - 2, p)
            by_two(dve, attend, NB, 4)
            scale_rows(NB - 1, 1)
            read_copy(NB - 2, 0)
            read_copy(NB - 1, 1)
            for n in range(NT // 2):
                dve.wait_ge(C["fx"], n + 1)
                xt = X[:, 2 * n * D:2 * (n + 1) * D]
                v.tensor_tensor(xt, xt, bank[6 + n % 2][:, :], ALU.add).then_inc(C["x"], 1)
            dve.wait_ge(C["x"], NT // 2)

            prepare(1)
            experts(1, experts1.shape[2])


def kernel(**inputs):
    import numpy as np
    import concourse.bacc as bacc
    from concourse.bass_utils import run_bass_kernel_spmd as run

    a = {k: np.asarray(v) for k, v in inputs.items()}
    x, c = a["x"], a["ctx_2048"]
    B, S, D = x.shape
    NT = a["L0_xattn_k"].shape[0]
    G = S // NT
    P, KB, E = 128, D // 128, a["L0_ffn_gate_w"].shape[0]

    def rows(t):
        return t.reshape(B, NT, G, D).transpose(0, 2, 1, 3).reshape(B * G, NT, D)

    def router(w):
        t = w.T.reshape(KB, P, E).transpose(1, 0, 2)
        return np.concatenate([t, np.zeros((P, KB, P - E), w.dtype)], axis=2).reshape(P, KB * P)

    def halves(w):
        return w.reshape(E, KB, P, -1).transpose(0, 2, 1, 3).reshape(E, P, -1)

    gu = a["L1_ffn_gate_up_proj"].transpose(0, 2, 1)
    I1 = gu.shape[2] // 2
    down1 = a["L1_ffn_down_proj"].transpose(0, 2, 1)
    down1 = np.concatenate([down1, np.zeros((E, P - I1, D), down1.dtype)], axis=1)
    k = a["L0_xattn_k"]
    arrays = {
        "x_rows": rows(x),
        "ctx_rows": rows(c),
        "ctx_cols": rows(c).transpose(2, 1, 0).reshape(KB, P, NT, P).transpose(1, 0, 2, 3),
        "ctx_batch": c,
        "filt": np.concatenate([np.zeros((NT, P), k.dtype), k], axis=1),
        "skip_cols": np.tile(a["fside_S2_0"].reshape(NT, G).T, (B, 1)),
        "mask": a["mask_BxS2_bk0"].reshape(1, B * S),
        "gates": np.concatenate([a["g_xattn"], a["g_ffn"]]),
        "router0": router(a["L0_ffn_gate_w"]),
        "router0_bias": a["L0_ffn_gate_b"].reshape(E, 1),
        "gate_bias0": a["L0_ffn_b_gate"].T,
        "up_bias0": a["L0_ffn_b_up"].T,
        "down_bias0": a["L0_ffn_b_down"],
        "experts0": np.concatenate([halves(a["L0_ffn_w_gate"]), halves(a["L0_ffn_w_up"]), a["L0_ffn_w_down"]], axis=2),
        "router1": router(a["L1_ffn_gate_weight"]),
        "experts1": np.concatenate([halves(gu[:, :, :I1]), halves(gu[:, :, I1:]), down1], axis=2),
    }
    arrays = {f"in_{n}": np.ascontiguousarray(v) for n, v in arrays.items()}
    nc = bacc.Bacc("TRN2", target_bir_lowering=False, num_devices=1)
    args = [nc.dram_tensor(n, v.shape, mybir.dt.from_np(v.dtype), kind="ExternalInput").ap() for n, v in arrays.items()]
    args.append(nc.dram_tensor("out", (P, NT, D), mybir.dt.from_np(x.dtype), kind="ExternalOutput").ap())
    bass_flamingo_gated_two_layers_kernel(nc, *args)
    got = run(nc, [arrays], core_ids=[0]).results[0]["out"]
    return got.reshape(B, G, NT, D).transpose(0, 2, 1, 3).reshape(B, S, D)
```

```python
import concourse.bass as bass
from concourse import mybir
from contextlib import ExitStack


def bass_flamingo_gated_two_layers_kernel(
    nc: bass.Bass,
    x_rows: bass.AP,
    ctx_rows: bass.AP,
    ctx_cols: bass.AP,
    ctx_batch: bass.AP,
    filt: bass.AP,
    skip_cols: bass.AP,
    mask: bass.AP,
    gates: bass.AP,
    router0: bass.AP,
    router0_bias: bass.AP,
    in_bias0: bass.AP,
    down_bias0: bass.AP,
    experts0: bass.AP,
    router1: bass.AP,
    experts1: bass.AP,
    out: bass.AP,
):
    fp32 = mybir.dt.float32
    fp32r = mybir.dt.float32r
    u32 = mybir.dt.uint32
    i32 = mybir.dt.int32
    u8 = mybir.dt.uint8
    ALU = mybir.AluOpType
    ACT = mybir.ActivationFunctionType
    AX = mybir.AxisListType
    ds = bass.ds

    P = 128
    NT = x_rows.shape[1]
    D = x_rows.shape[2]
    KB = D // P
    NB = ctx_batch.shape[0]
    G = P // NB
    TOK = NT * P
    NE = experts0.shape[1]
    CH = 512
    NCH = TOK // CH
    TPC = CH // P
    ROWS = TOK + P
    REG = NE + 1
    BODY = 4
    WR = D + 2
    OFF = 1 << 20
    SMAX = 2 * P
    EPS = 1e-5
    LIMIT = 7.0
    ALPHA = 1.702
    NEG = 1e30
    TOPK = (4, 8)
    THRESHOLD = 0.8
    INNER = (128, 96)
    SCALE = float(D) ** -0.5

    ctx = ExitStack()
    with ctx:
        def sb(name, shape, dt=fp32):
            return ctx.enter_context(nc.sbuf_tensor(name, shape, dt))

        def sem(name):
            return ctx.enter_context(nc.semaphore(name))

        def sems(prefix, names):
            return {n: sem(f"{prefix}_{n}") for n in names.split()}

        X = sb("X", [P, NT * D])
        cols = sb("cols", [P, KB, NT, P])
        scratch = sb("scratch", [P, 4096])
        big = sb("big", [P, NT * WR])
        wts = sb("wts", [P, NE * 6 * P])
        toep = sb("toep", [P, 2, D])
        xn = sb("xn", [P, 2, D])
        vT = sb("vT", [P, 2, KB, P])
        prod = sb("prod", [P, KB, 1024])
        fold1 = sb("fold1", [P, KB, 512])
        fold2 = sb("fold2", [P, KB, 256])
        skipv = sb("skipv", [P, 2, D])
        mixed = sb("mixed", [P, 2, D])
        skc = sb("skc", [P, NT])
        stats = sb("stats", [P, NT, 6])
        mv = sb("mv", [P, NT * 2])
        var_e = sb("var_e", [P, NT])
        std = sb("std", [P, NT])
        rstd = sb("rstd", [P, NT])
        newt = sb("newt", [P, NT])
        ident = sb("ident", [P, P])
        flip = sb("flip", [P, P])
        same_b = sb("same_b", [P, P])
        ones = sb("ones", [P, P])
        before = sb("before", [P, P])
        eye2 = sb("eye2", [2 * NE, NE])
        pad_row = sb("pad_row", [P, WR])
        steps_i = sb("steps_i", [P, NT - 1], i32)
        steps_f = sb("steps_f", [P, NT - 1])
        region_f = sb("region_f", [P, NE])
        tile_i = sb("tile_i", [P, 2], i32)
        tile_f = sb("tile_f", [P, 2])
        iota_i = sb("iota_i", [P, NE], i32)
        iota_f = sb("iota_f", [P, NE])
        gate_in = sb("gate_in", [P, 4])
        tg = sb("tg", [P, 4])
        mask_u8 = sb("mask_u8", [1, NB * P], u8)
        mrow = sb("mrow", [1, 2, P])
        valid = sb("valid", [1, NB])
        valid_t = sb("valid_t", [P, NB])
        rt = [sb(f"rt{m}", [P, KB * NE]) for m in range(2)]
        rt_bias = sb("rt_bias", [NE, 1])
        in_b = sb("in_b", [2 * NE, 2 * P])
        in_bp = sb("in_bp", [2 * NE, 2 * P], fp32r)
        down_b = sb("down_b", [NE, D])
        top = sb("top", [P, NT, 8])
        top_i = sb("top_i", [P, NT, 8], u32)
        top_f = sb("top_f", [P, NT, 8])
        tw = sb("tw", [P, NT, 8])
        tcum = sb("tcum", [P, NT, 8])
        row1 = sb("row1", [P, NT])
        row2 = sb("row2", [P, NT])
        pref = sb("pref", [P, NT + 1, NE])
        pos_k = sb("pos_k", [P, NT, 8])
        act_k = sb("act_k", [P, NT, 8])
        cnt_k = sb("cnt_k", [P, 8])
        pos_i = sb("pos_i", [P, NT, 8], i32)
        idx_now = sb("idx_now", [P, NT], i32)
        n_tiles = sb("n_tiles", [P, NE])
        cum = sb("cum", [P, 2, NE // 2 + NE])
        le = sb("le", [P, 2, NE])
        le_n = sb("le_n", [P, 2, NE])
        tab = sb("tab", [P, 4])
        past = sb("past", [P, 2])
        tab_i = sb("tab_i", [1, 4 * P], i32)
        cnt_i = sb("cnt_i", [1, NE + 2], i32)
        sel = sb("sel", [2 * NE, 2, 2, P], fp32r)
        idx_y = sb("idx_y", [P, 2, 2], i32)
        idle = sb("idle", [1, 1])
        smax = sb("smax", [P, NB])
        nbias = sb("nbias", [P, NB])
        psum_row = sb("psum_row", [P, NB])
        rinv = sb("rinv", [P, NB])

        kv = scratch[:, :].rearrange("p (s k n) -> p s k n", s=2, k=KB)
        rows = big[:, 0:NT * D]
        late = NE * 6 * P - NE // 4 * 6 * P
        toep_all = wts[:, late:late + NT * D].rearrange("p (t n) -> p t n", t=NT)
        send = big[:, :].rearrange("p (t n) -> p t n", t=NT)
        xT_all = scratch[:, :].rearrange("p (k n) -> p k n", k=KB)
        lgT = prod[0:NE, :, :].rearrange("p k n -> p (k n)")
        lg = toep[:, :, :].rearrange("p s (t e) -> p (s t) e", e=NE)
        mask_e = skipv[:, :, :].rearrange("p s n -> p (s n)")
        posn = vT[:, :, :, :].rearrange("p s k n -> p (s k n)")
        tot = mixed[:, :, :].rearrange("p s (t e) -> p (s t) e", e=NE)
        cw = fold2[:, :, :].rearrange("p k n -> p (k n)")
        no_row = pad_row[:, 0:D]
        one_hot = scratch[:, :]
        xT_b = scratch[:, :].rearrange("p (k b s) -> p k b s", k=KB, b=NB)
        one_hot_2 = fold1[:, :, :].rearrange("p k n -> p (k n)")
        acc1 = scratch[:, :]
        work = fold1[:, :, :].rearrange("p k n -> p (k n)")
        gmin = work[:, 0:512].rearrange("p (s t n) -> p s t n", s=2, t=2)
        umin = work[:, 512:1024].rearrange("p (s t n) -> p s t n", s=2, t=2)
        at = 4 * WR
        xt = X[:, 0:at].rearrange("p (s t n) -> p s t n", s=2, t=2)
        xT = X[:, at:at + 4 * D].rearrange("p (s n) -> p s n", s=2)
        y = X[:, at + 4 * D:at + 8 * D].rearrange("p (s t n) -> p s t n", s=2, t=2)
        tails = X[:, at + 8 * D:at + 8 * D + 2 * SMAX].rearrange("p (s n) -> p s n", n=2)
        sig = vT[:, :, :, :]
        hid = skipv[:, :, :].rearrange("p s (t n) -> p s t n", t=2)
        hT = mixed[:, :, :].rearrange("p s (t n) -> p s t n", t=2)
        turn = prod[:, :, :].rearrange("p k n -> p (k n)")
        xs_b = turn[:, 0:512].rearrange("p (s k n) -> p s k n", s=2, k=KB)
        mem_b = turn[:, 512:1024].rearrange("p (s n) -> p s n", s=2)
        prob = turn[:, 1024:1280].rearrange("p (s n) -> p s n", s=2)
        attn = turn[:, 1280:1536].rearrange("p (s n) -> p s n", s=2)
        attnT = turn[:, 1536:1792].rearrange("p (s n) -> p s n", s=2)
        roT = rows[:, :].rearrange("p (k h s) -> p k h s", k=KB, h=NT)
        lg2 = lg[:, :, :].rearrange("p t e -> p (t e)")

        bank = [ctx.enter_context(nc.psum_tensor(f"bank{i}", [P, 512], fp32)) for i in range(8)]

        s_x = sem("s_x")
        s_ctx = sem("s_ctx")
        s_cols = sem("s_cols")
        s_par = sem("s_par")
        s_par2 = sem("s_par2")
        s_toep = sem("s_toep")
        s_mem = [sem(f"s_mem{p}") for p in range(2)]
        s_w = [sem(f"s_w{m}") for m in range(2)]
        s_const = sem("s_const")
        s_tanh = sem("s_tanh")
        s_bias = sem("s_bias")
        s_tok = sem("s_tok")
        s_valid = sem("s_valid")
        s_vb = sem("s_vb")
        s_out = sem("s_out")
        s_chain = sem("s_chain")
        s_zeroed = sem("s_zeroed")
        A = sems("A", "var sd flip turned tp vn skv tr vt kv0 kv1 y z f1 f2 out mix mixed x")
        N = [sems(f"N{m}", "var sd xn cp tr xt lt lg l e0 e1 mk rk cw cwp cwt bd bdx tb tp tab send now") for m in range(2)]
        M = [sems(f"M{m}", "fill init dsp ld0 ld1 tx tail xt sel gu gmin umin sig gs h ht htc dn y ix sc0 sc1 rd0 rd1 rd2 rd3 x")
             for m in range(2)]
        C = sems("C", "var sd xn tr xt xs s mr mx nb e ri a at atc ro rot fx x")

        sent = nc.dram_tensor("sent", (REG * ROWS, WR), fp32, kind="Internal").ap()
        acc = [nc.dram_tensor(f"acc{r}", (TOK + P, D), fp32, kind="Internal").ap() for r in range(2)]

        block = ctx.enter_context(nc.Block())

        def wait(eng, s, n):
            if isinstance(n, int) and n <= 0:
                return
            eng.wait_ge(s, n)

        def by_two(eng, step, n, peel):
            for t in range(peel):
                step(t, t % 2)
            with eng.Fori(peel // 2, n // 2, 1) as pair:
                for p in range(2):
                    step(2 * pair + p, p)

        def by_tiles(eng, m, step, tail):
            eng.wait_ge(N[m]["tab"], 1)
            more = eng.value_load(cnt_i[0:1, NE:NE + 1], min_val=0, max_val=TOK * TOPK[m] // P)
            bodies = (more + (BODY - 1)) // BODY + NE // BODY
            for v in range(4):
                step(v, v % 2)
            with eng.Fori(2, bodies, 1) as q:
                for p in range(2):
                    step(2 * q + p, p)
            for n in range(tail):
                step(2 * bodies + n, n % 2, last=n + 1)
            return bodies

        def half(v):
            return v // 2 + 1

        def early(v, n):
            return isinstance(v, int) and v < n

        @block.sync
        def _(sp):
            def load_experts(m, src):
                n, width = NE // 4, src.shape[2]
                for e in range(0, NE, n):
                    if m == 0 and e == NE - n:
                        sp.wait_ge(A["tp"], NT)
                    sp.dma_start(wts[:, e * width:(e + n) * width],
                                 src[:, e:e + n, :].rearrange("p e n -> p (e n)")).then_inc(s_w[m], 16)

            def experts(m):
                s = M[m]
                sp.wait_ge(N[m]["tab"], 1)
                for n in range(BODY - 1):
                    at = NE * ROWS + n * P
                    sp.dma_start(sent[at:at + P, :], pad_row[:, :]).then_inc(s["fill"], 16)
                with sp.Fori(0, NE, 1) as e:
                    n_e = sp.value_load(cnt_i[0:1, ds(e, 1)], min_val=0, max_val=TOK)
                    sp.dma_start(sent[ds(e * ROWS + n_e, P), :], pad_row[:, :]).then_inc(s["fill"], 16)
                if m == 0:
                    sp.wait_ge(N[m]["bdx"], NT // 2)
                sp.dma_start(acc[0][0:TOK, :].rearrange("(p t) d -> p (t d)", t=NT), X[:, :]).then_inc(s["init"], 16)
                sp.dma_start(acc[1][0:TOK, :].rearrange("(p t) d -> p t d", t=NT),
                             no_row.unsqueeze(1).to_broadcast([P, NT, D])).then_inc(s["init"], 16)
                for r in range(2):
                    sp.dma_start(acc[r][TOK:TOK + P, :], no_row).then_inc(s["init"], 16)
                sp.wait_ge(s["fill"], 16 * (NE + BODY - 1))
                sp.wait_ge(s["init"], 64)
                ranks = sp.value_load(cnt_i[0:1, NE + 1:NE + 2], min_val=1, max_val=TOPK[m])
                def load(v, p):
                    at = [sp.value_load(tab_i[0:1, ds(2 * v + (SMAX + t), 1)], min_val=0, max_val=REG * ROWS - P)
                          for t in range(2)]
                    if early(v, 1):
                        sp.wait_ge(s["dsp"], ranks * (16 * NT))
                    wait(sp, s["tx"], v - 1)
                    wait(sp, s["tail"], v - 1)
                    for t in range(2):
                        sp.dma_start(xt[:, p, t, :], sent[ds(at[t], P), :]).then_inc(s[f"ld{p}"], 16)
                bodies = by_tiles(sp, m, load, 0)
                for r in range(2):
                    sp.wait_ge(s[f"sc{r}"], bodies * 32)
                n = TPC * D
                for c in range(NCH):
                    at = slice(c * n, (c + 1) * n)
                    for r, dst in enumerate((X, acc1)):
                        sp.dma_start(dst[:, at], acc[r][0:TOK, :].rearrange("(p t) d -> p (t d)", t=NT)[:, at])\
                            .then_inc(s[f"rd{c}"], 16)

            sp.dma_start(X[:, :], x_rows.rearrange("p t d -> p (t d)")).then_inc(s_x, 16)
            sp.dma_start(toep_all[:, :, :],
                         bass.AP(tensor=filt.tensor, offset=1, ap=[[1, P], [P + D, NT], [1, D]])).then_inc(s_toep, 16)
            sp.dma_start(skc[:, :], skip_cols).then_inc(s_par, 16)
            sp.dma_start(gate_in[:, :], gates.partition_broadcast(P)).then_inc(s_par, 16)
            sp.dma_start(cols[:, :, :, :], ctx_cols).then_inc(s_cols, 16)
            sp.dma_start(rows[:, :], ctx_rows.rearrange("p t d -> p (t d)")).then_inc(s_ctx, 16)
            sp.dma_start(mask_u8[:, :], mask).then_inc(s_par2, 16)
            sp.dma_start(rt[0][:, :], router0).then_inc(s_par2, 16)
            sp.dma_start(rt[1][:, :], router1).then_inc(s_par2, 16)
            sp.dma_start(rt_bias[:, :], router0_bias).then_inc(s_par2, 16)
            for n in range(2):
                sp.dma_start(in_b[n * NE:(n + 1) * NE, :], in_bias0).then_inc(s_par2, 16)
            sp.dma_start(down_b[:, :], down_bias0).then_inc(s_par2, 16)
            load_experts(0, experts0)
            experts(0)
            load_experts(1, experts1)

            def load_mem(b, p):
                wait(sp, C["ro"], b - 1)
                sp.dma_start(mem_b[:, p, :], ctx_batch[ds(b, 1), :, :].rearrange("a s d -> s (a d)"))\
                    .then_inc(s_mem[p], 16)
            by_two(sp, load_mem, NB, 2)
            experts(1)
            for c in range(NCH):
                sp.wait_ge(M[1]["x"], c + 1)
                n = TPC * D
                sp.dma_start(out.rearrange("p t d -> p (t d)")[:, c * n:(c + 1) * n], X[:, c * n:(c + 1) * n])\
                    .then_inc(s_out, 16)
            sp.wait_ge(s_out, 16 * NCH)

        @block.gpsimd
        def _(pool):
            g = nc.gpsimd
            g.memset(ident[:, :], 0.0).then_inc(s_zeroed, 1)
            g.memset(same_b[:, :], 1.0).then_inc(s_zeroed, 1)
            g.memset(flip[:, :], 0.0).then_inc(s_zeroed, 1)
            g.memset(before[:, :], 1.0).then_inc(s_zeroed, 1)
            g.memset(eye2[:, :], 0.0).then_inc(s_zeroed, 1)
            g.memset(pad_row[:, :], 0.0).then_inc(s_zeroed, 1)
            g.memset(ones[:, :], 1.0).then_inc(s_const, 1)
            g.memset(cum[:, :, :], 0.0).then_inc(s_const, 1)
            g.iota(steps_i[:, :], pattern=[[P, NT - 1]], base=P, channel_multiplier=0).then_inc(s_const, 1)
            g.iota(tile_i[:, :], pattern=[[P, 2]], base=0, channel_multiplier=1).then_inc(s_const, 1)
            g.iota(iota_i[:, :], pattern=[[1, NE]], base=0, channel_multiplier=0).then_inc(s_const, 1)
            pool.wait_ge(s_zeroed, 6)
            g.iota(pad_row[:, D:D + 1].bitcast(i32), pattern=[[0, 1]], base=TOK, channel_multiplier=1)\
                .then_inc(s_const, 1)
            g.affine_select(out=before[:, :], in_=before[:, :], compare_op=ALU.is_gt, fill=0.0, base=0,
                            pattern=[[1, P]], channel_multiplier=-1).then_inc(s_const, 1)
            g.affine_select(out=eye2[:, :], in_=eye2[:, :], compare_op=ALU.not_equal, fill=1.0, base=0,
                            pattern=[[-1, NE]], channel_multiplier=1).then_inc(s_zeroed, 1)
            pool.wait_ge(s_zeroed, 7)
            g.affine_select(out=eye2[:, :], in_=eye2[:, :], compare_op=ALU.not_equal, fill=1.0, base=-NE,
                            pattern=[[-1, NE]], channel_multiplier=1).then_inc(s_const, 1)
            g.affine_select(out=flip[:, :], in_=flip[:, :], compare_op=ALU.not_equal, fill=1.0, base=1 - P,
                            pattern=[[1, P]], channel_multiplier=1).then_inc(s_const, 1)
            g.affine_select(out=ident[:, :], in_=ident[:, :], compare_op=ALU.not_equal, fill=1.0, base=0,
                            pattern=[[-1, P]], channel_multiplier=1).then_inc(s_const, 1)
            blocks = same_b[:, :].rearrange("p (b j) -> p b j", j=G)
            g.affine_select(out=blocks, in_=blocks, compare_op=ALU.is_ge, fill=0.0, base=0,
                            pattern=[[-G, NB], [0, G]], channel_multiplier=1).then_inc(s_zeroed, 1)
            pool.wait_ge(s_zeroed, 8)
            g.affine_select(out=blocks, in_=blocks, compare_op=ALU.is_ge, fill=0.0, base=G - 1,
                            pattern=[[G, NB], [0, G]], channel_multiplier=-1).then_inc(s_const, 1)

            def kv_high(h, p):
                wait(pool, A["vt"], h + 1)
                wait(pool, A["y"], 4 * h - 4)
                g.tensor_tensor(
                    kv[:, p, 1, :].rearrange("p (b i j) -> p b i j", b=NB, i=G),
                    vT[:, p, 1, :].rearrange("p (b i) -> p b i", i=G).unsqueeze(3).to_broadcast([P, NB, G, G]),
                    cols[:, 1, ds(h, 1), :].rearrange("p a (b j) -> p (a b) j", j=G).unsqueeze(2).to_broadcast([P, NB, G, G]),
                    ALU.mult).then_inc(A["kv1"], 1)

            def add_mixed(h, p):
                pool.wait_ge(A["mixed"], h + 1)
                xt = X[:, ds(h * D, D)]
                g.tensor_tensor(xt, xt, mixed[:, p, :], ALU.add).then_inc(A["x"], 1)

            def stage_a(h, p):
                kv_high(h, p)
                if not (isinstance(h, int) and h < 2):
                    add_mixed(h - 2, p)
            pool.wait_ge(s_cols, 16)
            by_two(pool, stage_a, NT, 2)
            for h in range(NT - 2, NT):
                add_mixed(h, h % 2)

            def prepare(m):
                s = N[m]

                def keep_rows(t, p):
                    pool.wait_ge(s["xn"], t + 1)
                    g.tensor_copy(send[:, ds(t, 1), 0:D].rearrange("p a n -> p (a n)"), xn[:, p, :])\
                        .then_inc(s["cp"], 1)
                if m == 1:
                    ranks = TOPK[0]
                    pool.wait_ge(M[0]["dsp"], 16 * NT * ranks)
                pool.wait_ge(s["xn"], 1)
                g.iota(send[:, :, D].bitcast(i32), pattern=[[1, NT]], base=0, channel_multiplier=NT).then_inc(s_tok, 1)
                by_two(pool, keep_rows, NT, 2)

            def dispatch(m):
                s = M[m]
                pool.wait_ge(N[m]["tab"], 1)
                pool.wait_ge(s_tok, m + 1)
                pool.wait_ge(N[m]["cp"], NT)
                ranks = pool.value_load(cnt_i[0:1, NE + 1:NE + 2], min_val=1, max_val=TOPK[m])

                def rank(k):
                    if not isinstance(k, int):
                        pool.wait_ge(s["dsp"], k * (16 * NT))
                    g.tensor_copy(send[:, :, D + 1:D + 2], tw[:, :, ds(k, 1)]).then_inc(N[m]["now"], 1)
                    g.tensor_copy(idx_now[:, :].unsqueeze(2), pos_i[:, :, ds(k, 1)]).then_inc(N[m]["now"], 1)
                    pool.wait_ge(N[m]["now"], 2 * k + 2)
                    g.tensor_tensor(idle[:, :], ones[0:1, 0:1], ones[0:1, 0:1], ALU.mult)
                    for t in range(NT):
                        g.indirect_dma_start(out=sent, out_offset=bass.IndirectOffsetOnAxis(ap=idx_now[:, t:t + 1], axis=0),
                                             in_=send[:, t, :], in_offset=None, bounds_check=REG * ROWS - 1,
                                             oob_is_err=False).then_inc(s["dsp"], 16)
                rank(0)
                if m == 0:
                    with pool.Fori(1, TOPK[0], 1) as k:
                        rank(k)
                else:
                    with pool.Fori(1, ranks, 1) as k:
                        rank(k)

            def experts(m):
                s = M[m]
                dispatch(m)

                def keep_tails(v, p):
                    pool.wait_ge(s[f"ld{p}"], half(v) * 32)
                    g.tensor_copy(tails[:, ds(2 * v, 2), :], xt[:, p, :, D:D + 2]).then_inc(s["tail"], 1)

                def select(v, p):
                    e = [pool.value_load(tab_i[0:1, ds(2 * v + t, 1)], min_val=0, max_val=NE - 1) for t in range(2)]
                    wait(pool, s["gu"], v - 1)
                    for t in range(2):
                        last = g.tensor_copy(sel[:, p, t, :], eye2[:, ds(e[t], 1)].to_broadcast([2 * NE, P]))
                    last.then_inc(s["sel"], 1)

                def add_rows(v, p):
                    for t in range(2):
                        wait(pool, s[f"sc{t}"], 16 * v)
                    g.tensor_copy(idx_y[:, p, :].unsqueeze(2), tails[:, ds(2 * v, 2), 0:1].bitcast(i32))\
                        .then_inc(s["ix"], 1)
                    pool.wait_ge(s["ix"], v + 1)
                    pool.wait_ge(s["y"], v + 1)
                    g.tensor_tensor(idle[:, :], ones[0:1, 0:1], ones[0:1, 0:1], ALU.mult)
                    for t in range(2):
                        g.indirect_dma_start(out=acc[t], out_offset=bass.IndirectOffsetOnAxis(ap=idx_y[:, p, t:t + 1], axis=0),
                                             in_=y[:, p, t, :], in_offset=None, compute_op=ALU.add).then_inc(s[f"sc{t}"], 16)

                def step(v, p, last=0):
                    if not last:
                        keep_tails(v, p)
                        if m == 0:
                            select(v, p)
                    if not early(v, 3):
                        add_rows(v - 3, 1 - p)
                pool.wait_ge(s["init"], 64)
                by_tiles(pool, m, step, 3)

            prepare(0)
            experts(0)

            def stage_batch(b, p):
                wait(pool, C["s"], b - 1)
                g.tensor_copy(xs_b[:, p, :, :], xT_b[:, :, ds(b, 1), :].rearrange("p k a s -> p k (a s)"))\
                    .then_inc(C["xs"], 1)
            pool.wait_ge(C["xt"], NT)
            by_two(pool, stage_batch, NB, 2)

            prepare(1)
            experts(1)

        @block.scalar
        def _(act):
            a = nc.scalar
            act.wait_ge(s_par, 32)
            a.activation(tg[:, :], gate_in[:, :], ACT.Tanh).then_inc(s_tanh, 1)

            def std_of(s):
                act.wait_ge(s["var"], 1)
                a.activation(std[:, :], var_e[:, :], ACT.Sqrt).then_inc(s["sd"], 1)

            for n in range(NT // 2):
                act.wait_ge(A["flip"], n + 1)
                a.activation(toep_all[:, 2 * n:2 * n + 2, :], bank[n % 4][:, :].rearrange("p (a n) -> p a n", a=2),
                             ACT.Copy).then_inc(A["turned"], 1)
            act.wait_ge(A["turned"], NT // 2)
            std_of(A)
            act.wait_ge(s_bias, 1)
            a.activation(in_bp[:, :], in_b[:, :], ACT.Copy).then_inc(s_bias, 1)

            def v_copy(h, p):
                act.wait_ge(A["tr"], h + 1)
                wait(act, A["kv0"], h - 1)
                wait(act, A["kv1"], h - 1)
                a.activation(vT[:, p, :, :], bank[4 + p][:, 0:D].rearrange("p (k n) -> p k n", k=KB), ACT.Copy)\
                    .then_inc(A["vt"], 1)
            def filter_copy(h, p):
                wait(act, A["y"], 4 * h - 4)
                a.activation(toep[:, p, :], toep_all[:, ds(h, 1), :].rearrange("p a n -> p (a n)"), ACT.Copy)\
                    .then_inc(A["tp"], 1)

            def stage_a(h, p):
                filter_copy(h, p)
                v_copy(h, p)
            by_two(act, stage_a, NT, 2)

            def prepare(m):
                s = N[m]
                std_of(s)

                def x_copy(t, p):
                    act.wait_ge(s["tr"], t + 1)
                    a.activation(xT_all[:, :, ds(t * P, P)], bank[4 + p][:, 0:D].rearrange("p (k n) -> p k n", k=KB),
                                 ACT.Copy).then_inc(s["xt"], 1)
                by_two(act, x_copy, NT, 2)
                for c in range(NCH):
                    act.wait_ge(s["lt"], c + 1)
                    dst, src = lgT[:, c * CH:(c + 1) * CH], bank[c][0:NE, :]
                    if m == 0:
                        a.activation(dst, src, ACT.Identity, bias=rt_bias[:, 0:1]).then_inc(s["lg"], 1)
                    else:
                        a.activation(dst, src, ACT.Copy).then_inc(s["lg"], 1)
                act.wait_ge(s["e0"], 1)
                if m == 0:
                    a.activation(tw[:, :, 0:4], tw[:, :, 0:4], ACT.Exp).then_inc(s["e1"], 1)
                    for c in range(NCH):
                        act.wait_ge(s["cwp"], c + 1)
                        a.activation(lgT[:, c * CH:(c + 1) * CH], bank[c][0:NE, :], ACT.Copy).then_inc(s["cwt"], 1)
                else:
                    a.activation(lg2, lg2, ACT.Exp).then_inc(s["e1"], 1)

            def experts(m):
                s, I = M[m], INNER[m]

                def x_turned(v, p):
                    act.wait_ge(s["tx"], v + 1)
                    wait(act, s["gu"], v - 1)
                    a.activation(xT[:, p, :], bank[p][:, :], ACT.Copy).then_inc(s["xt"], 1)

                def sigmoid(v, p):
                    wait(act, s["h"], v - 1)
                    if m == 0:
                        act.wait_ge(s["gmin"], v + 1)
                        a.activation(sig[:, p, :, :], gmin[:, p, :, :], ACT.Sigmoid, scale=ALPHA).then_inc(s["sig"], 1)
                    else:
                        act.wait_ge(s["gu"], v + 1)
                        gu = bank[2 + p][:, :].rearrange("p (t n) -> p t n", t=2)
                        a.activation(sig[:, p, :, 0:I], gu[:, :, 0:I], ACT.Silu).then_inc(s["sig"], 1)

                def h_turned(v, p):
                    act.wait_ge(s["ht"], v + 1)
                    wait(act, s["dn"], v - 1)
                    a.activation(hT[0:I, p, :, :], bank[4 + p][0:I, 0:2 * P].rearrange("p (t n) -> p t n", t=2),
                                 ACT.Copy).then_inc(s["htc"], 1)

                def step(v, p, last=0):
                    if last == 0:
                        x_turned(v, p)
                    if not early(v, 1) and last < 2:
                        sigmoid(v - 1, 1 - p)
                    if not early(v, 2):
                        h_turned(v - 2, p)
                by_tiles(act, m, step, 2)

            prepare(0)
            experts(0)

            std_of(C)

            def x_cols(t, p):
                act.wait_ge(C["tr"], t + 1)
                a.activation(xT_b[:, :, :, ds(t * G, G)],
                             bank[4 + p][:, 0:D].rearrange("p (k b i) -> p k b i", k=KB, b=NB), ACT.Copy)\
                    .then_inc(C["xt"], 1)
            by_two(act, x_cols, NT, 2)

            def exps(b, p):
                act.wait_ge(C["nb"], b + 1)
                wait(act, C["a"], b - 1)
                a.activation(prob[:, p, :], bank[p][:, 0:P], ACT.Exp, bias=nbias[:, ds(b, 1)], scale=SCALE,
                             accum_out=psum_row[:, ds(b, 1)]).then_inc(C["e"], 1)

            def attn_copy(b, p):
                act.wait_ge(C["at"], b + 1)
                wait(act, C["ro"], b - 1)
                a.activation(attnT[:, p, :], bank[2 + p][:, 0:P], ACT.Copy).then_inc(C["atc"], 1)

            def attend(v, p):
                exps(v, p)
                if not (isinstance(v, int) and v < 1):
                    attn_copy(v - 1, 1 - p)
            by_two(act, attend, NB, 4)
            attn_copy(NB - 1, (NB - 1) % 2)

            prepare(1)
            experts(1)

        @block.tensor
        def _(pe):
            t_ = nc.tensor

            def transposes(s, free, t, p, n_free):
                pe.wait_ge(s["xn"], t + 1)
                wait(pe, free, n_free)
                for k in range(KB):
                    mm = t_.transpose(bank[4 + p][:, k * P:(k + 1) * P], xn[:, p, k * P:(k + 1) * P], ident[:, :])
                mm.then_inc(s["tr"], 1)

            pe.wait_ge(s_const, 11)
            pe.wait_ge(s_toep, 16)
            for n in range(NT // 2):
                wait(pe, A["turned"], n - 3)
                t_.matmul(bank[n % 4][:, :], flip[:, :], toep_all[:, 2 * n:2 * n + 2, :], start=True, stop=True)\
                    .then_inc(A["flip"], 1)
            pe.wait_ge(s_valid, 1)
            t_.matmul(bank[7][:, 0:NB], ones[0:1, :], valid[:, :], start=True, stop=True).then_inc(s_vb, 1)

            def conv(h, p):
                pe.wait_ge(A["tp"], h + 1)
                for n in range(4):
                    lh, half = n // 2, n % 2
                    if n == 0:
                        pe.wait_ge(A["kv0"], h + 1)
                    if n == 2:
                        pe.wait_ge(A["kv1"], h + 1)
                    wait(pe, A["z"], 4 * h - 3 + n)
                    for k in range(lh + 1):
                        mm = t_.matmul(bank[n][:, :], toep[:, p, (lh - k) * P:(lh - k + 1) * P],
                                       kv[:, p, k, half * 512:(half + 1) * 512], start=(k == 0), stop=(k == lh))
                    mm.then_inc(A["y"], 1)

            def gather_i(h, p):
                pe.wait_ge(A["f2"], 2 * h + 2)
                wait(pe, A["mixed"], h)
                for lh in range(KB):
                    for i in range(2):
                        t_.matmul(bank[6][:, lh * P:(lh + 1) * P],
                                  fold2[:, lh, i * P:(i + 1) * P],
                                  ident[:, :], start=(i == 0), stop=(i == 1))
                pe.wait_ge(A["skv"], h + 1)
                t_.matmul(bank[7][:, 0:D], same_b[:, :], skipv[:, p, :], start=True, stop=True).then_inc(A["out"], 1)

            sA = {"xn": A["vn"], "tr": A["tr"]}

            def stage_a(h, p):
                if not (isinstance(h, int) and h > NT - 3):
                    transposes(sA, A["vt"], h + 2, p, h + 1)
                if not (isinstance(h, int) and h > NT - 2):
                    conv(h + 1, 1 - p)
                gather_i(h, p)

            for t in range(2):
                transposes(sA, A["vt"], t, t, t - 1)
            conv(0, 0)
            pe.wait_ge(s_vb, 1)
            pe.wait_ge(s_tanh, 1)
            for h in range(2):
                stage_a(h, h)
            with pe.Fori(1, NT // 2 - 1, 1) as pair:
                for p in range(2):
                    stage_a(2 * pair + p, p)
            for h in range(NT - 2, NT):
                stage_a(h, h % 2)

            def prepare(m):
                s = N[m]
                by_two(pe, lambda t, p: transposes(s, s["xt"], t, p, t - 1), NT, 2)
                pe.wait_ge(s["xt"], NT)
                for c in range(NCH):
                    for k in range(KB):
                        mm = t_.matmul(bank[c][0:NE, :], rt[m][:, k * NE:(k + 1) * NE], xT_all[:, k, c * CH:(c + 1) * CH],
                                       start=(k == 0), stop=(k == KB - 1))
                    mm.then_inc(s["lt"], 1)
                pe.wait_ge(s["lg"], NCH)
                for t in range(NT):
                    mm = t_.matmul(bank[4][:, t * NE:(t + 1) * NE], lgT[:, t * P:(t + 1) * P], ident[0:NE, 0:NE],
                                   start=True, stop=True)
                mm.then_inc(s["l"], 1)
                pe.wait_ge(s["mk"], 1)
                t_.matmul(bank[6][:, :], before[:, :], mask_e[:, :], start=True, stop=True).then_inc(s["rk"], 1)
                t_.matmul(bank[7][:, :], ones[:, :], mask_e[:, :], start=True, stop=True).then_inc(s["rk"], 1)
                if m == 1:
                    t_.matmul(bank[5][:, 0:NT * 8], ones[:, :], act_k[:, :, :].rearrange("p t k -> p (t k)"),
                              start=True, stop=True).then_inc(s["rk"], 1)
                pe.wait_ge(s["tb"], 1)
                for n in range(4):
                    mm = t_.matmul(bank[4][0:1, n * P:(n + 1) * P], tab[:, n:n + 1], ident[:, :], start=True, stop=True)
                mm.then_inc(s["tp"], 1)
                if m == 0:
                    pe.wait_ge(s["cw"], 1)
                    for t in range(NT):
                        c, n = divmod(t, TPC)
                        mm = t_.matmul(bank[c][0:NE, n * P:(n + 1) * P], cw[:, t * NE:(t + 1) * NE], ident[:, :],
                                       start=True, stop=True)
                        if n == TPC - 1:
                            mm.then_inc(s["cwp"], 1)
                    pe.wait_ge(s["cwt"], NCH)
                    pe.wait_ge(s["tab"], 1)
                    for n in range(NT // 2):
                        wait(pe, s["bdx"], n - 1)
                        for t in range(2):
                            at = (2 * n + t) * P
                            mm = t_.matmul(bank[4 + n % 2][:, t * D:(t + 1) * D], lgT[:, at:at + P], down_b[:, :],
                                           start=True, stop=True)
                        mm.then_inc(s["bd"], 1)
                    pe.wait_ge(s["bdx"], NT // 2)

            def experts(m):
                s, I = M[m], INNER[m]
                width = 4 * I + D
                pe.wait_ge(s_w[m], 16 * (NE // 8))
                if m == 0:
                    pe.wait_ge(s_bias, 3)

                def expert(v, t):
                    return pe.value_load(tab_i[0:1, ds(2 * v + t, 1)], min_val=0, max_val=NE - 1) * width

                def x_turn(v, p):
                    pe.wait_ge(s[f"ld{p}"], half(v) * 32)
                    wait(pe, s["xt"], v - 1)
                    for t in range(2):
                        for k in range(KB):
                            mm = t_.transpose(bank[p][:, (t * KB + k) * P:(t * KB + k + 1) * P],
                                              xt[:, p, t, k * P:(k + 1) * P], ident[:, :])
                    mm.then_inc(s["tx"], 1)

                def gate_up(v, p):
                    e = [expert(v, t) for t in range(2)]
                    pe.wait_ge(s["xt"], v + 1)
                    if m == 0:
                        pe.wait_ge(s["sel"], v + 1)
                        wait(pe, s["gmin"], v - 1)
                        wait(pe, s["umin"], v - 1)
                    else:
                        wait(pe, s["sig"], v - 1)
                        wait(pe, s["h"], v - 1)
                    for t in range(2):
                        dst = bank[2 + p][:, t * 2 * P:t * 2 * P + 2 * I]
                        if m == 0:
                            t_.matmul(dst, sel[:, p, t, :], in_bp[:, :], start=True, stop=False)
                        for k in range(KB):
                            mm = t_.matmul(dst, xT[:, p, (t * KB + k) * P:(t * KB + k + 1) * P],
                                           wts[:, ds(e[t] + k * 2 * I, 2 * I)], start=(m == 1 and k == 0), stop=(k == KB - 1))
                    mm.then_inc(s["gu"], 1)

                def h_turn(v, p):
                    pe.wait_ge(s["h"], v + 1)
                    wait(pe, s["htc"], v - 1)
                    for t in range(2):
                        mm = t_.transpose(bank[4 + p][0:I, t * P:(t + 1) * P], hid[:, p, t, 0:I], ident[:, :])
                    mm.then_inc(s["ht"], 1)

                def down(v, p):
                    e = [expert(v, t) for t in range(2)]
                    pe.wait_ge(s["htc"], v + 1)
                    wait(pe, s["y"], v - 1)
                    for t in range(2):
                        mm = t_.matmul(bank[6 + p][:, t * D:(t + 1) * D], hT[0:I, p, t, :],
                                       wts[0:I, ds(e[t] + 4 * I, D)], start=True, stop=True)
                    mm.then_inc(s["dn"], 1)

                def step(v, p, last=0):
                    if last == 0:
                        x_turn(v, p)
                    if not early(v, 1) and last < 2:
                        gate_up(v - 1, 1 - p)
                    if not early(v, 2) and last < 3:
                        h_turn(v - 2, p)
                    if not early(v, 3):
                        down(v - 3, 1 - p)
                by_tiles(pe, m, step, 3)

            prepare(0)
            experts(0)

            by_two(pe, lambda t, p: transposes(C, C["xt"], t, p, t - 1), NT, 2)

            def scores(b, p):
                pe.wait_ge(C["xs"], b + 1)
                pe.wait_ge(C["mr"], b + 1)
                wait(pe, C["e"], b - 1)
                dst = bank[p][:, 0:P]
                t_.matmul(dst, ones[0:1, :], mrow[:, p, :], start=True, stop=False)
                for k in range(KB):
                    mm = t_.matmul(dst, xs_b[:, p, k, :], cols[:, k, :, ds(b * G, G)], start=False, stop=(k == KB - 1))
                mm.then_inc(C["s"], 1)

            def attn_turn(b, p):
                pe.wait_ge(C["a"], b + 1)
                wait(pe, C["atc"], b - 1)
                t_.transpose(bank[2 + p][:, 0:P], attn[:, p, :], ident[:, :]).then_inc(C["at"], 1)

            def readout(b, p, count):
                pe.wait_ge(C["atc"], b + 1)
                pe.wait_ge(s_mem[p], 16 * count)
                wait(pe, C["rot"], b - 1)
                for k in range(KB):
                    mm = t_.matmul(bank[4 + p][:, k * P:(k + 1) * P], mem_b[:, p, k * P:(k + 1) * P], attnT[:, p, :],
                                   start=True, stop=True)
                mm.then_inc(C["ro"], 1)

            def attend(v, p, count):
                scores(v, p)
                if not (isinstance(v, int) and v < 1):
                    attn_turn(v - 1, 1 - p)
                if not (isinstance(v, int) and v < 2):
                    readout(v - 2, p, count)
            for v in range(4):
                attend(v, v % 2, v // 2)
            with pe.Fori(2, NB // 2, 1) as vp:
                for p in range(2):
                    attend(2 * vp + p, p, vp)
            attn_turn(NB - 1, 1)
            readout(NB - 2, 0, NB // 2)
            readout(NB - 1, 1, NB // 2)
            pe.wait_ge(C["rot"], NB)
            for n in range(NT // 2):
                wait(pe, C["x"], n - 1)
                for t in range(2):
                    for k in range(KB):
                        mm = t_.transpose(bank[6 + n % 2][:, (t * KB + k) * P:(t * KB + k + 1) * P],
                                          roT[:, k, 2 * n + t, :], ident[:, :])
                mm.then_inc(C["fx"], 1)

            prepare(1)
            experts(1)

        @block.vector
        def _(dve):
            v = nc.vector
            chain = [0]

            def link(ins):
                chain[0] += 1
                ins.then_inc(s_chain, 1)
                dve.wait_ge(s_chain, chain[0])

            def token_stats(s):
                for t in range(NT):
                    last = v.bn_stats(stats[:, t, :], X[:, t * D:(t + 1) * D])
                link(last)
                for t in range(NT):
                    last = v.bn_aggr(mv[:, 2 * t:2 * t + 2], stats[:, t, :])
                link(last)
                v.tensor_scalar(var_e[:, :], mv[:, 1:2 * NT:2], EPS, None, ALU.add).then_inc(s["var"], 1)
                dve.wait_ge(s["sd"], 1)
                link(v.reciprocal(rstd[:, :], std[:, :]))
                link(v.tensor_tensor(newt[:, :], rstd[:, :], rstd[:, :], ALU.mult))
                link(v.tensor_tensor(newt[:, :], newt[:, :], var_e[:, :], ALU.mult))
                link(v.tensor_scalar(newt[:, :], newt[:, :], -0.5, 1.5, ALU.mult, ALU.add))
                link(v.tensor_tensor(rstd[:, :], rstd[:, :], newt[:, :], ALU.mult))

            def normalise(s, t, p, free, n_free):
                wait(dve, free, n_free)
                v.tensor_scalar(xn[:, p, :], X[:, ds(t * D, D)], mv[:, ds(2 * t, 1)], rstd[:, ds(t, 1)],
                                ALU.subtract, ALU.mult).then_inc(s["xn"], 1)

            dve.wait_ge(s_x, 16)
            token_stats(A)
            dve.wait_ge(s_const, 11)
            v.tensor_copy(iota_f[:, :], iota_i[:, :])
            dve.wait_ge(s_par2, 16 * 7)
            v.tensor_copy(steps_f[:, :], steps_i[:, :])
            v.tensor_scalar(region_f[:, :], iota_i[:, :], float(ROWS), None, ALU.mult)
            v.tensor_copy(tile_f[:, :], tile_i[:, :])
            v.tensor_reduce(valid[:, :], mask_u8[:, :].rearrange("a (b s) -> a b s", b=NB), AX.X, ALU.max)\
                .then_inc(s_valid, 1)
            v.tensor_scalar(in_b[:, P:2 * P], in_b[:, P:2 * P], 1.0, None, ALU.add).then_inc(s_bias, 1)
            dve.wait_ge(s_bias, 2)
            v.tensor_tensor(in_bp[NE:2 * NE, :], in_b[NE:2 * NE, :], in_bp[NE:2 * NE, :].bitcast(fp32), ALU.subtract)\
                .then_inc(s_bias, 1)
            dve.wait_ge(s_vb, 1)
            dve.wait_ge(s_tanh, 1)
            link(v.tensor_scalar(valid_t[:, :], bank[7][:, 0:NB], tg[:, 1:2], None, ALU.mult))

            sA = {"xn": A["vn"]}

            def v_rows(h, p):
                wait(dve, A["skv"], h - 1)
                normalise(sA, h, p, A["tr"], h - 1)

            def skip_rows(h, p):
                dve.wait_ge(A["vn"], h + 1)
                wait(dve, A["out"], h - 1)
                v.scalar_tensor_tensor(out=skipv[:, p, :], in0=xn[:, p, :], scalar=skc[:, ds(h, 1)],
                                       in1=rows[:, ds(h * D, D)], op0=ALU.mult, op1=ALU.mult)\
                    .then_inc(A["skv"], 1)

            def kv_low(h, p):
                dve.wait_ge(A["vt"], h + 1)
                wait(dve, A["y"], 4 * h - 4)
                v.tensor_tensor(
                    kv[:, p, 0, :].rearrange("p (b i j) -> p b i j", b=NB, i=G),
                    vT[:, p, 0, :].rearrange("p (b i) -> p b i", i=G).unsqueeze(3).to_broadcast([P, NB, G, G]),
                    cols[:, 0, ds(h, 1), :].rearrange("p a (b j) -> p (a b) j", j=G).unsqueeze(2).to_broadcast([P, NB, G, G]),
                    ALU.mult).then_inc(A["kv0"], 1)

            def mix_out(h, p):
                dve.wait_ge(A["out"], h + 1)
                wait(dve, A["x"], h - 1)
                v.scalar_tensor_tensor(out=mixed[:, p, :], in0=bank[7][:, 0:D], scalar=tg[:, 0:1],
                                       in1=rows[:, ds(h * D, D)], op0=ALU.mult, op1=ALU.mult).then_inc(A["mix"], 1)
                dve.wait_ge(A["mix"], h + 1)
                v.scalar_tensor_tensor(out=mixed[:, p, :], in0=bank[6][:, 0:D], scalar=tg[:, 0:1],
                                       in1=mixed[:, p, :], op0=ALU.mult, op1=ALU.add).then_inc(A["mixed"], 1)

            def times_x1(h, p):
                for n in range(4):
                    lh, half = n // 2, n % 2
                    dve.wait_ge(A["y"], 4 * h + n + 1)
                    wait(dve, A["f1"], 2 * h - 1 + lh)
                    v.tensor_tensor(
                        prod[:, lh, half * 512:(half + 1) * 512].rearrange("p (n j) -> p n j", j=G),
                        bank[n][:, :].rearrange("p (n j) -> p n j", j=G),
                        cols[:, lh, ds(h, 1), half * 64:(half + 1) * 64].rearrange("p a n -> p (a n)").unsqueeze(2)
                        .to_broadcast([P, 64, G]),
                        ALU.mult).then_inc(A["z"], 1)
                    if half:
                        dve.wait_ge(A["z"], 4 * h + n + 1)
                        wait(dve, A["f2"], 2 * h - 1 + lh)
                        z = prod[:, lh, :].rearrange("p (b i n) -> p b i n", b=NB, i=2)
                        v.tensor_tensor(fold1[:, lh, :].rearrange("p (b n) -> p b n", b=NB), z[:, :, 0, :],
                                        z[:, :, 1, :], ALU.add).then_inc(A["f1"], 1)
                for lh in range(KB):
                    dve.wait_ge(A["f1"], 2 * h + lh + 1)
                    wait(dve, A["out"], h)
                    z = fold1[:, lh, :].rearrange("p (b a i j) -> p a i b j", b=NB, a=2, i=2)
                    v.tensor_tensor(fold2[:, lh, :].rearrange("p (i b j) -> p i b j", i=2, b=NB), z[:, 0, :, :, :],
                                    z[:, 1, :, :, :], ALU.add).then_inc(A["f2"], 1)

            def stage_a(h, p):
                static = isinstance(h, int)
                if not (static and h > NT - 3):
                    v_rows(h + 2, p)
                if not (static and h > NT - 2):
                    kv_low(h + 1, 1 - p)
                if not (static and h < 1):
                    mix_out(h - 1, 1 - p)
                if not (static and h > NT - 2):
                    skip_rows(h + 1, 1 - p)
                times_x1(h, p)

            dve.wait_ge(s_par, 32)
            dve.wait_ge(s_ctx, 16)
            for h in range(2):
                v_rows(h, h)
            skip_rows(0, 0)
            dve.wait_ge(s_cols, 16)
            kv_low(0, 0)
            for h in range(2):
                stage_a(h, h)
            with dve.Fori(1, NT // 2 - 1, 1) as pair:
                for p in range(2):
                    stage_a(2 * pair + p, p)
            for h in range(NT - 2, NT):
                stage_a(h, h % 2)
            mix_out(NT - 1, 1)
            dve.wait_ge(A["x"], NT)

            def over_k(a, k):
                return a.unsqueeze(2).to_broadcast([P, NT, k])

            def prepare(m):
                s, K = N[m], TOPK[m]
                token_stats(s)

                def rows_out(t, p):
                    wait(dve, s["cp"], t - 1)
                    normalise(s, t, p, s["tr"], t - 1)
                by_two(dve, rows_out, NT, 2)

                dve.wait_ge(s["l"], 1)
                link(v.tensor_copy(lg2, bank[4][:, :]))
                if m == 1:
                    link(v.tensor_reduce(row1[:, :], lg[:, :, :], AX.X, ALU.max))
                    v.tensor_tensor(lg[:, :, :], lg[:, :, :], over_k(row1[:, :], NE), ALU.subtract).then_inc(s["e0"], 1)
                    dve.wait_ge(s["e1"], 1)
                    link(v.tensor_reduce(row1[:, :], lg[:, :, :], AX.X, ALU.add))
                    link(v.reciprocal(row2[:, :], row1[:, :]))
                    link(v.tensor_tensor(lg[:, :, :], lg[:, :, :], over_k(row2[:, :], NE), ALU.mult))
                for t in range(NT):
                    last = v.max(top[:, t, :], lg[:, t, :])
                link(last)
                for t in range(NT):
                    last = v.max_index(top_i[:, t, :], top[:, t, :], lg[:, t, :])
                link(last)
                link(v.tensor_copy(top_f[:, :, :], top_i[:, :, :]))
                wk = tw[:, :, 0:K]
                if m == 0:
                    v.tensor_tensor(wk, top[:, :, 0:K], over_k(top[:, :, 0:1].rearrange("p t a -> p (t a)"), K),
                                    ALU.subtract).then_inc(s["e0"], 1)
                    dve.wait_ge(s["e1"], 1)
                else:
                    link(v.tensor_reduce(row1[:, :], top[:, :, :], AX.X, ALU.add))
                    link(v.tensor_scalar(row1[:, :], row1[:, :], 1e-12, None, ALU.max))
                    link(v.reciprocal(row2[:, :], row1[:, :]))
                    link(v.tensor_tensor(tcum[:, :, :], top[:, :, :], over_k(row2[:, :], K), ALU.mult))
                    for k in range(1, K):
                        link(v.tensor_tensor(tcum[:, :, k], tcum[:, :, k], tcum[:, :, k - 1], ALU.add))
                    v.memset(act_k[:, :, 0:1], 1.0)
                    link(v.tensor_scalar(act_k[:, :, 1:K], tcum[:, :, 0:K - 1], THRESHOLD, None, ALU.is_lt))
                    v.tensor_tensor(wk, top[:, :, :], act_k[:, :, :], ALU.mult)
                    link(v.scalar_tensor_tensor(out=top_f[:, :, :], in0=top_f[:, :, :], scalar=1.0, in1=act_k[:, :, :],
                                                op0=ALU.add, op1=ALU.mult))
                    link(v.tensor_scalar(top_f[:, :, :], top_f[:, :, :], -1.0, None, ALU.add))
                link(v.tensor_reduce(row1[:, :], wk, AX.X, ALU.add))
                link(v.tensor_scalar(row1[:, :], row1[:, :], 1e-12, None, ALU.max))
                link(v.reciprocal(row2[:, :], row1[:, :]))
                link(v.tensor_scalar(row2[:, :], row2[:, :], tg[:, 2 + m:3 + m], None, ALU.mult))
                link(v.tensor_tensor(wk, wk, over_k(row2[:, :], K), ALU.mult))
                hot = one_hot[:, 0:NT * K * NE].rearrange("p (t k e) -> p t k e", t=NT, k=K)
                full = [P, NT, K, NE]
                link(v.tensor_tensor(hot, iota_f[:, :].unsqueeze(1).unsqueeze(1).to_broadcast(full),
                                     top_f[:, :, 0:K].unsqueeze(3).to_broadcast(full), ALU.is_equal))
                by_te = [P, NT, NE]
                v.tensor_reduce(mask_e[:, :].rearrange("p (t e) -> p t e", t=NT), hot.rearrange("p t k e -> p t e k"),
                                AX.X, ALU.add).then_inc(s["mk"], 1)
                dve.wait_ge(s["rk"], 2)
                v.memset(pref[:, 0, :], 0.0)
                link(v.tensor_copy(tot[:, :, :], bank[7][:, :].rearrange("p (t e) -> p t e", t=NT)))
                for t in range(NT):
                    link(v.tensor_tensor(pref[:, t + 1, :], pref[:, t, :], tot[:, t, :], ALU.add))
                wide = one_hot_2[:, 0:NE * (NT - 1)].rearrange("p (e n) -> p e n", e=NE)
                link(v.tensor_tensor(wide, pref[:, NT, :].unsqueeze(2).to_broadcast([P, NE, NT - 1]),
                                     steps_f[:, :].unsqueeze(1).to_broadcast([P, NE, NT - 1]), ALU.is_gt))
                link(v.tensor_reduce(n_tiles[:, :], wide, AX.X, ALU.add))
                link(v.tensor_scalar(n_tiles[:, :], n_tiles[:, :], 1.0, None, ALU.add))
                H, shift, c = NE // 2, 1, 0
                link(v.tensor_copy(cum[:, 0, H:H + NE], n_tiles[:, :]))
                while shift < NE:
                    link(v.tensor_tensor(cum[:, 1 - c, H:H + NE], cum[:, c, H:H + NE], cum[:, c, H - shift:H - shift + NE],
                                         ALU.add))
                    shift, c = 2 * shift, 1 - c
                ends = cum[:, c, H:H + NE]
                two = [P, 2, NE]
                link(v.tensor_tensor(le[:, :, :], ends.unsqueeze(1).to_broadcast(two),
                                     tile_f[:, :].unsqueeze(2).to_broadcast(two), ALU.is_le))
                link(v.tensor_tensor(le_n[:, :, :], le[:, :, :], n_tiles[:, :].unsqueeze(1).to_broadcast(two), ALU.mult))
                v.tensor_reduce(tab[:, 2:4], le[:, :, :], AX.X, ALU.add)
                link(v.tensor_reduce(past[:, :], le_n[:, :, :], AX.X, ALU.add))
                link(v.tensor_tensor(past[:, :], tile_f[:, :], past[:, :], ALU.subtract))
                v.tensor_scalar(tab[:, 0:2], tab[:, 2:4], float(NE - 1), None, ALU.min)
                link(v.tensor_scalar(past[:, :], past[:, :], float(P), None, ALU.mult))
                link(v.scalar_tensor_tensor(out=tab[:, 2:4], in0=tab[:, 2:4], scalar=float(ROWS), in1=past[:, :],
                                            op0=ALU.mult, op1=ALU.add))
                v.tensor_scalar(tab[:, 2:4], tab[:, 2:4], float(REG * ROWS - P), None, ALU.min).then_inc(s["tb"], 1)
                pos3 = posn[:, :].rearrange("p (t e) -> p t e", t=NT)
                link(v.tensor_tensor(pos3, bank[6][:, :].rearrange("p (t e) -> p t e", t=NT), pref[:, 0:NT, :], ALU.add))
                link(v.tensor_tensor(pos3, pos3, region_f[:, :].unsqueeze(1).to_broadcast(by_te), ALU.add))
                if m == 0:
                    hot_w = scratch[:, NT * K * NE:2 * NT * K * NE].rearrange("p (t k e) -> p t k e", t=NT, k=K)
                    link(v.tensor_tensor(hot_w, hot, wk.unsqueeze(3).to_broadcast(full), ALU.mult))
                    v.tensor_reduce(cw[:, :].rearrange("p (t e) -> p t e", t=NT), hot_w.rearrange("p t k e -> p t e k"),
                                    AX.X, ALU.add).then_inc(s["cw"], 1)
                link(v.tensor_tensor(hot, hot, pos3.unsqueeze(2).to_broadcast(full), ALU.mult))
                link(v.tensor_reduce(pos_k[:, :, 0:K], hot, AX.X, ALU.add))
                if m == 1:
                    link(v.tensor_scalar(tcum[:, :, :], act_k[:, :, :], -float(OFF), float(OFF), ALU.mult, ALU.add))
                    link(v.tensor_tensor(pos_k[:, :, :], pos_k[:, :, :], tcum[:, :, :], ALU.add))
                    dve.wait_ge(s["rk"], 3)
                    link(v.tensor_reduce(cnt_k[:, :], bank[5][:, 0:NT * 8].rearrange("p (t k) -> p k t", t=NT),
                                         AX.X, ALU.add))
                    link(v.tensor_scalar(cnt_k[:, :], cnt_k[:, :], 0.0, None, ALU.is_gt))
                    link(v.tensor_reduce(row1[:, 0:1], cnt_k[:, :], AX.X, ALU.add))
                    v.tensor_copy(cnt_i[:, NE + 1:NE + 2], row1[0:1, 0:1])
                else:
                    v.memset(cnt_i[:, NE + 1:NE + 2], K)
                v.tensor_copy(pos_i[:, :, 0:K], pos_k[:, :, 0:K])
                v.tensor_copy(cnt_i[:, 0:NE], pref[0:1, NT, :])
                link(v.tensor_scalar(cnt_i[:, NE:NE + 1], cum[0:1, c, H + NE - 1:H + NE], float(-NE), None, ALU.add))
                dve.wait_ge(s["tp"], 1)
                link(v.tensor_copy(tab_i[:, :], bank[4][0:1, :]))
                v.memset(row2[0:1, 0:1], 0.0).then_inc(s["tab"], 1)
                if m == 0:
                    for n in range(NT // 2):
                        dve.wait_ge(s["bd"], n + 1)
                        xt = X[:, 2 * n * D:2 * (n + 1) * D]
                        v.tensor_tensor(xt, xt, bank[4 + n % 2][:, :], ALU.add).then_inc(s["bdx"], 1)
                    dve.wait_ge(s["bdx"], NT // 2)

            def experts(m):
                s, I = M[m], INNER[m]

                def first_half(v_, p):
                    if m == 0:
                        gu = bank[2 + p][:, :].rearrange("p (t n) -> p t n", t=2)
                        dve.wait_ge(s["gu"], v_ + 1)
                        wait(dve, s["gs"], v_ - 1)
                        v.tensor_scalar(gmin[:, p, :, :], gu[:, :, 0:P], LIMIT, None, ALU.min).then_inc(s["gmin"], 1)
                        wait(dve, s["h"], v_ - 1)
                        v.tensor_scalar(umin[:, p, :, :], gu[:, :, P:2 * P], LIMIT + 1.0, 1.0 - LIMIT,
                                        ALU.min, ALU.max).then_inc(s["umin"], 1)

                def second_half(v_, p):
                    dve.wait_ge(s["sig"], v_ + 1)
                    wait(dve, s["ht"], v_ - 1)
                    if m == 0:
                        v.tensor_tensor(sig[:, p, :, :], sig[:, p, :, :], gmin[:, p, :, :], ALU.mult).then_inc(s["gs"], 1)
                        dve.wait_ge(s["gs"], v_ + 1)
                        dve.wait_ge(s["umin"], v_ + 1)
                        v.tensor_tensor(hid[:, p, :, :], sig[:, p, :, :], umin[:, p, :, :], ALU.mult).then_inc(s["h"], 1)
                    else:
                        gu = bank[2 + p][:, :].rearrange("p (t n) -> p t n", t=2)
                        v.tensor_tensor(hid[:, p, :, 0:I], sig[:, p, :, 0:I], gu[:, :, I:2 * I], ALU.mult)\
                            .then_inc(s["h"], 1)

                def weigh(v_, p):
                    dve.wait_ge(s["dn"], v_ + 1)
                    dve.wait_ge(s["tail"], v_ + 1)
                    for t in range(2):
                        wait(dve, s[f"sc{t}"], 16 * (v_ - 1))
                        last = v.tensor_scalar(y[:, p, t, :], bank[6 + p][:, t * D:(t + 1) * D],
                                               tails[:, ds(2 * v_ + t, 1), 1:2].rearrange("p a n -> p (a n)"), None,
                                               ALU.mult)
                    last.then_inc(s["y"], 1)

                def step(v_, p, last=0):
                    if not early(v_, 1) and last < 2:
                        first_half(v_ - 1, 1 - p)
                    if not early(v_, 3):
                        weigh(v_ - 3, 1 - p)
                    if not early(v_, 1) and last < 2:
                        second_half(v_ - 1, 1 - p)
                by_tiles(dve, m, step, 3)
                n = TPC * D
                for c in range(NCH):
                    at = slice(c * n, (c + 1) * n)
                    dve.wait_ge(s[f"rd{c}"], 32)
                    v.tensor_tensor(X[:, at], X[:, at], acc1[:, at], ALU.add).then_inc(s["x"], 1)
                dve.wait_ge(s["x"], NCH)

            prepare(0)
            experts(0)

            token_stats(C)
            by_two(dve, lambda t, p: normalise(C, t, p, C["tr"], t - 1), NT, 2)

            def row_max(b, p):
                wait(dve, C["s"], b - 1)
                v.tensor_scalar(mrow[:, p, :], mask_u8[:, ds(b * P, P)], -1.0, NEG, ALU.add, ALU.mult).then_inc(C["mr"], 1)
                dve.wait_ge(C["s"], b + 1)
                v.tensor_reduce(smax[:, ds(b, 1)], bank[p][:, 0:P], AX.X, ALU.max).then_inc(C["mx"], 1)
                dve.wait_ge(C["mx"], b + 1)
                v.tensor_scalar(nbias[:, ds(b, 1)], smax[:, ds(b, 1)], -SCALE, None, ALU.mult).then_inc(C["nb"], 1)

            def scale_rows(b, p):
                dve.wait_ge(C["e"], b + 1)
                v.reciprocal(rinv[:, ds(b, 1)], psum_row[:, ds(b, 1)]).then_inc(C["ri"], 1)
                dve.wait_ge(C["ri"], b + 1)
                wait(dve, C["at"], b - 1)
                v.tensor_scalar(attn[:, p, :], prob[:, p, :], rinv[:, ds(b, 1)], valid_t[:, ds(b, 1)],
                                ALU.mult, ALU.mult).then_inc(C["a"], 1)

            def read_copy(b, p):
                dve.wait_ge(C["ro"], b + 1)
                v.tensor_copy(roT[:, :, :, ds(b * G, G)],
                              bank[4 + p][:, 0:D].rearrange("p (k h i) -> p k h i", k=KB, h=NT)).then_inc(C["rot"], 1)

            def attend(b, p):
                row_max(b, p)
                if not (isinstance(b, int) and b < 1):
                    scale_rows(b - 1, 1 - p)
                if not (isinstance(b, int) and b < 2):
                    read_copy(b - 2, p)
            by_two(dve, attend, NB, 4)
            scale_rows(NB - 1, 1)
            read_copy(NB - 2, 0)
            read_copy(NB - 1, 1)
            for n in range(NT // 2):
                dve.wait_ge(C["fx"], n + 1)
                xt = X[:, 2 * n * D:2 * (n + 1) * D]
                v.tensor_tensor(xt, xt, bank[6 + n % 2][:, :], ALU.add).then_inc(C["x"], 1)
            dve.wait_ge(C["x"], NT // 2)

            prepare(1)
            experts(1)


def kernel(**inputs):
    import numpy as np
    import concourse.bacc as bacc
    from concourse.bass_utils import run_bass_kernel_spmd as run

    a = {k: np.asarray(v) for k, v in inputs.items()}
    x, c = a["x"], a["ctx_2048"]
    B, S, D = x.shape
    NT = a["L0_xattn_k"].shape[0]
    G = S // NT
    P, KB, E = 128, D // 128, a["L0_ffn_gate_w"].shape[0]

    def rows(t):
        return t.reshape(B, NT, G, D).transpose(0, 2, 1, 3).reshape(B * G, NT, D)

    def router(w):
        return w.T.reshape(KB, P, E).transpose(1, 0, 2).reshape(P, KB * E)

    def experts(gate, up, down):
        both = np.concatenate([gate, up], axis=2).reshape(E, KB, P, -1).transpose(0, 2, 1, 3).reshape(E, P, -1)
        down = np.concatenate([down, np.zeros((E, P - down.shape[1], D), down.dtype)], axis=1)
        return np.concatenate([both, down], axis=2).transpose(1, 0, 2)

    gu = a["L1_ffn_gate_up_proj"].transpose(0, 2, 1)
    I1 = gu.shape[2] // 2
    down1 = a["L1_ffn_down_proj"].transpose(0, 2, 1)
    k = a["L0_xattn_k"]
    arrays = {
        "x_rows": rows(x),
        "ctx_rows": rows(c),
        "ctx_cols": rows(c).transpose(2, 1, 0).reshape(KB, P, NT, P).transpose(1, 0, 2, 3),
        "ctx_batch": c,
        "filt": np.concatenate([np.zeros((NT, P), k.dtype), k], axis=1),
        "skip_cols": np.tile(a["fside_S2_0"].reshape(NT, G).T, (B, 1)),
        "mask": a["mask_BxS2_bk0"].reshape(1, B * S),
        "gates": np.concatenate([a["g_xattn"], a["g_ffn"]]),
        "router0": router(a["L0_ffn_gate_w"]),
        "router0_bias": a["L0_ffn_gate_b"].reshape(E, 1),
        "in_bias0": np.concatenate([a["L0_ffn_b_gate"], a["L0_ffn_b_up"]], axis=1),
        "down_bias0": a["L0_ffn_b_down"],
        "experts0": experts(a["L0_ffn_w_gate"], a["L0_ffn_w_up"], a["L0_ffn_w_down"]),
        "router1": router(a["L1_ffn_gate_weight"]),
        "experts1": experts(gu[:, :, :I1], gu[:, :, I1:], down1),
    }
    arrays = {f"in_{n}": np.ascontiguousarray(v) for n, v in arrays.items()}
    nc = bacc.Bacc("TRN2", target_bir_lowering=False, num_devices=1)
    args = [nc.dram_tensor(n, v.shape, mybir.dt.from_np(v.dtype), kind="ExternalInput").ap() for n, v in arrays.items()]
    args.append(nc.dram_tensor("out", (P, NT, D), mybir.dt.from_np(x.dtype), kind="ExternalOutput").ap())
    bass_flamingo_gated_two_layers_kernel(nc, *args)
    got = run(nc, [arrays], core_ids=[0]).results[0]["out"]
    return got.reshape(B, G, NT, D).transpose(0, 2, 1, 3).reshape(B, S, D)
```

```python
import concourse.bass as bass
from concourse import mybir
from contextlib import ExitStack


def bass_flamingo_gated_two_layers_kernel(
    nc: bass.Bass,
    x_rows: bass.AP,
    ctx_rows: bass.AP,
    ctx_cols: bass.AP,
    ctx_batch: bass.AP,
    filt: bass.AP,
    skip_cols: bass.AP,
    mask: bass.AP,
    gates: bass.AP,
    router0: bass.AP,
    router0_bias: bass.AP,
    in_bias0: bass.AP,
    down_bias0: bass.AP,
    experts0: bass.AP,
    router1: bass.AP,
    experts1: bass.AP,
    out: bass.AP,
):
    fp32 = mybir.dt.float32
    fp32r = mybir.dt.float32r
    i32 = mybir.dt.int32
    u8 = mybir.dt.uint8
    ALU = mybir.AluOpType
    ACT = mybir.ActivationFunctionType
    AX = mybir.AxisListType
    PE, DVE, ACTIVATION = mybir.EngineType.PE, mybir.EngineType.DVE, mybir.EngineType.Activation
    ds = bass.ds

    P = 128
    NT = x_rows.shape[1]
    D = x_rows.shape[2]
    KB = D // P
    NB = ctx_batch.shape[0]
    G = P // NB
    TOK = NT * P
    NE = experts0.shape[1]
    CH = 512
    NCH = TOK // CH
    TPC = CH // P
    BG = CH // P
    NG = NB // BG
    BODY = 4
    WR = D + NE
    WT = P + 2
    SMAX = 2 * P
    LAST = 6
    EPS = 1e-5
    LIMIT = 7.0
    ALPHA = 1.702
    NEG = 1e30
    TOPK = (4, 8)
    THRESHOLD = 0.8
    INNER = (128, 96)
    NONE = (-3e38, -1.0)
    GONE = (3e38, -2.0)
    SCALE = float(D) ** -0.5

    ctx = ExitStack()
    with ctx:
        def sb(name, shape, dt=fp32):
            return ctx.enter_context(nc.sbuf_tensor(name, shape, dt))

        def sem(name):
            return ctx.enter_context(nc.semaphore(name))

        def sems(prefix, names):
            return {n: sem(f"{prefix}_{n}") for n in names.split()}

        X = sb("X", [P, NT * D])
        cols = sb("cols", [P, KB, NT, P])
        scratch = sb("scratch", [P, 4096])
        big = sb("big", [P, NE * WT])
        wts = sb("wts", [P, NE * 6 * P])
        toep = sb("toep", [P, 2, D])
        xn = sb("xn", [P, 2, D])
        vT = sb("vT", [P, 2, KB, P])
        prod = sb("prod", [P, KB, 1024])
        fold1 = sb("fold1", [P, KB, 512])
        fold2 = sb("fold2", [P, KB, 256])
        skipv = sb("skipv", [P, 2, D])
        mixed = sb("mixed", [P, 2, D])
        skc = sb("skc", [P, NT])
        stats = sb("stats", [P, NT, 6])
        mv = sb("mv", [P, NT * 2])
        var_e = sb("var_e", [P, NT])
        std = sb("std", [P, NT])
        rstd = sb("rstd", [P, NT])
        newt = sb("newt", [P, NT])
        shift = sb("shift", [P, NT])
        ident = sb("ident", [P, P])
        flip = sb("flip", [P, P])
        same_b = sb("same_b", [P, P])
        ones = sb("ones", [P, P])
        up = sb("up", [P, 1 + P])
        eye2 = sb("eye2", [2 * NE, NE])
        no_row = sb("no_row", [P, D])
        steps_i = sb("steps_i", [P, NT - 1], i32)
        steps_f = sb("steps_f", [P, NT - 1])
        tile_i = sb("tile_i", [P, 2], i32)
        tile_f = sb("tile_f", [P, 2])
        iota_i = sb("iota_i", [P, P], i32)
        iota_f = sb("iota_f", [P, P])
        gate_in = sb("gate_in", [P, 4])
        tg = sb("tg", [P, 4])
        mask_u8 = sb("mask_u8", [1, NB * P], u8)
        valid = sb("valid", [1, NB])
        valid_t = sb("valid_t", [P, NB])
        rt = [sb(f"rt{m}", [P, KB * NE]) for m in range(2)]
        rt_bias = sb("rt_bias", [P, NE])
        in_b = sb("in_b", [2 * NE, 2 * P])
        in_bp = sb("in_bp", [2 * NE, 2 * P], fp32r)
        down_b = sb("down_b", [NE, D])
        top = sb("top", [P, NT, 8])
        tcum = sb("tcum", [P, NT, 8])
        row1 = sb("row1", [P, NT])
        row2 = sb("row2", [P, NT])
        n_e = sb("n_e", [P, NE])
        act_k = sb("act_k", [P, NT, 8])
        n_tiles = sb("n_tiles", [P, NE])
        cum = sb("cum", [P, 2, NE // 2 + NE])
        le = sb("le", [P, 2, NE])
        le_n = sb("le_n", [P, 2, NE])
        tab = sb("tab", [P, 4])
        past = sb("past", [P, 2])
        tab_i = sb("tab_i", [1, SMAX], i32)
        base = sb("base", [P, SMAX])
        place = sb("place", [P, SMAX])
        cnt_i = sb("cnt_i", [1, 1], i32)
        starts = sb("starts", [NT, NE])
        seek = sb("seek", [P, 2, 2])
        found = sb("found", [P, 2, 2])
        idx_x = sb("idx_x", [P, 2, 2], i32)
        sel = sb("sel", [2 * NE, 2, 2, P], fp32r)
        idx_y = sb("idx_y", [P, 2, 2], i32)
        smax = sb("smax", [P, NB])
        psum_row = sb("psum_row", [P, NB])
        rinv = sb("rinv", [P, NB])

        kv = scratch[:, :].rearrange("p (s k n) -> p s k n", s=2, k=KB)
        rows = big[:, 0:NT * D]
        late = NE * 6 * P - NE // 4 * 6 * P
        toep_all = wts[:, late:late + NT * D].rearrange("p (t n) -> p t n", t=NT)
        kept = big[:, 0:NT * D].rearrange("p (t n) -> p t n", t=NT)
        find = big[0:NT, :].rearrange("p (e n) -> p e n", e=NE)
        xT_all = scratch[:, :].rearrange("p (k n) -> p k n", k=KB)
        lgT = prod[0:NE, :, :].rearrange("p k n -> p (k n)")
        lg = toep[:, :, :].rearrange("p s (t e) -> p (s t) e", e=NE)
        mask_e = skipv[:, :, :].rearrange("p s n -> p (s n)")
        steps = vT[:, :, :, :].rearrange("p s k (t e) -> p (s k t) e", e=NE)
        cw = fold2[:, :, :].rearrange("p k n -> p (k n)")
        routed = scratch[:, 0:NT * (NE + 8)].rearrange("p (t e) -> p t e", t=NT)
        taken = scratch[:, NT * (NE + 8):2 * NT * (NE + 8)].rearrange("p (t e) -> p t e", t=NT)
        xT_b = scratch[:, :].rearrange("p (k b s) -> p k b s", k=KB, b=NB)
        one_hot_2 = fold1[:, :, :].rearrange("p k n -> p (k n)")
        spread = one_hot_2[:, 512:1024].rearrange("p (n q) -> p n q", n=4)
        acc1 = scratch[:, :]
        work = fold1[:, :, :].rearrange("p k n -> p (k n)")
        gmin = work[:, 0:512].rearrange("p (s t n) -> p s t n", s=2, t=2)
        umin = work[:, 512:1024].rearrange("p (s t n) -> p s t n", s=2, t=2)
        at = 4 * WR
        xt = X[:, 0:at].rearrange("p (s t n) -> p s t n", s=2, t=2)
        xT = X[:, at:at + 4 * D].rearrange("p (s n) -> p s n", s=2)
        y = X[:, at + 4 * D:at + 8 * D].rearrange("p (s t n) -> p s t n", s=2, t=2)
        compared = xn[:, :, :].rearrange("p s (t n) -> p s t n", t=2)
        wt_rows = X[:, at + 8 * D:at + 8 * D + SMAX]
        idx_rows = X[:, at + 8 * D + SMAX:at + 8 * D + 2 * SMAX]
        marks = toep[0:NT, :, :].rearrange("p s (t n) -> p s t n", t=2)
        sig = vT[:, :, :, :]
        hid = skipv[:, :, :].rearrange("p s (t n) -> p s t n", t=2)
        hT = mixed[:, :, :].rearrange("p s (t n) -> p s t n", t=2)
        turn = prod[:, :, :].rearrange("p k n -> p (k n)")
        memory = [work.rearrange("p (b n) -> p b n", b=BG)]
        memory += [turn[:, n:n + BG * D].rearrange("p (b n) -> p b n", b=BG) for n in (0, BG * D)]
        prob = [mixed[:, :, :].rearrange("p s n -> p (s n)"), cw]
        attnT = [toep[:, :, :].rearrange("p s n -> p (s n)"), xn[:, :, :].rearrange("p s n -> p (s n)")]
        mrow = [vT[0:1, :, :, :].rearrange("p s k n -> p (s k n)"), skipv[0:1, :, :].rearrange("p s n -> p (s n)")]
        roT = rows[:, :].rearrange("p (k h s) -> p k h s", k=KB, h=NT)
        lg2 = lg[:, :, :].rearrange("p t e -> p (t e)")

        bank = [ctx.enter_context(nc.psum_tensor(f"bank{i}", [P, 512], fp32)) for i in range(8)]

        s_x = sem("s_x")
        s_ctx = sem("s_ctx")
        s_cols = sem("s_cols")
        s_par = sem("s_par")
        s_par2 = sem("s_par2")
        s_toep = sem("s_toep")
        s_mem = [sem(f"s_mem{p}") for p in range(3)]
        s_w = [sem(f"s_w{m}") for m in range(2)]
        s_const = sem("s_const")
        s_tanh = sem("s_tanh")
        s_bias = sem("s_bias")
        s_valid = sem("s_valid")
        s_vb = sem("s_vb")
        s_out = sem("s_out")
        s_var = sem("s_var")
        s_shift = sem("s_shift")
        s_sd = sem("s_sd")
        s_sums = [sem(f"s_sums{c}") for c in range(NCH)]
        s_chain = sem("s_chain")
        s_zeroed = sem("s_zeroed")
        A = sems("A", "flip turned tp vn skv tr vt kv0 kv1 y z fp fd f2 out mix mixed x")
        N = [sems(f"N{m}", "xn tr xa xv l e0 e1 mk df cw tot tt fd ev pd tb tp tab tbl tbw"
                  + (" cwp cwt bd" if m == 0 else "")) for m in range(2)]
        M = [sems(f"M{m}", "init mark fnd fx ix ir ld0 ld1 tx wr xt gu sig h ht htc dn y sc0 sc1 "
                  "x" + (" sel gmin umin gs" if m == 0 else "")) for m in range(2)]
        C = sems("C", "xn tr xa xv s mr sb e a at atc ro rov roa fx x")

        table = [nc.dram_tensor(f"table{m}", (TOK, WR), fp32, kind="Internal").ap() for m in range(2)]
        acc = [[nc.dram_tensor(f"acc{m}{r}", (TOK, D), fp32, kind="Internal").ap() for r in range(2)] for m in range(2)]

        block = ctx.enter_context(nc.Block())

        def wait(eng, s, n):
            if isinstance(n, int) and n <= 0:
                return
            eng.wait_ge(s, n)

        def by_two(eng, step, n, peel):
            for t in range(peel):
                step(t, t % 2)
            with eng.Fori(peel // 2, n // 2, 1) as pair:
                for p in range(2):
                    step(2 * pair + p, p)

        def by_tiles(eng, m, step, lag):
            eng.wait_ge(N[m]["tab"], 1)
            more = eng.value_load(cnt_i[0:1, 0:1], min_val=0, max_val=TOK * TOPK[m] // P)
            bodies = (more + (BODY - 1)) // BODY + NE // BODY
            for v in range(8):
                step(v, v % 2, 0)
            with eng.Fori(4, bodies, 1) as q:
                for p in range(2):
                    step(2 * q + p, p, 0)
            for n in range(lag):
                step(2 * bodies + n, n % 2, n + 1)
            return bodies

        def due(v, over, lag):
            return not (isinstance(v, int) and v < lag) and over <= lag

        def experts_of(engine, v, pairs=1):
            _, values = nc.values_load_multi_w_load_instructions(
                tab_i[0:1, ds(2 * v, 2 * pairs)], engines=(engine,), min_val=0, max_val=NE - 1,
                skip_runtime_bounds_check_because="the tile table's experts are clamped to NE - 1")
            return values

        def half(v):
            return v // 2 + 1

        def turned(n, k):
            return bank[4 + n % 4][:, k * 2 * P:(k + 1) * 2 * P].rearrange("p (t b i) -> p t b i", t=2, b=NB)

        def by_batch(n, k):
            return xT_b[:, k, :, 2 * n * G:2 * (n + 1) * G].rearrange("p b (t i) -> p t b i", t=2)

        def readout_of(g, k):
            return (roT[:, k, :, g * BG * G:(g + 1) * BG * G].rearrange("p h (b i) -> p b h i", b=BG),
                    bank[4 + 2 * (g % 2) + k][:, :].rearrange("p (b h i) -> p b h i", b=BG, h=NT))

        @block.sync
        def _(sp):
            def load_experts(m, src, quarters=(0, 1, 2, 3)):
                n, width = NE // 4, src.shape[2]
                for e in [q * n for q in quarters]:
                    if m == 0 and e == NE - n:
                        sp.wait_ge(A["tp"], NT)
                    sp.dma_start(wts[:, e * width:(e + n) * width],
                                 src[:, e:e + n, :].rearrange("p e n -> p (e n)")).then_inc(s_w[m], 16)

            def experts(m):
                s = M[m]
                for c in range(NCH):
                    sp.wait_ge(N[m]["xn"], TPC * (c + 1))
                    rows_of = table[m][:, :].rearrange("(p t) n -> p t n", t=NT)
                    sp.dma_start(rows_of[:, TPC * c:TPC * (c + 1), 0:D], kept[:, TPC * c:TPC * (c + 1), :])\
                        .then_inc(N[m]["tbl"], 16)
                sp.dma_start(acc[m][0].rearrange("(p t) d -> p (t d)", t=NT), X[:, :]).then_inc(s["init"], 16)
                sp.wait_ge(N[m]["cw"], 1)
                sp.dma_start(rows_of[:, :, D:WR], cw[:, :].rearrange("p (t e) -> p t e", t=NT))\
                    .then_inc(N[m]["tbw"], 16)
                sp.wait_ge(N[m]["tab"], 1)
                more = sp.value_load(cnt_i[0:1, 0:1], min_val=0, max_val=TOK * TOPK[m] // P)
                bodies = (more + (BODY - 1)) // BODY + NE // BODY
                for r in range(2):
                    sp.wait_ge(s[f"sc{r}"], bodies * 32)
                n = TPC * D
                for c in range(NCH):
                    at = slice(c * n, (c + 1) * n)
                    for r, dst in enumerate((X, acc1)):
                        sp.dma_start(dst[:, at], acc[m][r].rearrange("(p t) d -> p (t d)", t=NT)[:, at])\
                            .then_inc(s_sums[c], 16)

            sp.dma_start(X[:, :], x_rows.rearrange("p t d -> p (t d)")).then_inc(s_x, 16)
            sp.dma_start(toep_all[:, :, :],
                         bass.AP(tensor=filt.tensor, offset=1, ap=[[1, P], [P + D, NT], [1, D]])).then_inc(s_toep, 16)
            sp.dma_start(skc[:, :], skip_cols).then_inc(s_par, 16)
            sp.dma_start(gate_in[:, :], gates.partition_broadcast(P)).then_inc(s_par, 16)
            sp.dma_start(cols[:, :, :, :], ctx_cols).then_inc(s_cols, 16)
            sp.dma_start(rows[:, :], ctx_rows.rearrange("p t d -> p (t d)")).then_inc(s_ctx, 16)
            sp.dma_start(mask_u8[:, :], mask).then_inc(s_par2, 16)
            sp.dma_start(rt[0][:, :], router0).then_inc(s_par2, 16)
            sp.dma_start(rt[1][:, :], router1).then_inc(s_par2, 16)
            sp.dma_start(rt_bias[:, :], router0_bias.partition_broadcast(P)).then_inc(s_par2, 16)
            for n in range(2):
                sp.dma_start(in_b[n * NE:(n + 1) * NE, :], in_bias0).then_inc(s_par2, 16)
            sp.dma_start(down_b[:, :], down_bias0).then_inc(s_par2, 16)
            load_experts(0, experts0, (0, 1))
            sp.wait_ge(s_const, 11)
            for m in range(2):
                sp.dma_start(acc[m][1].rearrange("(p t) d -> p t d", t=NT),
                             no_row[:, :].unsqueeze(1).to_broadcast([P, NT, D])).then_inc(M[m]["init"], 16)
            load_experts(0, experts0, (2, 3))
            experts(0)

            def load_memory(g):
                wait(sp, C["ro"], g - 2)
                sp.dma_start(memory[g % 3], ctx_batch[g * BG:(g + 1) * BG, :, :].rearrange("b s d -> s b d"))\
                    .then_inc(s_mem[g % 3], 16)
            sp.wait_ge(N[0]["bd"], NT // 2)
            for g in range(3):
                load_memory(g)
            load_experts(1, experts1, (0, 1))
            for g in range(3, NG):
                load_memory(g)
            load_experts(1, experts1, (2, 3))
            experts(1)
            for c in range(NCH):
                sp.wait_ge(M[1]["x"], c + 1)
                n = TPC * D
                sp.dma_start(out.rearrange("p t d -> p (t d)")[:, c * n:(c + 1) * n], X[:, c * n:(c + 1) * n])\
                    .then_inc(s_out, 16)
            sp.wait_ge(s_out, 16 * NCH)

        @block.gpsimd
        def _(pool):
            g = nc.gpsimd
            g.memset(ident[:, :], 0.0).then_inc(s_zeroed, 1)
            g.memset(same_b[:, :], 1.0).then_inc(s_zeroed, 1)
            g.memset(flip[:, :], 0.0).then_inc(s_zeroed, 1)
            g.memset(up[:, :], 1.0).then_inc(s_zeroed, 1)
            g.memset(eye2[:, :], 0.0).then_inc(s_zeroed, 1)
            g.memset(ones[:, :], 1.0).then_inc(s_const, 1)
            g.memset(cum[:, :, :], 0.0).then_inc(s_const, 1)
            g.memset(no_row[:, :], 0.0).then_inc(s_const, 1)
            g.iota(steps_i[:, :], pattern=[[P, NT - 1]], base=P, channel_multiplier=0).then_inc(s_const, 1)
            g.iota(tile_i[:, :], pattern=[[P, 2]], base=0, channel_multiplier=1).then_inc(s_const, 1)
            g.iota(iota_i[:, :], pattern=[[1, P]], base=0, channel_multiplier=0).then_inc(s_const, 1)
            pool.wait_ge(s_zeroed, 5)
            g.affine_select(out=up[:, :], in_=up[:, :], compare_op=ALU.is_gt, fill=0.0, base=0,
                            pattern=[[1, 1 + P]], channel_multiplier=-1).then_inc(s_const, 1)
            g.affine_select(out=eye2[:, :], in_=eye2[:, :], compare_op=ALU.not_equal, fill=1.0, base=0,
                            pattern=[[-1, NE]], channel_multiplier=1).then_inc(s_zeroed, 1)
            pool.wait_ge(s_zeroed, 6)
            g.affine_select(out=eye2[:, :], in_=eye2[:, :], compare_op=ALU.not_equal, fill=1.0, base=-NE,
                            pattern=[[-1, NE]], channel_multiplier=1).then_inc(s_const, 1)
            g.affine_select(out=flip[:, :], in_=flip[:, :], compare_op=ALU.not_equal, fill=1.0, base=1 - P,
                            pattern=[[1, P]], channel_multiplier=1).then_inc(s_const, 1)
            g.affine_select(out=ident[:, :], in_=ident[:, :], compare_op=ALU.not_equal, fill=1.0, base=0,
                            pattern=[[-1, P]], channel_multiplier=1).then_inc(s_const, 1)
            blocks = same_b[:, :].rearrange("p (b j) -> p b j", j=G)
            g.affine_select(out=blocks, in_=blocks, compare_op=ALU.is_ge, fill=0.0, base=0,
                            pattern=[[-G, NB], [0, G]], channel_multiplier=1).then_inc(s_zeroed, 1)
            pool.wait_ge(s_zeroed, 7)
            g.affine_select(out=blocks, in_=blocks, compare_op=ALU.is_ge, fill=0.0, base=G - 1,
                            pattern=[[G, NB], [0, G]], channel_multiplier=-1).then_inc(s_const, 1)

            def kv_high(h, p):
                wait(pool, A["vt"], h + 1)
                wait(pool, A["y"], 4 * h - 4)
                g.tensor_tensor(
                    kv[:, p, 1, :].rearrange("p (b i j) -> p b i j", b=NB, i=G),
                    vT[:, p, 1, :].rearrange("p (b i) -> p b i", i=G).unsqueeze(3).to_broadcast([P, NB, G, G]),
                    cols[:, 1, ds(h, 1), :].rearrange("p a (b j) -> p (a b) j", j=G).unsqueeze(2).to_broadcast([P, NB, G, G]),
                    ALU.mult).then_inc(A["kv1"], 1)

            def add_mixed(h, p):
                pool.wait_ge(A["mixed"], h + 1)
                xt = X[:, ds(h * D, D)]
                g.tensor_tensor(xt, xt, mixed[:, p, :], ALU.add).then_inc(A["x"], 1)

            def folds(h):
                pool.wait_ge(A["z"], 4 * h + 2)
                wait(pool, A["f2"], 2 * h - 1)
                z = prod[:, 0, :].rearrange("p (b i n) -> p b i n", b=NB, i=2)
                g.tensor_tensor(fold1[:, 0, :].rearrange("p (b n) -> p b n", b=NB), z[:, :, 0, :], z[:, :, 1, :],
                                ALU.add).then_inc(A["fp"], 1)
                for lh in range(KB):
                    pool.wait_ge(A["fd" if lh else "fp"], h + 1)
                    wait(pool, A["out"], h)
                    z = fold1[:, lh, :].rearrange("p (b a i j) -> p a i b j", b=NB, a=2, i=2)
                    g.tensor_tensor(fold2[:, lh, :].rearrange("p (i b j) -> p i b j", i=2, b=NB), z[:, 0, :, :, :],
                                    z[:, 1, :, :, :], ALU.add).then_inc(A["f2"], 1)

            def stage_a(h, p):
                kv_high(h, p)
                if not (isinstance(h, int) and h < 1):
                    folds(h - 1)
                if not (isinstance(h, int) and h < 2):
                    add_mixed(h - 2, p)
            pool.wait_ge(s_cols, 16)
            by_two(pool, stage_a, NT, 2)
            folds(NT - 1)
            for h in range(NT - 2, NT):
                add_mixed(h, h % 2)

            def experts(m):
                s = M[m]

                bound = pool.alloc_register(f"last_token{m}")
                pool.reg_mov(bound, TOK - 1)

                def last_token():
                    pool.reg_alu(bound, bound, TOK - 1, ALU.min)
                    return bass.RuntimeValue.of_register_unchecked(bound, min_val=0, max_val=TOK - 1)

                def gather(v, p):
                    pool.wait_ge(s["ix"], v + 1)
                    wait(pool, s["tx"], v - 1)
                    wait(pool, s["wr"], v - 1)
                    end = last_token()
                    for t in range(2):
                        g.indirect_dma_start(out=xt[:, p, t, :], out_offset=None, in_=table[m],
                                             in_offset=bass.IndirectOffsetOnAxis(ap=idx_x[:, p, t:t + 1], axis=0),
                                             bounds_check=end, oob_is_err=False).then_inc(s[f"ld{p}"], 16)

                def add_rows(v, p):
                    pool.wait_ge(s["y"], v + 1)
                    for t in range(2):
                        wait(pool, s[f"sc{t}"], 16 * v)
                        end = last_token()
                        g.indirect_dma_start(out=acc[m][t], out_offset=bass.IndirectOffsetOnAxis(ap=idx_y[:, p, t:t + 1], axis=0),
                                             in_=y[:, p, t, :], in_offset=None, bounds_check=end,
                                             oob_is_err=False, compute_op=ALU.add).then_inc(s[f"sc{t}"], 16)

                def step(v, p, over):
                    if due(v, over, 1):
                        gather(v - 1, 1 - p)
                    if due(v, over, LAST):
                        add_rows(v - LAST, p)
                pool.wait_ge(N[m]["tbl"], 16 * NCH)
                pool.wait_ge(N[m]["tbw"], 16)
                pool.wait_ge(s["init"], 32)
                g.memset(xt[:, :, :, :], 0.0).then_inc(s_zeroed, 1)
                pool.wait_ge(s_zeroed, 8 + m)
                by_tiles(pool, m, step, LAST)

            experts(0)

            pool.wait_ge(C["xn"], 1)
            for n in range(NG):
                wait(pool, C["s"], n - 1)
                g.tensor_scalar(mrow[n % 2], mask_u8[:, n * CH:(n + 1) * CH], -1.0, NEG, ALU.add, ALU.mult)\
                    .then_inc(C["mr"], 1)

            experts(1)

        @block.scalar
        def _(act):
            a = nc.scalar
            act.wait_ge(s_par, 32)
            a.activation(tg[:, :], gate_in[:, :], ACT.Tanh).then_inc(s_tanh, 1)

            def std_of(n):
                act.wait_ge(s_var, n + 1)
                a.activation(std[:, :], var_e[:, :], ACT.Sqrt).then_inc(s_sd, 1)

            std_of(0)
            for n in range(NT // 2):
                act.wait_ge(A["flip"], n + 1)
                a.activation(toep_all[:, 2 * n:2 * n + 2, :], bank[n % 4][:, :].rearrange("p (a n) -> p a n", a=2),
                             ACT.Copy).then_inc(A["turned"], 1)
            act.wait_ge(A["turned"], NT // 2)
            act.wait_ge(s_bias, 1)
            a.activation(in_bp[:, :], in_b[:, :], ACT.Copy).then_inc(s_bias, 1)

            def v_copy(h, p):
                act.wait_ge(A["tr"], h + 1)
                wait(act, A["kv0"], h - 1)
                wait(act, A["kv1"], h - 1)
                a.activation(vT[:, p, :, :], bank[4 + p][:, 0:D].rearrange("p (k n) -> p k n", k=KB), ACT.Copy)\
                    .then_inc(A["vt"], 1)
            def filter_copy(h, p):
                wait(act, A["y"], 4 * h - 4)
                a.activation(toep[:, p, :], toep_all[:, ds(h, 1), :].rearrange("p a n -> p (a n)"), ACT.Copy)\
                    .then_inc(A["tp"], 1)

            def v_rows(h, p):
                wait(act, A["tr"], h - 1)
                wait(act, A["skv"], h - 1)
                a.activation(xn[:, p, :], X[:, ds(h * D, D)], ACT.Identity, scale=rstd[:, ds(h, 1)],
                             bias=shift[:, ds(h, 1)]).then_inc(A["vn"], 1)

            def stage_a(h, p):
                filter_copy(h, p)
                if not (isinstance(h, int) and h > NT - 2):
                    v_copy(h + 1, 1 - p)
                if not (isinstance(h, int) and h > NT - 3):
                    v_rows(h + 2, p)
            act.wait_ge(s_shift, 1)
            for h in range(2):
                v_rows(h, h)
            v_copy(0, 0)
            for h in range(2):
                stage_a(h, h)
            with act.Fori(1, NT // 2 - 1, 1) as pair:
                for p in range(2):
                    stage_a(2 * pair + p, p)
            for h in range(NT - 2, NT):
                stage_a(h, h % 2)

            def prepare(m):
                s = N[m]
                std_of(1 + 2 * m)

                for n in range(0, NT // 2, 2):
                    act.wait_ge(s["tr"], n + 1)
                    a.activation(xT_all[:, :, 2 * n * P:2 * (n + 1) * P],
                                 bank[4 + n % 4][:, :].rearrange("p (k n) -> p k n", k=KB), ACT.Copy).then_inc(s["xa"], 1)
                act.wait_ge(s["e0"], 1)
                a.activation(lg2, lg2, ACT.Exp).then_inc(s["e1"], 1)
                act.wait_ge(s["tbl"], 16 * NCH)
                for n in range(0, NE // 4, 2):
                    act.wait_ge(s["fd"], n + 1)
                    a.activation(find[:, 4 * n:4 * n + 4, 0:P], bank[n][0:NT, :].rearrange("p (e n) -> p e n", e=4),
                                 ACT.Copy).then_inc(s["ev"], 1)
                if m == 0:
                    for c in range(NCH):
                        act.wait_ge(s["cwp"], c + 1)
                        a.activation(lgT[:, c * CH:(c + 1) * CH], bank[c][0:NE, :], ACT.Copy).then_inc(s["cwt"], 1)

            def experts(m):
                s, I = M[m], INNER[m]

                def x_turned(v, p):
                    act.wait_ge(s["tx"], v + 1)
                    wait(act, s["gu"], v - 1)
                    a.activation(xT[:, p, :], bank[0][:, :], ACT.Copy).then_inc(s["xt"], 1)

                def keep_weights(v, p):
                    e = experts_of(ACTIVATION, v)
                    act.wait_ge(s[f"ld{p}"], half(v) * 32)
                    for t in range(2):
                        last = a.activation(wt_rows[:, ds(2 * v + t, 1)], xt[:, p, t, ds(e[t] + D, 1)], ACT.Copy)
                    last.then_inc(s["wr"], 1)
                    if m == 0:
                        wait(act, s["gu"], v - 1)
                        for t in range(2):
                            last = a.activation(sel[:, p, t, :], eye2[:, ds(e[t], 1)].to_broadcast([2 * NE, P]), ACT.Copy)
                        last.then_inc(s["sel"], 1)

                def sigmoid(v, p):
                    wait(act, s["h"], v - 1)
                    if m == 0:
                        act.wait_ge(s["gmin"], v + 1)
                        a.activation(sig[:, p, :, :], gmin[:, p, :, :], ACT.Sigmoid, scale=ALPHA).then_inc(s["sig"], 1)
                    else:
                        act.wait_ge(s["gu"], v + 1)
                        gu = bank[2 + p][:, :].rearrange("p (t n) -> p t n", t=2)
                        a.activation(sig[:, p, :, 0:I], gu[:, :, 0:I], ACT.Silu).then_inc(s["sig"], 1)

                def h_turned(v, p):
                    act.wait_ge(s["ht"], v + 1)
                    wait(act, s["dn"], v - 1)
                    a.activation(hT[0:I, p, :, :], bank[4 + p][0:I, 0:2 * P].rearrange("p (t n) -> p t n", t=2),
                                 ACT.Copy).then_inc(s["htc"], 1)

                def step(v, p, over):
                    if due(v, over, 3):
                        x_turned(v - 3, 1 - p)
                    if due(v, over, 4):
                        sigmoid(v - 4, p)
                    if due(v, over, 5):
                        h_turned(v - 5, 1 - p)
                    if due(v, over, 2):
                        keep_weights(v - 2, p)
                by_tiles(act, m, step, 5)

            prepare(0)
            experts(0)

            std_of(2)

            for n in range(0, NT // 2, 2):
                act.wait_ge(C["tr"], n + 1)
                for k in range(KB):
                    mm = a.activation(by_batch(n, k), turned(n, k), ACT.Copy)
                mm.then_inc(C["xa"], 1)

            for v in range(NG + 2):
                if v < NG:
                    act.wait_ge(C["sb"], v + 1)
                    a.activation(prob[v % 2], prob[v % 2], ACT.Exp, scale=SCALE).then_inc(C["e"], 1)
                if 1 <= v <= NG:
                    act.wait_ge(C["at"], v)
                    wait(act, C["ro"], v - 2)
                    a.activation(attnT[(v - 1) % 2], bank[2 + (v - 1) % 2][:, :], ACT.Copy).then_inc(C["atc"], 1)
                if v >= 2:
                    act.wait_ge(C["ro"], v - 1)
                    a.activation(*readout_of(v - 2, 0), ACT.Copy).then_inc(C["roa"], 1)

            prepare(1)
            experts(1)

        @block.tensor
        def _(pe):
            t_ = nc.tensor

            def transposes(s, free, t, p, n_free):
                pe.wait_ge(s["xn"], t + 1)
                wait(pe, free, n_free)
                for k in range(KB):
                    mm = t_.transpose(bank[4 + p][:, k * P:(k + 1) * P], xn[:, p, k * P:(k + 1) * P], ident[:, :])
                mm.then_inc(s["tr"], 1)

            pe.wait_ge(s_const, 11)
            pe.wait_ge(s_toep, 16)
            for n in range(NT // 2):
                wait(pe, A["turned"], n - 3)
                t_.matmul(bank[n % 4][:, :], flip[:, :], toep_all[:, 2 * n:2 * n + 2, :], start=True, stop=True)\
                    .then_inc(A["flip"], 1)
            pe.wait_ge(s_valid, 1)
            t_.matmul(bank[7][:, 0:NB], ones[0:1, :], valid[:, :], start=True, stop=True).then_inc(s_vb, 1)

            def conv(h, p):
                pe.wait_ge(A["tp"], h + 1)
                for n in range(4):
                    lh, half = n // 2, n % 2
                    if n == 0:
                        pe.wait_ge(A["kv0"], h + 1)
                    if n == 2:
                        pe.wait_ge(A["kv1"], h + 1)
                    wait(pe, A["z"], 4 * h - 3 + n)
                    for k in range(lh + 1):
                        mm = t_.matmul(bank[n][:, :], toep[:, p, (lh - k) * P:(lh - k + 1) * P],
                                       kv[:, p, k, half * 512:(half + 1) * 512], start=(k == 0), stop=(k == lh))
                    mm.then_inc(A["y"], 1)

            def gather_i(h, p):
                pe.wait_ge(A["f2"], 2 * h + 2)
                wait(pe, A["mixed"], h)
                for lh in range(KB):
                    for i in range(2):
                        t_.matmul(bank[6][:, lh * P:(lh + 1) * P],
                                  fold2[:, lh, i * P:(i + 1) * P],
                                  ident[:, :], start=(i == 0), stop=(i == 1))
                pe.wait_ge(A["skv"], h + 1)
                t_.matmul(bank[7][:, 0:D], same_b[:, :], skipv[:, p, :], start=True, stop=True).then_inc(A["out"], 1)

            sA = {"xn": A["vn"], "tr": A["tr"]}

            def stage_a(h, p):
                if not (isinstance(h, int) and h > NT - 3):
                    transposes(sA, A["vt"], h + 2, p, h + 1)
                if not (isinstance(h, int) and h > NT - 2):
                    conv(h + 1, 1 - p)
                gather_i(h, p)

            for t in range(2):
                transposes(sA, A["vt"], t, t, t - 1)
            conv(0, 0)
            pe.wait_ge(s_vb, 1)
            pe.wait_ge(s_tanh, 1)
            for h in range(2):
                stage_a(h, h)
            with pe.Fori(1, NT // 2 - 1, 1) as pair:
                for p in range(2):
                    stage_a(2 * pair + p, p)
            for h in range(NT - 2, NT):
                stage_a(h, h % 2)

            def all_transposes(s, then=None):
                for n in range(NT // 2):
                    if then and n >= 2:
                        then(n - 2)
                    pe.wait_ge(s["xn"], 2 * n + 2)
                    wait(pe, s["xv" if n % 2 else "xa"], n // 2 - 1)
                    for t in range(2):
                        for k in range(KB):
                            mm = t_.transpose(bank[4 + n % 4][:, (2 * k + t) * P:(2 * k + t + 1) * P],
                                              kept[:, 2 * n + t, k * P:(k + 1) * P], ident[:, :])
                    mm.then_inc(s["tr"], 1)

            def prepare(m):
                s = N[m]
                def logits(n):
                    pe.wait_ge(s["xv" if n % 2 else "xa"], n // 2 + 1)
                    for t in range(2 * n, 2 * n + 2):
                        for k in range(KB):
                            mm = t_.matmul(bank[0][:, t * NE:(t + 1) * NE], xT_all[:, k, t * P:(t + 1) * P],
                                           rt[m][:, k * NE:(k + 1) * NE], start=(k == 0), stop=(k == KB - 1))
                    return mm
                all_transposes(s, logits)
                logits(NT // 2 - 2)
                logits(NT // 2 - 1).then_inc(s["l"], 1)
                pe.wait_ge(s["mk"], 1)
                t_.matmul(bank[4][:, :], ones[:, :], mask_e[:, :], start=True, stop=True).then_inc(s["tot"], 1)
                pe.wait_ge(s["df"], 1)
                for n in range(NE // 4):
                    if n == 4:
                        pe.wait_ge(s["tt"], 1)
                    for i in range(4):
                        mm = t_.matmul(bank[n][0:NT, i * P:(i + 1) * P], steps[:, :, 4 * n + i], up[:, 1:1 + P],
                                       start=True, stop=True)
                    mm.then_inc(s["fd"], 1)
                pe.wait_ge(s["ev"], NE // 4)
                t_.matmul(bank[5][0:NT, 0:NE], up[0:NT, 0:NT], find[:, :, P - 1], start=True, stop=True)\
                    .then_inc(s["pd"], 1)
                pe.wait_ge(s["tt"], 2)
                t_.matmul(bank[5][0:NT, NE:2 * NE], up[0:NT, 1:1 + NT], find[:, :, P], start=True, stop=True)\
                    .then_inc(s["pd"], 1)
                pe.wait_ge(s["tb"], 1)
                t_.matmul(bank[6][:, :], ones[:, :], spread[:, :, :].rearrange("p n q -> p (n q)"), start=True, stop=True)\
                    .then_inc(s["tp"], 1)
                if m == 0:
                    pe.wait_ge(s["cw"], 1)
                    for t in range(NT):
                        c, n = divmod(t, TPC)
                        mm = t_.matmul(bank[c][0:NE, n * P:(n + 1) * P], cw[:, t * NE:(t + 1) * NE], ident[:, :],
                                       start=True, stop=True)
                        if n == TPC - 1:
                            mm.then_inc(s["cwp"], 1)

            def experts(m):
                s, I = M[m], INNER[m]
                width = 4 * I + D
                pe.wait_ge(s_w[m], 16 * (NE // 8))
                if m == 0:
                    pe.wait_ge(s_bias, 3)
                    pe.wait_ge(N[m]["cwt"], NCH)

                def find_rows(v, p, e):
                    pe.wait_ge(s["mark"], v + 1)
                    wait(pe, s["ir"], v)
                    for t in range(2):
                        mm = t_.matmul(bank[1][:, t * WT:(t + 1) * WT], marks[:, p, t, :], big[0:NT, ds(e[t] * WT, WT)],
                                       start=True, stop=True)
                    mm.then_inc(s["fnd"], 1)

                def x_turn(v, p):
                    pe.wait_ge(s[f"ld{p}"], half(v) * 32)
                    wait(pe, s["xt"], v)
                    for t in range(2):
                        for k in range(KB):
                            mm = t_.transpose(bank[0][:, (t * KB + k) * P:(t * KB + k + 1) * P],
                                              xt[:, p, t, k * P:(k + 1) * P], ident[:, :])
                    mm.then_inc(s["tx"], 1)

                def gate_up(v, p, e, turned_before):
                    if not turned_before:
                        pe.wait_ge(s["xt"], v + 1)
                    if m == 0:
                        pe.wait_ge(s["sel"], v + 1)
                    for t in range(2):
                        dst = bank[2 + p][:, t * 2 * P:t * 2 * P + 2 * I]
                        if m == 0:
                            t_.matmul(dst, sel[:, p, t, :], in_bp[:, :], start=True, stop=False)
                        for k in range(KB):
                            mm = t_.matmul(dst, xT[:, p, (t * KB + k) * P:(t * KB + k + 1) * P],
                                           wts[:, ds(e[t] * width + k * 2 * I, 2 * I)], start=(m == 1 and k == 0), stop=(k == KB - 1))
                    mm.then_inc(s["gu"], 1)

                def h_turn(v, p):
                    pe.wait_ge(s["h"], v + 1)
                    for t in range(2):
                        mm = t_.transpose(bank[4 + p][0:I, t * P:(t + 1) * P], hid[:, p, t, 0:I], ident[:, :])
                    mm.then_inc(s["ht"], 1)

                def down(v, p, e):
                    pe.wait_ge(s["htc"], v + 1)
                    wait(pe, s["y"], v - 1)
                    for t in range(2):
                        mm = t_.matmul(bank[6 + p][:, t * D:(t + 1) * D], hT[0:I, p, t, :],
                                       wts[0:I, ds(e[t] * width + 4 * I, D)], start=True, stop=True)
                    mm.then_inc(s["dn"], 1)

                def step(v, p, over):
                    first = v - LAST if due(v, over, LAST) else 0
                    pairs = LAST if due(v, over, LAST) else v
                    if isinstance(v, int) and v == 0:
                        return
                    e = experts_of(PE, first, pairs - max(over - 1, 0))

                    def of(lag):
                        at = 2 * (LAST - lag if due(v, over, LAST) else v - lag)
                        return e[at:at + 2]
                    if due(v, over, 1):
                        find_rows(v - 1, 1 - p, of(1))
                    if due(v, over, 3):
                        x_turn(v - 3, 1 - p)
                    if due(v, over, 4):
                        gate_up(v - 4, p, of(4), due(v, over, 3))
                    if due(v, over, 5):
                        h_turn(v - 5, 1 - p)
                    if due(v, over, 6):
                        down(v - 6, p, of(6))
                bodies = by_tiles(pe, m, step, LAST)
                if m == 0:
                    pe.wait_ge(s["y"], 2 * bodies)
                    for n in range(NT // 2):
                        for t in range(2):
                            at = (2 * n + t) * P
                            mm = t_.matmul(bank[n][:, t * D:(t + 1) * D], lgT[:, at:at + P], down_b[:, :],
                                           start=True, stop=True)
                        mm.then_inc(N[m]["bd"], 1)

            prepare(0)
            experts(0)

            all_transposes(C)
            for kind in ("xa", "xv"):
                pe.wait_ge(C[kind], NT // 4)
            for v in range(NG + 2):
                if v < NG:
                    pe.wait_ge(C["mr"], v + 1)
                    wait(pe, C["sb"], v - 1)
                    for j in range(BG):
                        b = v * BG + j
                        t_.matmul(bank[v % 2][:, j * P:(j + 1) * P], ones[0:1, :], mrow[v % 2][:, j * P:(j + 1) * P],
                                  start=True, stop=False)
                        for k in range(KB):
                            mm = t_.matmul(bank[v % 2][:, j * P:(j + 1) * P], xT_b[:, k, b, :],
                                           cols[:, k, :, b * G:(b + 1) * G], start=False, stop=(k == KB - 1))
                    mm.then_inc(C["s"], 1)
                if 1 <= v <= NG:
                    g, p = v - 1, (v - 1) % 2
                    pe.wait_ge(C["a"], g + 1)
                    wait(pe, C["atc"], g - 1)
                    for j in range(BG):
                        mm = t_.transpose(bank[2 + p][:, j * P:(j + 1) * P], prob[p][:, j * P:(j + 1) * P], ident[:, :])
                    mm.then_inc(C["at"], 1)
                if v >= 2:
                    g, p = v - 2, v % 2
                    pe.wait_ge(C["atc"], g + 1)
                    pe.wait_ge(s_mem[g % 3], 16 * (g // 3 + 1))
                    wait(pe, C["roa"], g - 1)
                    wait(pe, C["rov"], g - 1)
                    for k in range(KB):
                        for j in range(BG):
                            mm = t_.matmul(bank[4 + 2 * p + k][:, j * P:(j + 1) * P],
                                           memory[g % 3][:, j, k * P:(k + 1) * P], attnT[p][:, j * P:(j + 1) * P],
                                           start=True, stop=True)
                    mm.then_inc(C["ro"], 1)
            pe.wait_ge(C["roa"], NG)
            pe.wait_ge(C["rov"], NG)
            for n in range(NT // 2):
                wait(pe, C["x"], n - 3)
                for t in range(2):
                    for k in range(KB):
                        mm = t_.transpose(bank[n % 4][:, (t * KB + k) * P:(t * KB + k + 1) * P],
                                          roT[:, k, 2 * n + t, :], ident[:, :])
                mm.then_inc(C["fx"], 1)

            prepare(1)
            experts(1)

        @block.vector
        def _(dve):
            v = nc.vector
            chain = [0]

            def link(ins):
                chain[0] += 1
                ins.then_inc(s_chain, 1)
                dve.wait_ge(s_chain, chain[0])

            def moments(tiles):
                for t in tiles:
                    v.bn_stats(stats[:, t, :], X[:, t * D:(t + 1) * D])

            def constants():
                dve.wait_ge(s_const, 11)
                v.tensor_copy(iota_f[:, :], iota_i[:, :])
                dve.wait_ge(s_par2, 16 * 7)
                v.tensor_copy(steps_f[:, :], steps_i[:, :])
                v.tensor_copy(tile_f[:, :], tile_i[:, :])
                v.tensor_reduce(valid[:, :], mask_u8[:, :].rearrange("a (b s) -> a b s", b=NB), AX.X, ALU.max)\
                    .then_inc(s_valid, 1)
                v.tensor_scalar(in_b[:, P:2 * P], in_b[:, P:2 * P], 1.0, None, ALU.add).then_inc(s_bias, 1)

            def token_stats(n):
                if n == 0:
                    moments(range(NT))
                link(v.memset(row2[:, :], 0.0))
                for t in range(NT):
                    last = v.bn_aggr(mv[:, 2 * t:2 * t + 2], stats[:, t, :])
                link(last)
                v.tensor_scalar(var_e[:, :], mv[:, 1:2 * NT:2], EPS, None, ALU.add).then_inc(s_var, 1)
                if n == 0:
                    constants()
                dve.wait_ge(s_sd, n + 1)
                link(v.reciprocal(rstd[:, :], std[:, :]))
                link(v.tensor_tensor(newt[:, :], rstd[:, :], rstd[:, :], ALU.mult))
                link(v.tensor_tensor(newt[:, :], newt[:, :], var_e[:, :], ALU.mult))
                link(v.tensor_scalar(newt[:, :], newt[:, :], -0.5, 1.5, ALU.mult, ALU.add))
                link(v.tensor_tensor(rstd[:, :], rstd[:, :], newt[:, :], ALU.mult))
                if n == 0:
                    v.scalar_tensor_tensor(out=shift[:, :], in0=mv[:, 0:2 * NT:2], scalar=-1.0, in1=rstd[:, :],
                                           op0=ALU.mult, op1=ALU.mult).then_inc(s_shift, 1)

            def normalise_all(s):
                for t in range(NT):
                    v.tensor_scalar(kept[:, t, :], X[:, t * D:(t + 1) * D], mv[:, 2 * t:2 * t + 1], rstd[:, t:t + 1],
                                    ALU.subtract, ALU.mult).then_inc(s["xn"], 1)

            dve.wait_ge(s_x, 16)
            token_stats(0)
            dve.wait_ge(s_bias, 2)
            v.tensor_tensor(in_bp[NE:2 * NE, :], in_b[NE:2 * NE, :], in_bp[NE:2 * NE, :].bitcast(fp32), ALU.subtract)\
                .then_inc(s_bias, 1)
            dve.wait_ge(s_vb, 1)
            dve.wait_ge(s_tanh, 1)
            link(v.tensor_scalar(valid_t[:, :], bank[7][:, 0:NB], tg[:, 1:2], None, ALU.mult))

            def skip_rows(h, p):
                dve.wait_ge(A["vn"], h + 1)
                wait(dve, A["out"], h - 1)
                v.scalar_tensor_tensor(out=skipv[:, p, :], in0=xn[:, p, :], scalar=skc[:, ds(h, 1)],
                                       in1=rows[:, ds(h * D, D)], op0=ALU.mult, op1=ALU.mult)\
                    .then_inc(A["skv"], 1)

            def kv_low(h, p):
                dve.wait_ge(A["vt"], h + 1)
                wait(dve, A["y"], 4 * h - 4)
                v.tensor_tensor(
                    kv[:, p, 0, :].rearrange("p (b i j) -> p b i j", b=NB, i=G),
                    vT[:, p, 0, :].rearrange("p (b i) -> p b i", i=G).unsqueeze(3).to_broadcast([P, NB, G, G]),
                    cols[:, 0, ds(h, 1), :].rearrange("p a (b j) -> p (a b) j", j=G).unsqueeze(2).to_broadcast([P, NB, G, G]),
                    ALU.mult).then_inc(A["kv0"], 1)

            def mix_out(h, p):
                dve.wait_ge(A["out"], h + 1)
                wait(dve, A["x"], h - 1)
                v.scalar_tensor_tensor(out=mixed[:, p, :], in0=bank[7][:, 0:D], scalar=tg[:, 0:1],
                                       in1=rows[:, ds(h * D, D)], op0=ALU.mult, op1=ALU.mult).then_inc(A["mix"], 1)
                dve.wait_ge(A["mix"], h + 1)
                v.scalar_tensor_tensor(out=mixed[:, p, :], in0=bank[6][:, 0:D], scalar=tg[:, 0:1],
                                       in1=mixed[:, p, :], op0=ALU.mult, op1=ALU.add).then_inc(A["mixed"], 1)

            def times_x1(h, p):
                for n in range(4):
                    lh, half = n // 2, n % 2
                    dve.wait_ge(A["y"], 4 * h + n + 1)
                    wait(dve, A["fd" if lh else "fp"], h)
                    v.tensor_tensor(
                        prod[:, lh, half * 512:(half + 1) * 512].rearrange("p (n j) -> p n j", j=G),
                        bank[n][:, :].rearrange("p (n j) -> p n j", j=G),
                        cols[:, lh, ds(h, 1), half * 64:(half + 1) * 64].rearrange("p a n -> p (a n)").unsqueeze(2)
                        .to_broadcast([P, 64, G]),
                        ALU.mult).then_inc(A["z"], 1)
                    if n == 1 and not (isinstance(h, int) and h < 1):
                        mix_out(h - 1, 1 - p)
                dve.wait_ge(A["z"], 4 * h + 4)
                wait(dve, A["f2"], 2 * h)
                z = prod[:, 1, :].rearrange("p (b i n) -> p b i n", b=NB, i=2)
                v.tensor_tensor(fold1[:, 1, :].rearrange("p (b n) -> p b n", b=NB), z[:, :, 0, :], z[:, :, 1, :],
                                ALU.add).then_inc(A["fd"], 1)

            def stage_a(h, p):
                static = isinstance(h, int)
                if not (static and h > NT - 2):
                    kv_low(h + 1, 1 - p)
                times_x1(h, p)
                if not (static and h > NT - 2):
                    skip_rows(h + 1, 1 - p)
                if not (static and h < 4):
                    dve.wait_ge(A["x"], h - 3)
                    v.bn_stats(stats[:, ds(h - 4, 1), :].rearrange("p a n -> p (a n)"), X[:, ds((h - 4) * D, D)])

            dve.wait_ge(s_par, 32)
            dve.wait_ge(s_ctx, 16)
            skip_rows(0, 0)
            dve.wait_ge(s_cols, 16)
            kv_low(0, 0)
            for h in range(2):
                stage_a(h, h)
            for h in range(2, 6):
                stage_a(h, h % 2)
            with dve.Fori(3, NT // 2 - 1, 1) as pair:
                for p in range(2):
                    stage_a(2 * pair + p, p)
            for h in range(NT - 2, NT):
                stage_a(h, h % 2)
            mix_out(NT - 1, 1)
            dve.wait_ge(A["x"], NT)
            moments(range(NT - 4, NT))

            def over_k(a, k):
                return a.unsqueeze(2).to_broadcast([P, NT, k])

            def prepare(m):
                s, K = N[m], TOPK[m]
                token_stats(1 + 2 * m)

                normalise_all(s)
                for n in range(1, NT // 2, 2):
                    dve.wait_ge(s["tr"], n + 1)
                    v.tensor_copy(xT_all[:, :, 2 * n * P:2 * (n + 1) * P],
                                  bank[4 + n % 4][:, :].rearrange("p (k n) -> p k n", k=KB)).then_inc(s["xv"], 1)

                dve.wait_ge(s["l"], 1)
                logits = bank[0][:, :].rearrange("p (t e) -> p t e", t=NT)
                values = routed[:, :, 0:NE]
                v.memset(routed[:, :, NE:], NONE[m])
                if m == 0:
                    link(v.tensor_tensor(values, logits, rt_bias[:, :].unsqueeze(1).to_broadcast([P, NT, NE]), ALU.add))
                else:
                    link(v.tensor_reduce(row1[:, :], logits, AX.X, ALU.max))
                    v.tensor_tensor(lg[:, :, :], logits, over_k(row1[:, :], NE), ALU.subtract).then_inc(s["e0"], 1)
                    dve.wait_ge(s["e1"], 1)
                    link(v.tensor_reduce(row1[:, :], lg[:, :, :], AX.X, ALU.add))
                    link(v.reciprocal(row2[:, :], row1[:, :]))
                    link(v.tensor_tensor(values, lg[:, :, :], over_k(row2[:, :], NE), ALU.mult))
                for t in range(NT):
                    last = v.max(top[:, t, :], routed[:, t, 0:NE])
                link(last)
                if m == 0:
                    v.tensor_tensor(lg[:, :, :], values, over_k(top[:, :, 0], NE), ALU.subtract).then_inc(s["e0"], 1)
                    dve.wait_ge(s["e0"], 1)
                    link(v.memset(top[:, :, K:8], NONE[m]))
                else:
                    link(v.tensor_reduce(row1[:, :], top[:, :, :], AX.X, ALU.add))
                    link(v.tensor_scalar(row1[:, :], row1[:, :], 1e-12, None, ALU.max))
                    link(v.reciprocal(row2[:, :], row1[:, :]))
                    link(v.tensor_tensor(tcum[:, :, :], top[:, :, :], over_k(row2[:, :], K), ALU.mult))
                    for k in range(1, K):
                        link(v.tensor_tensor(tcum[:, :, k], tcum[:, :, k], tcum[:, :, k - 1], ALU.add))
                    v.memset(act_k[:, :, 0:1], 1.0)
                    link(v.tensor_scalar(act_k[:, :, 1:K], tcum[:, :, 0:K - 1], THRESHOLD, None, ALU.is_lt))
                    link(v.tensor_tensor(top[:, :, :], top[:, :, :], act_k[:, :, :], ALU.mult))
                    link(v.scalar_tensor_tensor(out=top[:, :, :], in0=act_k[:, :, :], scalar=NONE[m], in1=top[:, :, :],
                                                op0=ALU.add, op1=ALU.add))
                for t in range(NT):
                    last = v.match_replace(taken[:, t, :], top[:, t, :], routed[:, t, :], GONE[m])
                link(last)
                mask3 = mask_e[:, :].rearrange("p (t e) -> p t e", t=NT)
                v.tensor_tensor(mask3, taken[:, :, 0:NE], values, ALU.not_equal).then_inc(s["mk"], 1)
                dve.wait_ge(s["mk"], 1)
                dve.wait_ge(s["mk"], 1)
                v.tensor_copy(steps[:, 0, :], mask3[:, 0, :])
                v.tensor_tensor(steps[:, 1:NT, :], mask3[:, 1:NT, :], mask3[:, 0:NT - 1, :], ALU.subtract)\
                    .then_inc(s["df"], 1)
                if m == 0:
                    dve.wait_ge(s["e1"], 1)
                cw3 = cw[:, :].rearrange("p (t e) -> p t e", t=NT)
                link(v.tensor_tensor(cw3, lg[:, :, :] if m == 0 else values, mask3, ALU.mult))
                link(v.tensor_reduce(row1[:, :], cw3, AX.X, ALU.add))
                link(v.tensor_scalar(row1[:, :], row1[:, :], 1e-12, None, ALU.max))
                link(v.reciprocal(row2[:, :], row1[:, :]))
                link(v.tensor_scalar(row2[:, :], row2[:, :], tg[:, 2 + m:3 + m], None, ALU.mult))
                v.tensor_tensor(cw3, cw3, over_k(row2[:, :], NE), ALU.mult).then_inc(s["cw"], 1)
                dve.wait_ge(s["tot"], 1)
                v.tensor_reduce(n_e[:, :], bank[4][:, :].rearrange("p (t e) -> p e t", t=NT), AX.X, ALU.add)\
                    .then_inc(s["tt"], 1)
                dve.wait_ge(s["tt"], 1)
                wide = one_hot_2[:, 0:NE * (NT - 1)].rearrange("p (e n) -> p e n", e=NE)
                link(v.tensor_tensor(wide, n_e[:, :].unsqueeze(2).to_broadcast([P, NE, NT - 1]),
                                     steps_f[:, :].unsqueeze(1).to_broadcast([P, NE, NT - 1]), ALU.is_gt))
                link(v.tensor_reduce(n_tiles[:, :], wide, AX.X, ALU.add))
                link(v.tensor_scalar(n_tiles[:, :], n_tiles[:, :], 1.0, None, ALU.add))
                H, shift, c = NE // 2, 1, 0
                link(v.tensor_copy(cum[:, 0, H:H + NE], n_tiles[:, :]))
                while shift < NE:
                    link(v.tensor_tensor(cum[:, 1 - c, H:H + NE], cum[:, c, H:H + NE], cum[:, c, H - shift:H - shift + NE],
                                         ALU.add))
                    shift, c = 2 * shift, 1 - c
                ends = cum[:, c, H:H + NE]
                two = [P, 2, NE]
                link(v.tensor_tensor(le[:, :, :], ends.unsqueeze(1).to_broadcast(two),
                                     tile_f[:, :].unsqueeze(2).to_broadcast(two), ALU.is_le))
                link(v.tensor_tensor(le_n[:, :, :], le[:, :, :], n_tiles[:, :].unsqueeze(1).to_broadcast(two), ALU.mult))
                v.tensor_reduce(tab[:, 2:4], le[:, :, :], AX.X, ALU.add)
                link(v.tensor_reduce(past[:, :], le_n[:, :, :], AX.X, ALU.add))
                link(v.tensor_tensor(past[:, :], tile_f[:, :], past[:, :], ALU.subtract))
                v.tensor_scalar(tab[:, 0:2], tab[:, 2:4], float(NE - 1), None, ALU.min)
                link(v.tensor_scalar(past[:, :], past[:, :], float(P), None, ALU.mult))
                link(v.tensor_scalar(tab[:, 2:4], tab[:, 2:4], NE - 0.5, float(TOK), ALU.is_gt, ALU.mult))
                link(v.tensor_tensor(tab[:, 2:4], tab[:, 2:4], past[:, :], ALU.add))
                v.tensor_tensor(spread[:, :, :], ident[:, :].unsqueeze(1).to_broadcast([P, 4, P]),
                                tab[:, :].unsqueeze(2).to_broadcast([P, 4, P]), ALU.mult).then_inc(s["tb"], 1)
                dve.wait_ge(s["tbl"], 16 * NCH)
                link(v.memset(find[:, :, P + 1:P + 2], 1.0))
                link(v.memset(find[0:1, :, P + 1:P + 2], 0.0))
                for n in range(1, NE // 4, 2):
                    dve.wait_ge(s["fd"], n + 1)
                    v.tensor_copy(find[:, 4 * n:4 * n + 4, 0:P],
                                  bank[n][0:NT, :].rearrange("p (e n) -> p e n", e=4)).then_inc(s["ev"], 1)
                dve.wait_ge(s["pd"], 1)
                v.tensor_copy(find[:, :, P], bank[5][0:NT, 0:NE]).then_inc(s["tt"], 1)
                v.tensor_scalar(cnt_i[:, :], cum[0:1, c, H + NE - 1:H + NE], float(-NE), None, ALU.add)
                dve.wait_ge(s["tp"], 1)
                v.tensor_copy(tab_i[:, :], bank[6][0:1, 0:SMAX])
                v.tensor_copy(base[:, :], bank[6][:, SMAX:2 * SMAX])
                link(v.tensor_scalar(place[:, :], bank[6][:, SMAX:2 * SMAX], tile_f[:, 0:1], None, ALU.add))
                dve.wait_ge(s["pd"], 2)
                v.tensor_copy(starts[:, :], bank[5][0:NT, NE:2 * NE]).then_inc(s["tab"], 1)
                dve.wait_ge(s["tab"], 1)
            def experts(m):
                s, I = M[m], INNER[m]

                def mark(v_, p):
                    e = experts_of(DVE, v_)
                    wait(dve, s["fnd"], v_ - 1)
                    for t in range(2):
                        last = v.tensor_scalar(marks[:, p, t, :], iota_f[0:NT, :], base[0:NT, ds(2 * v_ + t, 1)],
                                               starts[:, ds(e[t], 1)], ALU.add, ALU.is_ge)
                    last.then_inc(s["mark"], 1)

                def index(v_, p):
                    at = bank[1][:, 0:2 * WT].rearrange("p (t n) -> p t n", t=2)
                    dve.wait_ge(s["fnd"], v_ + 1)
                    v.tensor_tensor(seek[:, p, :], place[:, ds(2 * v_, 2)], at[:, :, P], ALU.subtract).then_inc(s["fx"], 1)
                    dve.wait_ge(s["fx"], 3 * v_ + 1)
                    v.tensor_tensor(compared[:, p, :, :], at[:, :, 0:P],
                                    seek[:, p, :].unsqueeze(2).to_broadcast([P, 2, P]), ALU.is_le).then_inc(s["fx"], 1)
                    dve.wait_ge(s["fx"], 3 * v_ + 2)
                    v.tensor_reduce(found[:, p, :], compared[:, p, :, :], AX.X, ALU.add).then_inc(s["fx"], 1)
                    dve.wait_ge(s["fx"], 3 * v_ + 3)
                    wait(dve, s[f"ld{p}"], 32 * (half(v_) - 1))
                    v.scalar_tensor_tensor(out=idx_x[:, p, :], in0=found[:, p, :], scalar=float(NT),
                                           in1=at[:, :, P + 1], op0=ALU.mult, op1=ALU.add).then_inc(s["ix"], 1)
                    v.scalar_tensor_tensor(out=idx_rows[:, ds(2 * v_, 2)], in0=found[:, p, :], scalar=float(NT),
                                           in1=at[:, :, P + 1], op0=ALU.mult, op1=ALU.add).then_inc(s["ir"], 1)

                def first_half(v_, p):
                    if m == 0:
                        gu = bank[2 + p][:, :].rearrange("p (t n) -> p t n", t=2)
                        dve.wait_ge(s["gu"], v_ + 1)
                        wait(dve, s["gs"], v_ - 1)
                        v.tensor_scalar(gmin[:, p, :, :], gu[:, :, 0:P], LIMIT, None, ALU.min).then_inc(s["gmin"], 1)
                        wait(dve, s["h"], v_ - 1)
                        v.tensor_scalar(umin[:, p, :, :], gu[:, :, P:2 * P], LIMIT + 1.0, 1.0 - LIMIT,
                                        ALU.min, ALU.max).then_inc(s["umin"], 1)

                def second_half(v_, p):
                    dve.wait_ge(s["sig"], v_ + 1)
                    wait(dve, s["ht"], v_ - 1)
                    if m == 0:
                        v.tensor_tensor(sig[:, p, :, :], sig[:, p, :, :], gmin[:, p, :, :], ALU.mult).then_inc(s["gs"], 1)
                        dve.wait_ge(s["gs"], v_ + 1)
                        dve.wait_ge(s["umin"], v_ + 1)
                        v.tensor_tensor(hid[:, p, :, :], sig[:, p, :, :], umin[:, p, :, :], ALU.mult).then_inc(s["h"], 1)
                    else:
                        gu = bank[2 + p][:, :].rearrange("p (t n) -> p t n", t=2)
                        v.tensor_tensor(hid[:, p, :, 0:I], sig[:, p, :, 0:I], gu[:, :, I:2 * I], ALU.mult)\
                            .then_inc(s["h"], 1)

                def weigh(v_, p):
                    for t in range(2):
                        wait(dve, s[f"sc{t}"], 16 * (v_ - 1))
                    dve.wait_ge(s["ir"], v_ + 1)
                    v.tensor_scalar(idx_y[:, p, :], idx_rows[:, ds(2 * v_, 2)], 0.0, None, ALU.add)
                    dve.wait_ge(s["dn"], v_ + 1)
                    dve.wait_ge(s["wr"], v_ + 1)
                    for t in range(2):
                        last = v.tensor_scalar(y[:, p, t, :], bank[6 + p][:, t * D:(t + 1) * D],
                                               wt_rows[:, ds(2 * v_ + t, 1)], None, ALU.mult)
                    last.then_inc(s["y"], 1)

                def step(v_, p, over):
                    if due(v_, over, 0):
                        mark(v_, p)
                    if due(v_, over, 1):
                        index(v_ - 1, 1 - p)
                    if due(v_, over, 4):
                        first_half(v_ - 4, p)
                    if due(v_, over, 6):
                        weigh(v_ - 6, p)
                    if due(v_, over, 4):
                        second_half(v_ - 4, p)
                dve.wait_ge(s["init"], 32)
                by_tiles(dve, m, step, LAST)
                n = TPC * D
                for c in range(NCH):
                    at = slice(c * n, (c + 1) * n)
                    dve.wait_ge(s_sums[c], 32 * (m + 1))
                    last = v.tensor_tensor(X[:, at], X[:, at], acc1[:, at], ALU.add)
                    if m == 0:
                        link(last)
                        for q in range(2 * c, 2 * c + 2):
                            dve.wait_ge(N[m]["bd"], q + 1)
                            xt_ = X[:, q * CH:(q + 1) * CH]
                            last = v.tensor_tensor(xt_, xt_, bank[q][:, :], ALU.add)
                        link(last)
                        moments(range(c * TPC, (c + 1) * TPC))
                    else:
                        last.then_inc(s["x"], 1)

            prepare(0)
            experts(0)

            token_stats(2)
            normalise_all(C)
            for n in range(1, NT // 2, 2):
                dve.wait_ge(C["tr"], n + 1)
                for k in range(KB):
                    last = v.tensor_copy(by_batch(n, k), turned(n, k))
                last.then_inc(C["xv"], 1)

            def by_four(a):
                return a.rearrange("p (b n) -> p b n", b=BG)
            each = [P, BG, P]
            for w in range(NG + 2):
                if w < NG:
                    of = slice(w * BG, (w + 1) * BG)
                    dve.wait_ge(C["s"], w + 1)
                    wait(dve, C["at"], w - 1)
                    link(v.tensor_reduce(smax[:, of], by_four(bank[w % 2][:, :]), AX.X, ALU.max))
                    v.tensor_tensor(by_four(prob[w % 2]), by_four(bank[w % 2][:, :]),
                                    smax[:, of].unsqueeze(2).to_broadcast(each), ALU.subtract).then_inc(C["sb"], 1)
                if 1 <= w <= NG:
                    g, of = w - 1, slice((w - 1) * BG, w * BG)
                    dve.wait_ge(C["e"], g + 1)
                    link(v.tensor_reduce(psum_row[:, of], by_four(prob[g % 2]), AX.X, ALU.add))
                    link(v.reciprocal(rinv[:, of], psum_row[:, of]))
                    link(v.tensor_tensor(rinv[:, of], rinv[:, of], valid_t[:, of], ALU.mult))
                    v.tensor_tensor(by_four(prob[g % 2]), by_four(prob[g % 2]),
                                    rinv[:, of].unsqueeze(2).to_broadcast(each), ALU.mult).then_inc(C["a"], 1)
                if w >= 2:
                    dve.wait_ge(C["ro"], w - 1)
                    v.tensor_copy(*readout_of(w - 2, 1)).then_inc(C["rov"], 1)
            for n in range(NT // 2):
                dve.wait_ge(C["fx"], n + 1)
                xt = X[:, 2 * n * D:2 * (n + 1) * D]
                v.tensor_tensor(xt, xt, bank[n % 4][:, :], ALU.add).then_inc(C["x"], 1)
                if n >= 1:
                    dve.wait_ge(C["x"], n)
                    moments(range(2 * n - 2, 2 * n))
            dve.wait_ge(C["x"], NT // 2)
            moments(range(NT - 2, NT))

            prepare(1)
            experts(1)


def kernel(**inputs):
    import numpy as np
    import concourse.bacc as bacc
    from concourse.bass_utils import run_bass_kernel_spmd as run

    a = {k: np.asarray(v) for k, v in inputs.items()}
    x, c = a["x"], a["ctx_2048"]
    B, S, D = x.shape
    NT = a["L0_xattn_k"].shape[0]
    G = S // NT
    P, KB, E = 128, D // 128, a["L0_ffn_gate_w"].shape[0]

    def rows(t):
        return t.reshape(B, NT, G, D).transpose(0, 2, 1, 3).reshape(B * G, NT, D)

    def router(w):
        return w.T.reshape(KB, P, E).transpose(1, 0, 2).reshape(P, KB * E)

    def experts(gate, up, down):
        both = np.concatenate([gate, up], axis=2).reshape(E, KB, P, -1).transpose(0, 2, 1, 3).reshape(E, P, -1)
        down = np.concatenate([down, np.zeros((E, P - down.shape[1], D), down.dtype)], axis=1)
        return np.concatenate([both, down], axis=2).transpose(1, 0, 2)

    gu = a["L1_ffn_gate_up_proj"].transpose(0, 2, 1)
    I1 = gu.shape[2] // 2
    down1 = a["L1_ffn_down_proj"].transpose(0, 2, 1)
    k = a["L0_xattn_k"]
    arrays = {
        "x_rows": rows(x),
        "ctx_rows": rows(c),
        "ctx_cols": rows(c).transpose(2, 1, 0).reshape(KB, P, NT, P).transpose(1, 0, 2, 3),
        "ctx_batch": c,
        "filt": np.concatenate([np.zeros((NT, P), k.dtype), k], axis=1),
        "skip_cols": np.tile(a["fside_S2_0"].reshape(NT, G).T, (B, 1)),
        "mask": a["mask_BxS2_bk0"].reshape(1, B * S),
        "gates": np.concatenate([a["g_xattn"], a["g_ffn"]]),
        "router0": router(a["L0_ffn_gate_w"]),
        "router0_bias": a["L0_ffn_gate_b"],
        "in_bias0": np.concatenate([a["L0_ffn_b_gate"], a["L0_ffn_b_up"]], axis=1),
        "down_bias0": a["L0_ffn_b_down"],
        "experts0": experts(a["L0_ffn_w_gate"], a["L0_ffn_w_up"], a["L0_ffn_w_down"]),
        "router1": router(a["L1_ffn_gate_weight"]),
        "experts1": experts(gu[:, :, :I1], gu[:, :, I1:], down1),
    }
    arrays = {f"in_{n}": np.ascontiguousarray(v) for n, v in arrays.items()}
    nc = bacc.Bacc("TRN2", target_bir_lowering=False, num_devices=1)
    args = [nc.dram_tensor(n, v.shape, mybir.dt.from_np(v.dtype), kind="ExternalInput").ap() for n, v in arrays.items()]
    args.append(nc.dram_tensor("out", (P, NT, D), mybir.dt.from_np(x.dtype), kind="ExternalOutput").ap())
    bass_flamingo_gated_two_layers_kernel(nc, *args)
    got = run(nc, [arrays], core_ids=[0]).results[0]["out"]
    return got.reshape(B, G, NT, D).transpose(0, 2, 1, 3).reshape(B, S, D)
```
